# Optimizing a Trainium2 kernel written in Bass

```python
import numpy as np
import jax
import jax.numpy as jnp

def _softmax(x, axis=-1):
    return jax.nn.softmax(x, axis=axis)

def _gelu(x):
    return jax.nn.gelu(x, approximate=True)

def _silu(x):
    return jax.nn.silu(x)

def _sigmoid(x):
    return jax.nn.sigmoid(x)

def _layernorm(x, axis=-1, eps=1e-05):
    m = jnp.mean(x, axis=axis, keepdims=True)
    v = jnp.var(x, axis=axis, keepdims=True)
    return (x - m) / jnp.sqrt(v + eps)

def _scatter_add(tgt, idx, src, axis=0):
    return tgt.at[idx].add(src)

def _segment_sum(src, seg, n):
    return jax.ops.segment_sum(src, seg, n)
kernel_name = 'mk_vit_tower_d2_tok_img1024_r4_31fc86'

def setup_inputs(seed: int=0):
    np.random.seed(seed)
    _w = jnp.asarray

    def _rec_inputs():
        import jax
        import jax.numpy as jnp
        _rk = jax.random.key(seed)
        x = -0.00016672 + 0.999947 * jax.random.normal(jax.random.fold_in(_rk, 1), (32, 3, 96, 96), jnp.float32)
        return x
    x = _rec_inputs()

    def _L0_tok_setup():
        import jax, jax.numpy as jnp
        import numpy as np
        PATCH = 16

        def _patchify(x, p):
            B, C, H, W = x.shape
            nh, nw = (H // p, W // p)
            x = x.reshape(B, C, nh, p, nw, p)
            x = x.transpose(0, 2, 4, 1, 3, 5)
            return x.reshape(B, nh * nw, C * p * p)
        key = jax.random.key(seed)
        k1, k2, k3, k4, k5 = jax.random.split(key, 5)
        B, C, H = (64, 3, 96)
        d_model = 256
        p = PATCH
        num_patches = (H // p) ** 2
        in_dim = p * p * C
        x = jax.random.normal(k1, (B, C, H, H), dtype=jnp.float32)
        bound = 1.0 / np.sqrt(in_dim)
        W = jax.random.uniform(k2, (d_model, in_dim), dtype=jnp.float32, minval=-bound, maxval=bound)
        b = jax.random.uniform(k3, (d_model,), dtype=jnp.float32, minval=-bound, maxval=bound)
        cls_token = jax.random.normal(k4, (1, 1, d_model), dtype=jnp.float32)
        pos_enc = jax.random.normal(k5, (1, num_patches + 1, d_model), dtype=jnp.float32)
        return {'x': x, 'W': W, 'b': b, 'cls_token': cls_token, 'pos_enc': pos_enc}
    _L0_tok_all = _L0_tok_setup()
    _L0_tok_in = {k: v for k, v in _L0_tok_all.items() if k in ('W', 'b', 'cls_token', 'pos_enc')}
    del _L0_tok_all

    def _L0_attn_setup():
        import jax, jax.numpy as jnp
        import numpy as np
        SEG = 4
        H = 8
        D = 256
        B = 8
        S = 1024
        key = jax.random.key(seed)
        ks = jax.random.split(key, 9)
        s = 0.02
        return {'x': jax.random.normal(ks[0], (B, S, D), dtype=jnp.float32), 'proj_qk_w': jax.random.normal(ks[1], (D, D), dtype=jnp.float32) * s, 'proj_qk_b': jax.random.normal(ks[2], (D,), dtype=jnp.float32) * s, 'proj_v_w': jax.random.normal(ks[3], (D, D), dtype=jnp.float32) * s, 'proj_v_b': jax.random.normal(ks[4], (D,), dtype=jnp.float32) * s, 'in_proj_w': jax.random.normal(ks[5], (3 * D, D), dtype=jnp.float32) * s, 'in_proj_b': jax.random.normal(ks[6], (3 * D,), dtype=jnp.float32) * s, 'out_proj_w': jax.random.normal(ks[7], (D, D), dtype=jnp.float32) * s, 'out_proj_b': jax.random.normal(ks[8], (D,), dtype=jnp.float32) * s}
    _L0_attn_all = _L0_attn_setup()
    _L0_attn_in = {k: v for k, v in _L0_attn_all.items() if k in ('proj_qk_w', 'proj_qk_b', 'proj_v_w', 'proj_v_b', 'in_proj_w', 'in_proj_b', 'out_proj_w', 'out_proj_b')}
    del _L0_attn_all

    def _L0_ffn_setup():
        import jax, jax.numpy as jnp
        import numpy as np
        B, S, D_MODEL, D_HIDDEN = (4, 512, 256, 1024)

        def act_quant(x):
            scale = 127.0 / jnp.clip(jnp.max(jnp.abs(x), axis=-1, keepdims=True), 1e-05)
            return jnp.clip(jnp.round(x * scale), -128, 127) / scale

        def weight_quant(w):
            scale = 1.0 / jnp.clip(jnp.mean(jnp.abs(w)), 1e-05)
            return jnp.clip(jnp.round(w * scale), -1, 1) / scale

        def bit_linear(x, w):
            xq = x + jax.lax.stop_gradient(act_quant(x) - x)
            wq = w + jax.lax.stop_gradient(weight_quant(w) - w)
            return jnp.einsum('bsd,hd->bsh', xq, wq)

        def depthwise_conv1d(x_bcl, w, b):
            y = jax.lax.conv_general_dilated(x_bcl, w, window_strides=(1,), padding=[(1, 1)], dimension_numbers=('NCH', 'OIH', 'NCH'), feature_group_count=x_bcl.shape[1])
            return y + b[None, :, None]
        key = jax.random.key(seed)
        ks = jax.random.split(key, 5)
        lim1 = 1.0 / np.sqrt(D_MODEL)
        lim2 = 1.0 / np.sqrt(D_HIDDEN)
        limc = 1.0 / np.sqrt(3.0)
        return {'x': jax.random.normal(ks[0], (B, S, D_MODEL), dtype=jnp.float32), 'w1': jax.random.uniform(ks[1], (D_HIDDEN, D_MODEL), jnp.float32, -lim1, lim1), 'conv_w': jax.random.uniform(ks[2], (D_HIDDEN, 1, 3), jnp.float32, -limc, limc), 'conv_b': jax.random.uniform(ks[3], (D_HIDDEN,), jnp.float32, -limc, limc), 'w2': jax.random.uniform(ks[4], (D_MODEL, D_HIDDEN), jnp.float32, -lim2, lim2)}
    _L0_ffn_all = _L0_ffn_setup()
    _L0_ffn_in = {k: v for k, v in _L0_ffn_all.items() if k in ('w1', 'conv_w', 'conv_b', 'w2')}
    del _L0_ffn_all

    def _L1_attn_setup():
        import jax, jax.numpy as jnp
        import numpy as np
        B, S, D_IN, D_OUT = (4, 512, 256, 256)
        key = jax.random.key(seed)
        kx, kq, kk, kv = jax.random.split(key, 4)
        x = jax.random.normal(kx, (B, S, D_IN), dtype=jnp.float32)
        sc = 1.0 / np.sqrt(D_IN)
        Wq = jax.random.uniform(kq, (D_OUT, D_IN), jnp.float32, -sc, sc)
        Wk = jax.random.uniform(kk, (D_OUT, D_IN), jnp.float32, -sc, sc)
        Wv = jax.random.uniform(kv, (D_OUT, D_IN), jnp.float32, -sc, sc)
        return {'x': x, 'Wq': Wq, 'Wk': Wk, 'Wv': Wv}
    _L1_attn_all = _L1_attn_setup()
    _L1_attn_in = {k: v for k, v in _L1_attn_all.items() if k in ('Wq', 'Wk', 'Wv')}
    del _L1_attn_all

    def _L1_ffn_setup():
        import jax, jax.numpy as jnp
        import numpy as np
        HIDDEN = 256
        NUM_EXPERTS = 8
        TOP_K = 2
        B, S = (4, 256)
        key = jax.random.key(seed)
        ks = jax.random.split(key, 8)
        H, E = (HIDDEN, NUM_EXPERTS)
        sc = lambda fan_in: 1.0 / np.sqrt(fan_in)
        x = jax.random.normal(ks[0], (B, S, H), dtype=jnp.float32)
        Wr = jax.random.uniform(ks[1], (H, E), minval=-sc(H), maxval=sc(H), dtype=jnp.float32)
        br = jax.random.uniform(ks[2], (E,), minval=-sc(H), maxval=sc(H), dtype=jnp.float32)
        W1 = jax.random.uniform(ks[3], (E, H, 2 * H), minval=-sc(H), maxval=sc(H), dtype=jnp.float32)
        b1 = jax.random.uniform(ks[4], (E, 2 * H), minval=-sc(H), maxval=sc(H), dtype=jnp.float32)
        W2 = jax.random.uniform(ks[5], (E, 2 * H, H), minval=-sc(2 * H), maxval=sc(2 * H), dtype=jnp.float32)
        b2 = jax.random.uniform(ks[6], (E, H), minval=-sc(2 * H), maxval=sc(2 * H), dtype=jnp.float32)
        return {'x': x, 'Wr': Wr, 'br': br, 'W1': W1, 'b1': b1, 'W2': W2, 'b2': b2}
    _L1_ffn_all = _L1_ffn_setup()
    _L1_ffn_in = {k: v for k, v in _L1_ffn_all.items() if k in ('Wr', 'br', 'W1', 'b1', 'W2', 'b2')}
    del _L1_ffn_all
    return {'x': x, 'L0_tok_W': _L0_tok_in['W'], 'L0_tok_b': _L0_tok_in['b'], 'L0_tok_cls_token': _L0_tok_in['cls_token'], 'L0_tok_pos_enc': _L0_tok_in['pos_enc'], 'L0_attn_proj_qk_w': _L0_attn_in['proj_qk_w'], 'L0_attn_proj_qk_b': _L0_attn_in['proj_qk_b'], 'L0_attn_proj_v_w': _L0_attn_in['proj_v_w'], 'L0_attn_proj_v_b': _L0_attn_in['proj_v_b'], 'L0_attn_in_proj_w': _L0_attn_in['in_proj_w'], 'L0_attn_in_proj_b': _L0_attn_in['in_proj_b'], 'L0_attn_out_proj_w': _L0_attn_in['out_proj_w'], 'L0_attn_out_proj_b': _L0_attn_in['out_proj_b'], 'L0_ffn_w1': _L0_ffn_in['w1'], 'L0_ffn_conv_w': _L0_ffn_in['conv_w'], 'L0_ffn_conv_b': _L0_ffn_in['conv_b'], 'L0_ffn_w2': _L0_ffn_in['w2'], 'L1_attn_Wq': _L1_attn_in['Wq'], 'L1_attn_Wk': _L1_attn_in['Wk'], 'L1_attn_Wv': _L1_attn_in['Wv'], 'L1_ffn_Wr': _L1_ffn_in['Wr'], 'L1_ffn_br': _L1_ffn_in['br'], 'L1_ffn_W1': _L1_ffn_in['W1'], 'L1_ffn_b1': _L1_ffn_in['b1'], 'L1_ffn_W2': _L1_ffn_in['W2'], 'L1_ffn_b2': _L1_ffn_in['b2']}

def reference(x, L0_tok_W, L0_tok_b, L0_tok_cls_token, L0_tok_pos_enc, L0_attn_proj_qk_w, L0_attn_proj_qk_b, L0_attn_proj_v_w, L0_attn_proj_v_b, L0_attn_in_proj_w, L0_attn_in_proj_b, L0_attn_out_proj_w, L0_attn_out_proj_b, L0_ffn_w1, L0_ffn_conv_w, L0_ffn_conv_b, L0_ffn_w2, L1_attn_Wq, L1_attn_Wk, L1_attn_Wv, L1_ffn_Wr, L1_ffn_br, L1_ffn_W1, L1_ffn_b1, L1_ffn_W2, L1_ffn_b2):
    import jax
    import jax.numpy as jnp

    def _L0_tok_ref(x, W, b, cls_token, pos_enc):
        import jax, jax.numpy as jnp
        import numpy as np
        PATCH = 16

        def _patchify(x, p):
            B, C, H, W = x.shape
            nh, nw = (H // p, W // p)
            x = x.reshape(B, C, nh, p, nw, p)
            x = x.transpose(0, 2, 4, 1, 3, 5)
            return x.reshape(B, nh * nw, C * p * p)
        B = x.shape[0]
        patches = _patchify(x, PATCH)
        proj = jnp.einsum('bnf,df->bnd', patches, W) + b
        cls = jnp.broadcast_to(cls_token, (B, 1, cls_token.shape[-1]))
        out = jnp.concatenate([cls, proj], axis=1) + pos_enc
        return out

    def _L0_attn_ref(x, proj_qk_w, proj_qk_b, proj_v_w, proj_v_b, in_proj_w, in_proj_b, out_proj_w, out_proj_b):
        import jax, jax.numpy as jnp
        import numpy as np
        SEG = 4
        H = 8
        D = 256
        B = 8
        S = 1024
        b, seq_len, d = x.shape
        hd = d // H
        pad = SEG - seq_len % SEG
        x = jnp.concatenate([x, x[:, :pad]], axis=1)
        T = seq_len + pad
        a = T // SEG
        xb = x.reshape(b, a, SEG, d).transpose(1, 0, 2, 3).reshape(a * b, SEG, d)
        qk_in = xb @ proj_qk_w.T + proj_qk_b
        v_in = xb @ proj_v_w.T + proj_v_b
        wq, wk, wv = jnp.split(in_proj_w, 3, axis=0)
        bq, bk, bv = jnp.split(in_proj_b, 3)
        q = (qk_in @ wq.T + bq).reshape(a * b, SEG, H, hd)
        k = (qk_in @ wk.T + bk).reshape(a * b, SEG, H, hd)
        v = (v_in @ wv.T + bv).reshape(a * b, SEG, H, hd)
        scale = 1.0 / np.sqrt(hd).astype(np.float32)
        scores = jnp.einsum('nqhd,nkhd->nhqk', q * scale, k)
        diag = jnp.eye(SEG, dtype=bool)
        scores = jnp.where(diag[None, None], jnp.finfo(scores.dtype).min, scores)
        attn = jax.nn.softmax(scores, axis=-1)
        o = jnp.einsum('nhqk,nkhd->nqhd', attn, v).reshape(a * b, SEG, d)
        o = o @ out_proj_w.T + out_proj_b
        out = o.reshape(a, b, SEG, d).transpose(1, 0, 2, 3).reshape(b, T, d)
        return out[:, :seq_len]

    def _L0_ffn_ref(x, w1, conv_w, conv_b, w2):
        import jax, jax.numpy as jnp
        import numpy as np
        B, S, D_MODEL, D_HIDDEN = (4, 512, 256, 1024)

        def act_quant(x):
            scale = 127.0 / jnp.clip(jnp.max(jnp.abs(x), axis=-1, keepdims=True), 1e-05)
            return jnp.clip(jnp.round(x * scale), -128, 127) / scale

        def weight_quant(w):
            scale = 1.0 / jnp.clip(jnp.mean(jnp.abs(w)), 1e-05)
            return jnp.clip(jnp.round(w * scale), -1, 1) / scale

        def bit_linear(x, w):
            xq = x + jax.lax.stop_gradient(act_quant(x) - x)
            wq = w + jax.lax.stop_gradient(weight_quant(w) - w)
            return jnp.einsum('bsd,hd->bsh', xq, wq)

        def depthwise_conv1d(x_bcl, w, b):
            y = jax.lax.conv_general_dilated(x_bcl, w, window_strides=(1,), padding=[(1, 1)], dimension_numbers=('NCH', 'OIH', 'NCH'), feature_group_count=x_bcl.shape[1])
            return y + b[None, :, None]
        h = bit_linear(x, w1)
        h = depthwise_conv1d(h.transpose(0, 2, 1), conv_w, conv_b)
        h = h.transpose(0, 2, 1)
        h = jax.nn.silu(h)
        return bit_linear(h, w2)

    def _L1_attn_ref(x, Wq, Wk, Wv):
        import jax, jax.numpy as jnp
        import numpy as np
        B, S, D_IN, D_OUT = (4, 512, 256, 256)
        q = jnp.einsum('bsi,oi->bso', x, Wq)
        k = jnp.einsum('bsi,oi->bso', x, Wk)
        v = jnp.einsum('bsi,oi->bso', x, Wv)
        scores = jnp.einsum('bqd,bkd->bqk', q, k)
        s = scores.shape[-1]
        causal = jnp.tril(jnp.ones((s, s), dtype=bool))
        scores = jnp.where(causal, scores, -jnp.inf)
        scale = 1.0 / jnp.sqrt(jnp.asarray(k.shape[-1], dtype=scores.dtype))
        attn = jax.nn.softmax(scores * scale, axis=-1)
        return jnp.einsum('bqk,bkd->bqd', attn, v)

    def _L1_ffn_ref(x, Wr, br, W1, b1, W2, b2):
        import jax, jax.numpy as jnp
        import numpy as np
        HIDDEN = 256
        NUM_EXPERTS = 8
        TOP_K = 2
        B, S = (4, 256)
        B_, S_, H = x.shape
        xf = x.reshape(-1, H)
        logits = xf @ Wr + br
        topk_w, topk_idx = jax.lax.top_k(logits, TOP_K)
        topk_w = jax.nn.softmax(topk_w, axis=-1)
        gate = jnp.sum(jax.nn.one_hot(topk_idx, NUM_EXPERTS, dtype=xf.dtype) * topk_w[..., None], axis=1)
        h = jax.nn.relu(jnp.einsum('th,ehf->etf', xf, W1) + b1[:, None, :])
        y = jnp.einsum('etf,efh->eth', h, W2) + b2[:, None, :]
        out = jnp.einsum('te,eth->th', gate, y)
        return out.reshape(B_, S_, H)
    h = _L0_tok_ref(x, L0_tok_W, L0_tok_b, L0_tok_cls_token, L0_tok_pos_enc)
    h = h + _L0_attn_ref(_layernorm(h, axis=-1), L0_attn_proj_qk_w, L0_attn_proj_qk_b, L0_attn_proj_v_w, L0_attn_proj_v_b, L0_attn_in_proj_w, L0_attn_in_proj_b, L0_attn_out_proj_w, L0_attn_out_proj_b)
    h = h + _L0_ffn_ref(_layernorm(h, axis=-1), L0_ffn_w1, L0_ffn_conv_w, L0_ffn_conv_b, L0_ffn_w2)
    h = h + _L1_attn_ref(_layernorm(h, axis=-1), L1_attn_Wq, L1_attn_Wk, L1_attn_Wv)
    h = h + _L1_ffn_ref(_layernorm(h, axis=-1), L1_ffn_Wr, L1_ffn_br, L1_ffn_W1, L1_ffn_b1, L1_ffn_W2, L1_ffn_b2)
    return h

_drawn_inputs = setup_inputs


def setup_inputs(seed=0):
    import zlib

    import numpy as np

    out = dict(_drawn_inputs(seed))
    spreads = {}
    factors = {'L0_attn_proj_qk_w': 30.647,
     'L0_attn_proj_qk_b': 64.0,
     'L0_attn_proj_v_b': 21.927,
     'L0_attn_in_proj_b': 4.611,
     'L1_ffn_b1': 6.368,
     'L1_ffn_b2': 3.655}
    for name, (base, spread) in spreads.items():
        noise = np.random.default_rng([zlib.crc32(name.encode()), seed]).standard_normal(out[name].shape)
        drawn = base * np.exp(spread * noise) if base else spread * noise
        out[name] = jnp.asarray(drawn.astype(out[name].dtype))
    for name, factor in factors.items():
        out[name] = (out[name] * factor).astype(out[name].dtype)
    return out
```

```python
from contextlib import ExitStack

import concourse.bass as bass
from concourse import mybir

F32 = mybir.dt.float32
BF16 = mybir.dt.bfloat16
U32 = mybir.dt.uint32
I32 = mybir.dt.int32
ALU = mybir.AluOpType
ACT = mybir.ActivationFunctionType
AX = mybir.AxisListType.X

B, C, IMG, PATCH, D = 32, 3, 96, 16, 256
S = (IMG // PATCH) ** 2 + 1
SEG, HEADS = 4, 8
HD = D // HEADS
SP4 = (S // SEG + 1) * SEG
GI = 8
G = B // GI
T = GI * S
TP = GI * SP4
TILES = [(0, 3), (3, 3), (6, 2)]
NT = len(TILES)
PT = 3 * S
DC = D // 128
FC = C * PATCH * PATCH // 128
HID, HC = 1024, 1024 // 128
E, FF = 8, 512
FFC = FF // 128
ROWS = [n * S for _, n in TILES]
COL = [a * S for a, _ in TILES]
RING = 5
BANKED = (2, 2, 3)
NBLK = (2 * B * S + E * 127) // 128
RS = -(-B * S // 128) * 128 + 128
LEAST = -(-2 * B * S // 128)
DUMMY = E * RS
ROWS_ALL = DUMMY + (NBLK - LEAST) * 128
MAGIC = 1.5 * 2.0 ** 23
QSCALE = float(HD) ** -0.5
ASCALE = float(D) ** -0.5
NEG = -1.0e30


class Signal:

    def __init__(self, sem, per):
        self.sem, self.per = sem, per

    def at(self, g, k):
        return g * self.per + (1 + k)


def vit_tower(nc, a, out):
    ctx = ExitStack()
    with ctx:
        def sb(name, shape, dt=F32):
            return ctx.enter_context(nc.sbuf_tensor(name, shape, dt))

        def pb(name, shape, dt=F32):
            return ctx.enter_context(nc.psum_tensor(name, shape, dt))

        def sem(name):
            return ctx.enter_context(nc.semaphore(name))

        mw1 = sb("mw1", [128, E, DC, FF])
        early = mw1[:].rearrange("p e c f -> p (e c f)")
        at = 0

        def view(shape):
            nonlocal at
            n = shape[0] * shape[1]
            at += n
            return early[:, at - n:at].rearrange("p (a b) -> p a b", b=shape[1])

        w1f, w2f = view([DC, HID]), view([HC, D])
        qkw, pvw, inwT = view([DC, D]), view([DC, D]), view([DC, 3 * D])
        aq, ak = view([DC, D]), view([DC, D])
        tokw = sb("tokw", [128, FC, D])
        rowc = sb("rowc", [PT, D])
        posr = sb("posr", [PT, D])
        qkb = sb("qkb", [128, DC])
        pvb = sb("pvb", [128, DC])
        inb = sb("inb", [128, 3 * DC])
        fusw = sb("fusw", [128, DC, 3 * D])
        fusb = sb("fusb", [128, 3 * DC])
        owT = sb("owT", [128, DC, D])
        ob3 = sb("ob3", [PT, D])
        headsel = sb("headsel", [128, HEADS // DC])
        expsel = sb("expsel", [24, 3, DC, 128])
        w1q = sb("w1q", [128, DC, HID], BF16)
        w2q = sb("w2q", [128, HC, D], BF16)
        wsum = sb("wsum", [128, 2])
        wmean = sb("wmean", [128, 2])
        wscale = sb("wscale", [128, 2])
        wdeq = sb("wdeq", [128, 2])
        convw = sb("convw", [128, HC, 3])
        convb = sb("convb", [128, HC])
        avT = sb("avT", [128, DC, D])
        aqk = sb("aqk", [128, DC, D])
        wr = sb("wr", [128, DC, E])
        brb = sb("brb", [128, 2, E])
        mw2 = sb("mw2", [128, E, FFC, D])
        mb1 = sb("mb1", [128, E, FFC])
        ident = sb("ident", [128, 128])
        onesf = sb("onesf", [128, 128])
        cmask = sb("cmask", [PT, PT])
        cmask2 = sb("cmask2", [PT, PT])
        epsc = sb("epsc", [128, 1])
        magic = sb("magic", [128, 1])
        power = sb("power", [128, NT])
        front = sb("front", [128, FC * T + 3 * DC * TP])
        pat = front[:, 0:FC * T].rearrange("p (c t) -> p c t", t=T)
        prod = front[:, FC * T:].rearrange("p (r c t) -> p r c t", c=DC, t=TP)
        mb2 = front[:, 0:E * D].rearrange("p (e d) -> p e d", d=D)
        hA = sb("hA", [PT, NT, D])
        xnA = sb("xnA", [PT, NT, D])
        xT40 = sb("xT40", [128, DC, TP])
        qT = sb("qT", [128, DC, TP])
        kT = sb("kT", [128, DC, TP])
        vT = sb("vT", [128, DC, TP])
        smax = sb("smax", [128, 3, HEADS])
        ssum = sb("ssum", [128, 3, HEADS])
        sexp = sb("sexp", [128, 3, 3, HEADS])
        prb = sb("prb", [128, 3, 3, HEADS])
        prT = sb("prT", [24, TP])
        pv1, pv2 = qT, kT
        oT = sb("oT", [128, DC, TP])
        oTc = sb("oTc", [128, DC, T])
        hall = sb("hall", [PT, G * NT, D])
        xnB = sb("xnB", [PT, NT, D])
        xq = sb("xq", [PT, NT, D])
        am = sb("am", [PT, NT])
        amr = sb("amr", [PT, NT])
        qsc = sb("qsc", [PT, NT])
        deqs = sb("deqs", [PT, NT])
        am2 = sb("am2", [PT, NT])
        am2r = sb("am2r", [PT, NT])
        qsc2 = sb("qsc2", [PT, NT])
        deqs2 = sb("deqs2", [PT, NT])
        diag = sb("diag", [PT, NT, PT])
        xqT = sb("xqT", [128, DC, T], BF16)
        deqB = sb("deqB", [128, T])
        hpad = sb("hpad", [128, RING, GI, S + 2])
        yc = sb("yc", [128, RING, T])
        v = sb("v", [128, HC, T])
        vmax = sb("vmax", [128, T])
        vq = sb("vq", [128, HC, T], BF16)
        xT3 = sb("xT3", [128, DC, T])
        yT3 = sb("yT3", [128, DC, T])
        V3 = xq
        S3 = sb("S3", [PT, NT, PT])
        P3 = sb("P3", [PT, NT, PT])
        PT3 = S3
        mx3 = sb("mx3", [PT, NT])
        nm3 = sb("nm3", [PT, NT])
        rs3 = sb("rs3", [PT, NT])
        rr3 = sb("rr3", [PT, NT])
        xs = sb("xs", [PT, NT, D])
        lgt = sb("lgt", [PT, NT, E])
        top = sb("top", [PT, NT, 8])
        topi = sb("topi", [PT, NT, 8], U32)
        topf = sb("topf", [PT, NT, 2])
        hot = sb("hot", [PT, 2, NT, E])
        cnt = sb("cnt", [PT, NT, E])
        cntb = sb("cntb", [PT, NT + 1, E], BF16)
        valid = sb("valid", [PT, NT, E])
        iota8 = sb("iota8", [PT, NT, E])
        before = sb("before", [PT, 128], BF16)
        onesb = sb("onesb", [PT, 128], BF16)
        run = sb("run", [128, E])
        base = sb("base", [128, E])
        slot = sb("slot", [PT, NT, E])
        hslot = sb("hslot", [PT, 2, NT, E])
        slotf = sb("slotf", [PT, 2, NT])
        slotu = sb("slotu", [PT, 2, NT], U32)
        slots = sb("slots", [PT, G, 2 * NT], U32)
        gd = sb("gd", [PT, NT])
        ge = sb("ge", [PT, NT])
        gs = sb("gs", [PT, NT])
        gates = sb("gates", [PT, G * NT, 2])
        zeros = sb("zeros", [128, D])
        nblk = sb("nblk", [128, 6, E])
        hots = sb("hots", [PT, G, 2 * NT, E])
        hcor = sb("hcor", [PT, G * 2 * NT])
        slotfs = sb("slotfs", [PT, G, 2 * NT])
        idle = sb("idle", [1, NBLK])
        blkno = sb("blkno", [1, NBLK, E])
        eno = sb("eno", [1, NBLK, E])
        bw = sb("bw", [1, 4, NBLK, E])
        bres = sb("bres", [1, 2, NBLK])
        bint = sb("bint", [1, 2, NBLK], I32)
        padint = sb("padint", [1, E], I32)
        vflat = v[:].rearrange("p m t -> p (m t)")
        hraw = vflat[:, 0:2 * FF].rearrange("p (j f) -> p j f", f=FF)
        hTe = vflat[:, 2 * FF:4 * FF].rearrange("p (j f t) -> p j f t", f=FFC, t=128)
        late = front[:, E * D:]
        xb = late[:, 0:2 * D].rearrange("p (j d) -> p j d", d=D)
        xbT = xT3[:].rearrange("p c t -> p (c t)")[:, 0:512].rearrange("p (j c t) -> p j c t", c=DC, t=128)
        yb = late[:, 2 * D:4 * D].rearrange("p (j d) -> p j d", d=D)
        back = early[0:PT, 0:2 * G * NT * D].rearrange("p (t k d) -> p t k d", k=2, d=D)
        disp = nc.dram_tensor("dispatched", (ROWS_ALL, D), F32, kind="Internal").ap()
        ydisp = nc.dram_tensor("expert_out", (NBLK * 128, D), F32, kind="Internal").ap()
        lnst = [sb(f"lnst{n}", [PT, NT, 6]) for n in range(2)]
        lnmv = [sb(f"lnmv{n}", [PT, NT, 2]) for n in range(2)]
        lnv = [sb(f"lnv{n}", [PT, NT]) for n in range(2)]
        lnr = [sb(f"lnr{n}", [PT, NT]) for n in range(2)]
        psA = pb("psA", [128, 4, 512])
        psB = pb("psB", [128, 4, 512])

        per = dict(
            tok_mm=3, h0=3, st1=3, mv1=3, eps1=1, rstd1=1, xn1=3, hb=1, xT1_ps=1, xT1=1, proj_mm=6, proj_sb=6,
            prods=3, sc_mm=1, smx=5, pexp=1, prT_ps=1, prTs=1, ex_mm=3, pv=5, op_mm=3, h1=3,
            st2=3, mv2=3, eps2=1, rstd2=1, xn2=3, qs1=5, xqs=3, diag1=1, xTq_ps=1, deq_ps=1, xqTs=1, deqBs=1,
            f1_mm=8, deq=8, cact=8, cv1=8, cv2=8, silu=8, vmaxs=1, vT_ps=1, qs2=5, diag2=1, scb_ps=1,
            vsc=2, vqs=2, f2_mm=3, h2=3, st3=3, mv3=3, eps3=1, rstd3=1, xn3=3, xT3_ps=1, xT3s=1,
            yT_ps=1, vv_ps=1, yTs=1, v3s=1, s3_mm=1, s3=5, p3=3, rr=1, pT3_ps=1, pT3s=1, pv3_mm=3, h3=3,
            st4=3, mv4=3, eps4=1, rstd4=1, xn4=3, xT4_ps=1, xT4s=1, lg_mm=1, lg=1,
            rt=16, gexp=1, rank_mm=1)
        per_block = dict(x_turned=1, xTs=1, h_mm=1, hraws=1, h_turned=1, hTs=FFC, y_mm=1, ys=1)
        sg = {k: Signal(sem(k), n) for k, n in (per | per_block).items()}
        dispatched, pads, plan, added = (sem(n) for n in ("dispatched", "pads", "plan", "added"))
        x_loaded = [sem(f"x_loaded{n}") for n in range(2)]
        y_stored = [sem(f"y_stored{n}") for n in range(2)]
        gathered = [sem(f"gathered{n}") for n in range(G * NT)]
        pat_loaded = sem("pat_loaded")
        w_tok, w_attn, w_ffn, w_l1, w_moe = (sem(n) for n in ("w_tok", "w_attn", "w_ffn", "w_l1", "w_moe"))
        setup_dve, setup_pool, setup_pe, setup_act = (sem(n) for n in ("setup_dve", "setup_pool", "setup_pe", "setup_act"))
        out_done = sem("out_done")
        route_cnt = sem("route_cnt")

        block = ctx.enter_context(nc.Block())

        def inc(ins, name):
            ins.then_inc(sg[name].sem, 1)

        def need(eng, name, g, k=None):
            s = sg[name]
            value = s.at(g, s.per if k is None else k)
            if not isinstance(value, int) or value > 1:
                eng.wait_ge(s.sem, value)

        N_TOK, N_ATTN, N_FFN, N_L1, N_MOE = 3 * 16, 8 * 16, 4 * 16, 5 * 16, 4 * 16
        PLAN = 10

        @block.sync
        def _(sp):
            for s in sg.values():
                sp.sem_inc(s.sem, 1)
            sp.dma_start(pat[:], a["pat"][:, 0]).then_inc(pat_loaded, 16)
            loads = [(w_tok, tokw, "tokw"), (w_tok, rowc, "rowc"), (w_tok, posr, "posr"),
                     (w_attn, qkw, "qkw"), (w_attn, inwT, "inwT"), (w_attn, pvw, "pvw"), (w_attn, qkb, "qkb"),
                     (w_attn, pvb, "pvb"), (w_attn, inb, "inb"), (w_attn, owT, "owT"), (w_attn, ob3, "ob3"),
                     (w_ffn, w1f, "w1f"), (w_ffn, w2f, "w2f"), (w_ffn, convw, "convw"), (w_ffn, convb, "convb"),
                     (w_l1, aq, "aq"), (w_l1, ak, "ak"), (w_l1, avT, "avT"), (w_l1, wr, "wr"), (w_l1, brb, "brb")]
            for s, t, n in loads:
                sp.dma_start(t[:], a[n]).then_inc(s, 16)
            for g in range(1, G):
                need(sp, "tok_mm", g - 1)
                sp.dma_start(pat[:], a["pat"][:, g]).then_inc(pat_loaded, 16)
            sp.wait_ge(setup_dve, 7)
            sp.wait_ge(setup_pe, 3)
            for s, t, n in [(w_moe, mw1, "mw1"), (w_moe, mw2, "mw2"), (w_moe, mb1, "mb1")]:
                sp.dma_start(t[:], a[n]).then_inc(s, 16)
            need(sp, "sc_mm", G - 1)
            sp.dma_start(mb2, a["mb2"]).then_inc(w_moe, 16)
            sp.wait_ge(plan, PLAN)
            sp.dma_start(disp[DUMMY:, :].rearrange("(n p) d -> p n d", p=128),
                         zeros[:].unsqueeze(1).to_broadcast([128, NBLK - LEAST, D])).then_inc(pads, 16)
            for e in range(E):
                row = sp.value_load(padint[0:1, e:e + 1], min_val=0, max_val=E * RS - 128)
                sp.dma_start(disp[bass.ds(row, 128), :], zeros[:]).then_inc(pads, 16)
            sp.wait_ge(pads, 16 * (E + 1))
            sp.wait_ge(dispatched, 16 * 2 * G * NT)
            need(sp, "lg_mm", G - 1)

            def load(b, j):
                need(sp, "x_turned", b - 2)
                row = sp.value_load(bint[0:1, 1, bass.ds(b, 1)], min_val=0, max_val=ROWS_ALL - 128)
                sp.dma_start(xb[:, j, :], disp[bass.ds(row, 128), :]).then_inc(x_loaded[j], 16)

            for b in range(2):
                row = sp.value_load(bint[0:1, 1, b:b + 1], min_val=0, max_val=ROWS_ALL - 128)
                sp.dma_start(xb[:, b, :], disp[bass.ds(row, 128), :]).then_inc(x_loaded[b], 16)
            for b in range(2, NBLK):
                load(b, b % 2)
            for t in range(G * NT):
                n = ROWS[t % NT]
                r0 = (t // NT) * T + COL[t % NT]
                sp.wait_ge(added, 2 * t + 2)
                sp.dma_start(out[r0:r0 + n, :], hall[0:n, t, :]).then_inc(out_done, 16)
            sp.wait_ge(out_done, 16 * G * NT)
            sp.wait_ge(w_moe, N_MOE)


        @block.gpsimd
        def _(pool):
            p = nc.gpsimd
            p.memset(ident[:], 0.0)
            p.memset(onesf[:], 1.0)
            p.memset(headsel[:], 1.0)
            p.memset(expsel[:], 1.0)
            p.memset(cmask[:], 0.0)
            p.memset(zeros[:], 0.0)
            p.memset(onesb[:], 1.0)
            p.memset(before[:], 1.0)
            p.memset(valid[:], 1.0)
            p.iota(iota8[:], pattern=[[0, NT], [1, E]], base=0, channel_multiplier=0, allow_small_or_imprecise_dtypes=True)
            p.iota(run[:], pattern=[[RS, E]], base=0, channel_multiplier=0, allow_small_or_imprecise_dtypes=True)
            p.iota(base[:], pattern=[[RS, E]], base=0, channel_multiplier=0, allow_small_or_imprecise_dtypes=True)
            p.iota(blkno[:], pattern=[[1, NBLK], [0, E]], base=0, channel_multiplier=0, allow_small_or_imprecise_dtypes=True)
            p.iota(idle[:], pattern=[[128, NBLK]], base=DUMMY - 128 * LEAST, channel_multiplier=0, allow_small_or_imprecise_dtypes=True)
            p.iota(eno[:], pattern=[[0, NBLK], [1, E]], base=0, channel_multiplier=0, allow_small_or_imprecise_dtypes=True)
            p.memset(power[:], -0.5).then_inc(setup_pool, 1)
            pool.wait_ge(setup_pool, 1)
            p.affine_select(out=ident[:], in_=ident[:], compare_op=ALU.not_equal, fill=1.0, base=0,
                            pattern=[[-1, 128]], channel_multiplier=1)
            p.affine_select(out=before[:], in_=before[:], compare_op=ALU.is_gt, fill=0.0, base=0,
                            pattern=[[1, 128]], channel_multiplier=-1)
            p.affine_select(out=valid[:, 2, :], in_=valid[:, 2, :], compare_op=ALU.is_ge, fill=0.0, base=ROWS[2] - 1,
                            pattern=[[0, E]], channel_multiplier=-1)
            p.affine_select(out=headsel[:], in_=headsel[:], compare_op=ALU.is_ge, fill=0.0, base=0,
                            pattern=[[-HD, HEADS // DC]], channel_multiplier=1).then_inc(setup_pool, 1)
            pool.wait_ge(setup_pool, 2)
            p.affine_select(out=headsel[:], in_=headsel[:], compare_op=ALU.is_ge, fill=0.0, base=HD - 1,
                            pattern=[[HD, HEADS // DC]], channel_multiplier=-1)
            ev = expsel[:].rearrange("p r c (h m) -> p r (c h) m", m=HD)
            p.affine_select(out=ev, in_=ev, compare_op=ALU.is_equal, fill=0.0, base=0,
                            pattern=[[-HEADS, 3], [-1, HEADS], [0, HD]], channel_multiplier=1)
            p.affine_select(out=cmask[:], in_=cmask[:], compare_op=ALU.is_ge, fill=NEG, base=0,
                            pattern=[[-1, PT]], channel_multiplier=1).then_inc(setup_pool, 1)
            pool.wait_ge(setup_pool, 3)
            cv = cmask[:].rearrange("p (n s) -> p n s", s=S)
            p.affine_select(out=cv, in_=cv, compare_op=ALU.is_ge, fill=NEG, base=S - 1,
                            pattern=[[S, 3], [0, S]], channel_multiplier=-1).then_inc(setup_pool, 1)

            def rstd(g, mv, ep, rs, n):
                need(pool, mv, g)
                inc(p.tensor_scalar(lnv[n][:], lnmv[n][:, :, 1], 1e-5, None, ALU.add), ep)
                need(pool, ep, g)
                inc(p.tensor_tensor(lnr[n][:], lnv[n][:], power[0:PT, :], ALU.pow), rs)

            def first(g):
                rstd(g, "mv1", "eps1", "rstd1", 0)
                if isinstance(g, int) and g == 0:
                    pool.wait_ge(w_attn, N_ATTN)
                need(pool, "xn1", g)
                inc(p.tensor_tensor(hA[:], hA[:], ob3[:].unsqueeze(1).to_broadcast([PT, NT, D]), ALU.add), "hb")

            def second(g):
                rstd(g, "mv2", "eps2", "rstd2", 1)
                need(pool, "qs1", g)
                need(pool, "scb_ps", g - 1)
                for i in range(NT):
                    ins = p.tensor_scalar(diag[:, i, :], ident[0:PT, 0:PT], deqs[:, i:i + 1], None, ALU.mult)
                inc(ins, "diag1")
                need(pool, "qs2", g, 4)
                need(pool, "deq_ps", g)
                for i in range(NT):
                    ins = p.tensor_scalar(diag[:, i, :], ident[0:PT, 0:PT], qsc2[:, i:i + 1], None, ALU.mult)
                inc(ins, "diag2")
                need(pool, "f2_mm", g - 1)
                for k in range(2):
                    need(pool, "vsc", g, k + 1)
                    h = slice(k * HC // 2, (k + 1) * HC // 2)
                    inc(p.tensor_scalar(vq[:, h, :], v[:, h, :], MAGIC, -MAGIC, ALU.add, ALU.add), "vqs")
                rstd(g, "mv3", "eps3", "rstd3", 1)
                rstd(g, "mv4", "eps4", "rstd4", 1)
                need(pool, "rt", g)
                for k in range(2):
                    for i in range(NT):
                        n = ROWS[i]
                        p.indirect_dma_start(out=disp, out_offset=bass.IndirectOffsetOnAxis(ap=slotu[0:n, k, i:i + 1], axis=0),
                                             in_=xs[0:n, i, :], in_offset=None).then_inc(dispatched, 16)

            for g in range(G):
                first(g)
                second(g)
            pool.wait_ge(dispatched, 16 * 2 * NT * G)

            def store(b, j):
                need(pool, "ys", b)
                p.dma_start(ydisp[bass.ts(b, 128), :], yb[:, j, :]).then_inc(y_stored[j], 16)

            pool.wait_ge(plan, PLAN)
            for b in range(NBLK):
                store(b, b % 2)
            for j in range(2):
                pool.wait_ge(y_stored[j], 16 * (NBLK // 2))
            pool.wait_ge(plan, PLAN + 3)
            for t in range(G * NT):
                for k in range(2):
                    n = ROWS[t % NT]
                    o = k * NT + t % NT
                    p.indirect_dma_start(out=back[0:n, t, k, :], out_offset=None, in_=ydisp,
                                         in_offset=bass.IndirectOffsetOnAxis(ap=slots[0:n, t // NT, o:o + 1], axis=0))\
                        .then_inc(gathered[t], 16)

        @block.tensor
        def _(pe):
            mm, tr = nc.tensor.matmul, nc.tensor.transpose
            pe.wait_ge(setup_pool, 4)
            pe.wait_ge(w_attn, N_ATTN)
            for j, w in enumerate((qkw, qkw, pvw)):
                for c in range(DC):
                    for m in range(DC):
                        ins = mm(psA[:, j, c * D:(c + 1) * D], w[:, m, c * 128:(c + 1) * 128],
                                 inwT[:, m, j * D:(j + 1) * D], start=(m == 0), stop=(m == DC - 1))
            for o in range(3 * DC):
                b = qkb if o < 2 * DC else pvb
                for m in range(DC):
                    ins = mm(psA[:, 3, o:o + 1], inwT[:, m, o * 128:(o + 1) * 128], b[:, m:m + 1],
                             start=(m == 0), stop=(m == DC - 1))
            ins.then_inc(setup_pe, 1)
            pe.wait_ge(setup_dve, 2)
            mm(psB[:, 0, 0:2], onesf[:], wsum[:], start=True, stop=True).then_inc(setup_pe, 1)
            pe.wait_ge(w_l1, N_L1)
            for c in range(DC):
                for o in range(DC):
                    ins = mm(psB[:, 1, c * D:(c + 1) * D], aq[:, o, c * 128:(c + 1) * 128], ak[:, o, :],
                             start=(o == 0), stop=(o == DC - 1))
            ins.then_inc(setup_pe, 1)
            pe.wait_ge(w_tok, N_TOK)
            pe.wait_ge(setup_act, 2)
            pe.wait_ge(setup_dve, 5)

            def to_columns(src, ps, tile_signal, g, done):
                for i in range(NT):
                    need(pe, tile_signal, g, i + 1)
                    for c in range(DC):
                        ins = tr(ps[:, c, COL[i]:COL[i] + ROWS[i]], src[0:ROWS[i], i, c * 128:(c + 1) * 128],
                                 ident[0:ROWS[i], 0:ROWS[i]])
                inc(ins, done)

            def row_slot(ps, i, b):
                return ps[0:ROWS[i], b + i // 2, (i % 2) * D:(i % 2) * D + D]

            def first(g):
                pe.wait_ge(pat_loaded, g * 16 + 16)
                for i in range(NT):
                    for c in range(FC):
                        ins = mm(row_slot(psA, i, 2), pat[:, c, COL[i]:COL[i] + ROWS[i]], tokw[:, c, :],
                                 start=(c == 0), stop=(c == FC - 1))
                    inc(ins, "tok_mm")
                need(pe, "h1", g - 1)
                to_columns(xnA, psA, "xn1", g, "xT1_ps")
                need(pe, "xT1", g)
                for o, bank in enumerate((2, 3, 0, 1, 2, 3)):
                    if o >= 4:
                        need(pe, "proj_sb", g, o - 3)
                    for c in range(DC):
                        ins = mm(psA[:, bank, 0:TP], fusw[:, c, o * 128:(o + 1) * 128], xT40[:, c, :],
                                 start=(c == 0), stop=(c == DC - 1))
                    inc(ins, "proj_mm")
                for r in range(3):
                    need(pe, "prods", g, r + 1)
                    for t, off in enumerate((0, 128, TP - 128)):
                        for c in range(DC):
                            o = t * 24 + r * 8 + c * 4
                            ins = mm(psA[:, 0, o:o + 4], prod[:, r, c, off:off + 128], headsel[:], start=True, stop=True)
                inc(ins, "sc_mm")
                need(pe, "smx", g)
                for t in range(3):
                    ins = tr(psA[0:24, 1, t * 128:(t + 1) * 128],
                             prb[:, t].rearrange("p r h -> p (r h)"), ident[:])
                inc(ins, "prT_ps")
                need(pe, "prTs", g)
                need(pe, "proj_sb", g)
                for r in range(3):
                    if r == 2:
                        need(pe, "pv", g, 1)
                    for c in range(DC):
                        ins = mm(psA[:, (2, 0, 2)[r] + c, 0:TP], expsel[:, r, c, :], prT[:], start=True, stop=True)
                    inc(ins, "ex_mm")
                need(pe, "pv", g)
                for i in range(NT):
                    for c in range(DC):
                        ins = mm(row_slot(psA, i, 0), oTc[:, c, COL[i]:COL[i] + ROWS[i]], owT[:, c, :],
                                 start=(c == 0), stop=(c == DC - 1))
                    inc(ins, "op_mm")

            def spread(g, done, bank):
                for i in range(NT):
                    ins = mm(psB[:, bank, COL[i]:COL[i] + ROWS[i]], onesf[0:ROWS[i], :],
                             diag[0:ROWS[i], i, 0:ROWS[i]], start=True, stop=True)
                inc(ins, done)

            def second(g):
                need(pe, "lg", g - 1)
                need(pe, "rt", g - 1)
                to_columns(xq, psB, "xqs", g, "xTq_ps")
                need(pe, "diag1", g)
                spread(g, "deq_ps", 2)
                need(pe, "xqTs", g)
                for m in range(HC):
                    if m == 2:
                        need(pe, "deqBs", g)
                    if m >= 4:
                        need(pe, "deq", g, m - 3)
                    for c in range(DC):
                        ins = mm(psB[:, m % 4, 0:T], w1q[:, c, m * 128:(m + 1) * 128], xqT[:, c, :],
                                 start=(c == 0), stop=(c == DC - 1))
                    inc(ins, "f1_mm")
                need(pe, "vmaxs", g)
                for i in range(NT):
                    ins = tr(psB[0:ROWS[i], 0, i * 128:(i + 1) * 128], vmax[:, COL[i]:COL[i] + ROWS[i]], ident[:])
                inc(ins, "vT_ps")
                need(pe, "diag2", g)
                spread(g, "scb_ps", 1)
                need(pe, "vqs", g)
                for i in range(NT):
                    for m in range(HC):
                        ins = mm(row_slot(psB, i, 2), vq[:, m, COL[i]:COL[i] + ROWS[i]], w2q[:, m, :],
                                 start=(m == 0), stop=(m == HC - 1))
                    inc(ins, "f2_mm")
                to_columns(xnB, psB, "xn3", g, "xT3_ps")
                need(pe, "xT3s", g)
                need(pe, "h2", g)
                for o in range(DC):
                    for c in range(DC):
                        ins = mm(psB[:, 2 + o, 0:T], aqk[:, c, o * 128:(o + 1) * 128], xT3[:, c, :],
                                 start=(c == 0), stop=(c == DC - 1))
                inc(ins, "yT_ps")
                for i in range(NT):
                    for c in range(DC):
                        ins = mm(row_slot(psB, i, 0), xT3[:, c, COL[i]:COL[i] + ROWS[i]], avT[:, c, :],
                                 start=(c == 0), stop=(c == DC - 1))
                inc(ins, "vv_ps")
                need(pe, "yTs", g)
                for i in range(NT):
                    cols = slice(COL[i], COL[i] + ROWS[i])
                    for c in range(DC):
                        ins = mm(psB[0:ROWS[i], 2, i * PT:i * PT + ROWS[i]], yT3[:, c, cols], xT3[:, c, cols],
                                 start=(c == 0), stop=(c == DC - 1))
                inc(ins, "s3_mm")
                for i in range(NT):
                    need(pe, "p3", g, i + 1)
                    n = ROWS[i]
                    ins = tr(psB[0:n, 3, i * PT:i * PT + n], P3[0:n, i, 0:n], ident[0:n, 0:n])
                inc(ins, "pT3_ps")
                need(pe, "v3s", g)
                need(pe, "pT3s", g)
                for i in range(NT):
                    n = ROWS[i]
                    ins = mm(row_slot(psB, i, 0), PT3[0:n, i, 0:n], V3[0:n, i, :], start=True, stop=True)
                    inc(ins, "pv3_mm")
                to_columns_x4(g)
                need(pe, "xT4s", g)
                for i in range(NT):
                    for c in range(DC):
                        ins = mm(psB[0:ROWS[i], 0, i * E:(i + 1) * E], xT3[:, c, COL[i]:COL[i] + ROWS[i]], wr[:, c, :],
                                 start=(c == 0), stop=(c == DC - 1))
                inc(ins, "lg_mm")
                need(pe, "rt", g, 5)
                need(pe, "lg", g)
                mm(psB[:, 1, 0:(NT + 1) * E], before[:], cntb[:].rearrange("p t e -> p (t e)"), start=True, stop=False)
                for i in range(NT):
                    ins = mm(psB[:, 1, (i + 1) * E:(NT + 1) * E].rearrange("p (t e) -> p t e", e=E), onesb[:],
                             cntb[:, i, :].unsqueeze(1).to_broadcast([PT, NT - i, E]), start=False, stop=(i == NT - 1))
                inc(ins, "rank_mm")

            def to_columns_x4(g):
                for i in range(NT):
                    need(pe, "xn4", g, i + 1)
                    for c in range(DC):
                        ins = tr(psB[:, 2 + c, COL[i]:COL[i] + ROWS[i]], xs[0:ROWS[i], i, c * 128:(c + 1) * 128],
                                 ident[0:ROWS[i], 0:ROWS[i]])
                inc(ins, "xT4_ps")

            for g in range(G):
                first(g)
                second(g)

            def turn_x(b, j):
                pe.wait_ge(x_loaded[j], (b - j) * 8 + 16)
                need(pe, "xTs", b - 2)
                for c in range(DC):
                    ins = tr(psA[:, j, c * 128:(c + 1) * 128], xb[:, j, c * 128:(c + 1) * 128], ident[:])
                inc(ins, "x_turned")

            def up(b, j):
                e = pe.value_load(bint[0:1, 0, bass.ds(b, 1)], min_val=0, max_val=E - 1)
                need(pe, "xTs", b)
                need(pe, "hraws", b - 2)
                for c in range(DC):
                    ins = mm(psB[:, j, :], xbT[:, j, c, :], mw1[:, bass.ds(e, 1), c, :], start=(c == 0), stop=(c == DC - 1))
                inc(ins, "h_mm")

            def turn_h(b, j):
                need(pe, "hraws", b)
                need(pe, "hTs", b - 2)
                for f in range(FFC):
                    ins = tr(psB[:, 2 + j, f * 128:(f + 1) * 128], hraw[:, j, f * 128:(f + 1) * 128], ident[:])
                inc(ins, "h_turned")

            def down(b, j):
                e = pe.value_load(bint[0:1, 0, bass.ds(b, 1)], min_val=0, max_val=E - 1)
                need(pe, "ys", b - 2)
                for f in range(FFC):
                    need(pe, "hTs", b, f + 1)
                    ins = mm(psA[:, 2 + j, 0:D], hTe[:, j, f, :], mw2[:, bass.ds(e, 1), f, :],
                             start=(f == 0), stop=(f == FFC - 1))
                inc(ins, "y_mm")

            need(pe, "rt", G - 1)
            need(pe, "h1", G - 1)
            pe.wait_ge(plan, PLAN)
            pe.wait_ge(w_moe, N_MOE)
            turn_x(0, 0)
            up(0, 0)
            turn_x(1, 1)
            for b in range(1, NBLK):
                up(b, b % 2)
                turn_h(b - 1, (b - 1) % 2)
                if b + 1 < NBLK:
                    turn_x(b + 1, (b + 1) % 2)
                down(b - 1, (b - 1) % 2)
            turn_h(NBLK - 1, (NBLK - 1) % 2)
            down(NBLK - 1, (NBLK - 1) % 2)

        @block.scalar
        def _(act):
            A = nc.scalar.activation
            act.wait_ge(setup_dve, 1)
            act.wait_ge(setup_pe, 1)
            for j in range(3):
                A(fusw[:, :, j * D:(j + 1) * D], psA[:, j, :].rearrange("p (c d) -> p c d", d=D), ACT.Copy)\
                    .then_inc(setup_act, 1) if j == 2 else \
                    A(fusw[:, :, j * D:(j + 1) * D], psA[:, j, :].rearrange("p (c d) -> p c d", d=D), ACT.Copy)
            act.wait_ge(setup_pe, 3)
            A(aqk[:], psB[:, 1, :].rearrange("p (c d) -> p c d", d=D), ACT.Copy).then_inc(setup_act, 1)
            act.wait_ge(setup_dve, 5)

            def first(g):
                need(act, "xT1_ps", g)
                need(act, "proj_mm", g - 1)
                x4 = xT40[:].rearrange("p c (n s) -> p c n s", s=SP4)
                for c in range(DC):
                    src = psA[:, c, 0:T].rearrange("p (n s) -> p n s", s=S)
                    A(x4[:, c, :, 0:S], src, ACT.Copy)
                    ins = A(x4[:, c, :, S:SP4], src[:, :, 0:SP4 - S], ACT.Copy)
                inc(ins, "xT1")
                need(act, "prods", g - 1)
                need(act, "pv", g - 1)
                for o, bank in enumerate((2, 3, 0, 1, 2, 3)):
                    dst = (qT, qT, kT, kT, vT, vT)[o][:, o % 2, :]
                    need(act, "proj_mm", g, o + 1)
                    inc(A(dst, psA[:, bank, 0:TP], ACT.Identity, bias=fusb[:, o:o + 1], scale=QSCALE if o < 2 else 1.0), "proj_sb")
                need(act, "smx", g, 2)
                inc(A(sexp[:], sexp[:], ACT.Exp), "pexp")
                need(act, "prT_ps", g)
                need(act, "ex_mm", g - 1)
                A(prT[:, 0:256], psA[0:24, 1, 0:256], ACT.Copy)
                inc(A(prT[:, 256:TP], psA[0:24, 1, 256 + (384 - TP):384], ACT.Copy), "prTs")

            def second(g):
                need(act, "qs1", g, 4)
                need(act, "xTq_ps", g - 1)
                for i in range(NT):
                    n = ROWS[i]
                    inc(A(xq[0:n, i, :], xnB[0:n, i, :], ACT.Identity, bias=magic[0:n, :], scale=qsc[0:n, i:i + 1]), "xqs")
                need(act, "deq_ps", g)
                need(act, "deq", g - 1)
                inc(A(deqB[:], psB[:, 2, 0:T], ACT.Copy), "deqBs")
                need(act, "vqs", g - 1)
                for m in range(HC + 3):
                    if m < HC:
                        need(act, "deq", g, m + 1)
                        need(act, "silu", g, max(m - RING + 1, 0))
                        dst = yc[:, m % RING, :].rearrange("p (n s) -> p n s", s=S)
                        inc(A(dst, hpad[:, m % RING, :, 1:S + 1], ACT.Identity, bias=convb[:, m:m + 1],
                              scale=convw[:, m, 1:2]), "cact")
                    if m >= 3:
                        need(act, "cv2", g, m - 2)
                        inc(A(v[:, m - 3, :], yc[:, (m - 3) % RING, :], ACT.Silu), "silu")
                need(act, "xT3_ps", g)
                need(act, "lg_mm", g - 1)
                inc(A(xT3[:], psB[:, 0:2, 0:T], ACT.Copy), "xT3s")
                need(act, "yT_ps", g)
                inc(A(yT3[:], psB[:, 2:4, 0:T], ACT.Copy), "yTs")
                need(act, "vv_ps", g)
                A(V3[:, 0:2, :].rearrange("p i d -> p (i d)"), psB[0:PT, 0, :], ACT.Copy)
                inc(A(V3[0:ROWS[2], 2, :], psB[0:ROWS[2], 1, 0:D], ACT.Copy), "v3s")
                need(act, "s3", g)
                for i in range(NT):
                    n = ROWS[i]
                    inc(A(P3[0:n, i, 0:n], S3[0:n, i, 0:n], ACT.Exp, bias=nm3[0:n, i:i + 1], scale=ASCALE,
                          accum_out=rs3[0:n, i:i + 1]), "p3")
                need(act, "pT3_ps", g)
                n = ROWS[2]
                A(PT3[:, 0:2, :].rearrange("p i q -> p (i q)"), psB[0:PT, 3, 0:2 * PT], ACT.Copy)
                inc(A(PT3[0:n, 2, 0:n], psB[0:n, 3, 2 * PT:2 * PT + n], ACT.Copy), "pT3s")
                need(act, "xT4_ps", g)
                inc(A(xT3[:], psB[:, 2:4, 0:T], ACT.Copy), "xT4s")
                need(act, "rt", g, 10)
                inc(A(ge[:], gd[:], ACT.Exp), "gexp")

            for g in range(G):
                first(g)
                second(g)
            need(act, "rank_mm", G - 1)

            def x_columns(b, j):
                need(act, "x_turned", b)
                need(act, "h_mm", b - 2)
                inc(A(xbT[:, j], psA[:, j, 0:D].rearrange("p (c t) -> p c t", t=128), ACT.Copy), "xTs")

            def h_rows(b, j):
                need(act, "h_mm", b)
                need(act, "h_turned", b - 2)
                inc(A(hraw[:, j, :], psB[:, j, :], ACT.Copy), "hraws")

            x_columns(0, 0)
            for b in range(NBLK):
                if b + 1 < NBLK:
                    x_columns(b + 1, (b + 1) % 2)
                h_rows(b, b % 2)

        @block.vector
        def _(dve):
            d = nc.vector
            for t in (hA, xnB, am2, mx3, rs3, lgt, xs, lnmv[0], lnmv[1]):
                d.memset(t[:], 1.0)
            d.memset(hpad[:], 0.0)
            d.memset(cntb[:], 0.0)
            d.memset(epsc[:], 1e-5)
            d.memset(magic[:], MAGIC).then_inc(setup_dve, 1)
            dve.wait_ge(w_ffn, N_FFN)
            d.tensor_reduce(wsum[:, 0:1], w1f[:].rearrange("p c f -> p (c f)"), AX, ALU.add, apply_absolute_value=True)
            d.tensor_reduce(wsum[:, 1:2], w2f[:].rearrange("p c f -> p (c f)"), AX, ALU.add,
                            apply_absolute_value=True).then_inc(setup_dve, 1)
            dve.wait_ge(setup_pe, 2)
            d.tensor_scalar(wmean[:], psB[:, 0, 0:2], 1.0 / (HID * D), 1e-5, ALU.mult, ALU.max).then_inc(setup_dve, 1)
            dve.wait_ge(setup_dve, 3)
            d.tensor_scalar(wdeq[:], wmean[:], 1.0 / 127.0, None, ALU.mult)
            d.reciprocal(wscale[:], wmean[:]).then_inc(setup_dve, 1)
            dve.wait_ge(setup_dve, 4)
            d.tensor_scalar(w1f[:], w1f[:], wscale[:, 0:1], MAGIC, ALU.mult, ALU.add)
            d.tensor_scalar(w2f[:], w2f[:], wscale[:, 1:2], MAGIC, ALU.mult, ALU.add)
            dve.wait_ge(w_tok, N_TOK)
            d.tensor_tensor(rowc[:], rowc[:], posr[:], ALU.add)
            d.tensor_tensor(fusb[:], psA[:, 3, 0:6], inb[:], ALU.add).then_inc(setup_dve, 1)
            dve.wait_ge(setup_dve, 5)
            d.tensor_scalar(fusb[:, 0:2], fusb[:, 0:2], QSCALE, None, ALU.mult)
            d.tensor_scalar(w1f[:], w1f[:], MAGIC - 1.0, MAGIC + 1.0, ALU.max, ALU.min)
            d.tensor_scalar(w2f[:], w2f[:], MAGIC - 1.0, MAGIC + 1.0, ALU.max, ALU.min).then_inc(setup_dve, 1)
            dve.wait_ge(setup_dve, 6)
            d.tensor_scalar(w1q[:], w1f[:], MAGIC, None, ALU.subtract)
            d.tensor_scalar(w2q[:], w2f[:], MAGIC, None, ALU.subtract).then_inc(setup_dve, 1)
            dve.wait_ge(w_l1, N_L1)

            def stats(g, x, ready, st, mv, n):
                for i in range(NT):
                    r = ROWS[i]
                    need(dve, ready, g, i + 1)
                    inc(d.bn_stats(lnst[n][0:r, i, :], x(i)), st)
                for i in range(NT):
                    need(dve, st, g, i + 1)
                    inc(d.bn_aggr(lnmv[n][0:ROWS[i], i, :], lnst[n][0:ROWS[i], i, :]), mv)

            def normalise(g, x, y, n, rs, done):
                need(dve, rs, g)
                for i in range(NT):
                    r = ROWS[i]
                    inc(d.tensor_scalar(y[0:r, i, :], x(i), lnmv[n][0:r, i, 0:1], lnr[n][0:r, i:i + 1],
                                        ALU.subtract, ALU.mult), done)

            def row_slot(ps, i, b):
                return ps[0:ROWS[i], b + i // 2, (i % 2) * D:(i % 2) * D + D]

            def first(g):
                for i in range(NT):
                    r = ROWS[i]
                    need(dve, "tok_mm", g, BANKED[i])
                    inc(d.tensor_tensor(hA[0:r, i, :], row_slot(psA, i, 2), rowc[0:r, :], ALU.add), "h0")
                stats(g, lambda i: hA[0:ROWS[i], i, :], "h0", "st1", "mv1", 0)
                need(dve, "xT1_ps", g - 1)
                normalise(g, lambda i: hA[0:ROWS[i], i, :], xnA, 0, "rstd1", "xn1")
                need(dve, "proj_sb", g, 4)
                need(dve, "sc_mm", g - 1)
                q4, k4, v4 = (t[:].rearrange("p c (n s) -> p c n s", s=SEG) for t in (qT, kT, vT))
                for r in range(1, SEG):
                    o4 = prod[:, r - 1].rearrange("p c (n s) -> p c n s", s=SEG)
                    d.tensor_tensor(o4[:, :, :, 0:SEG - r], q4[:, :, :, 0:SEG - r], k4[:, :, :, r:SEG], ALU.mult)
                    inc(d.tensor_tensor(o4[:, :, :, SEG - r:SEG], q4[:, :, :, SEG - r:SEG], k4[:, :, :, 0:r], ALU.mult), "prods")
                need(dve, "sc_mm", g)
                sc = psA[:, 0, 0:72].rearrange("p (t r h) -> p t r h", r=3, h=HEADS)
                inc(d.tensor_reduce(smax[:], sc.rearrange("p t r h -> p t h r"), AX, ALU.max), "smx")
                need(dve, "smx", g, 1)
                inc(d.tensor_tensor(sexp[:], sc, smax[:].unsqueeze(2).to_broadcast([128, 3, 3, HEADS]), ALU.subtract), "smx")
                need(dve, "pexp", g)
                inc(d.tensor_reduce(ssum[:], sexp[:].rearrange("p t r h -> p t h r"), AX, ALU.add), "smx")
                need(dve, "smx", g, 3)
                inc(d.reciprocal(smax[:], ssum[:]), "smx")
                need(dve, "smx", g, 4)
                inc(d.tensor_tensor(prb[:], sexp[:], smax[:].unsqueeze(2).to_broadcast([128, 3, 3, HEADS]), ALU.mult), "smx")
                need(dve, "op_mm", g - 1)
                for r in range(1, SEG):
                    bank = (2, 0, 2)[r - 1]
                    dst = (oT, pv1, pv2)[r - 1][:].rearrange("p c (n s) -> p c n s", s=SEG)
                    w4 = psA[:, bank:bank + 2, 0:TP].rearrange("p c (n s) -> p c n s", s=SEG)
                    need(dve, "ex_mm", g, r)
                    if r == 1:
                        need(dve, "proj_sb", g)
                    d.tensor_tensor(dst[:, :, :, 0:SEG - r], w4[:, :, :, 0:SEG - r], v4[:, :, :, r:SEG], ALU.mult)
                    inc(d.tensor_tensor(dst[:, :, :, SEG - r:SEG], w4[:, :, :, SEG - r:SEG], v4[:, :, :, 0:r], ALU.mult), "pv")
                    if r > 1:
                        need(dve, "pv", g, 2 * r - 2)
                        if r == 2:
                            inc(d.tensor_tensor(oT[:], oT[:], pv1[:], ALU.add), "pv")
                        else:
                            a4, b4 = (t[:].rearrange("p c (n s) -> p c n s", s=SP4)[:, :, :, 0:S] for t in (oT, pv2))
                            inc(d.tensor_tensor(oTc[:].rearrange("p c (n s) -> p c n s", s=S), a4, b4, ALU.add), "pv")
                need(dve, "hb", g)
                for i in range(NT):
                    r = ROWS[i]
                    need(dve, "op_mm", g, BANKED[i])
                    inc(d.tensor_tensor(hall[0:r, g * NT + i, :], row_slot(psA, i, 0), hA[0:r, i, :], ALU.add), "h1")

            def scales(g, amx, rec, qs, dq, w, name):
                need(dve, name, g, 1)
                inc(d.tensor_scalar(amx[:], amx[:], 1e-5, None, ALU.max), name)
                need(dve, name, g, 2)
                inc(d.reciprocal(rec[:], amx[:]), name)
                need(dve, name, g, 3)
                inc(d.tensor_scalar(qs[:], rec[:], 127.0, None, ALU.mult), name)
                inc(d.tensor_scalar(dq[:], amx[:], wdeq[0:PT, w:w + 1], None, ALU.mult), name)

            def second(g):
                def row(i):
                    return hall[0:ROWS[i], g * NT + i, :]
                stats(g, row, "h1", "st2", "mv2", 1)
                need(dve, "xT4_ps", g - 1)
                normalise(g, row, xnB, 1, "rstd2", "xn2")
                need(dve, "xn2", g)
                inc(d.tensor_reduce(am[:], xnB[:], AX, ALU.max, apply_absolute_value=True), "qs1")
                scales(g, am, amr, qsc, deqs, 0, "qs1")
                need(dve, "xTq_ps", g)
                need(dve, "f1_mm", g - 1)
                inc(d.tensor_scalar(xqT[:], psB[:, 0:2, 0:T], MAGIC, None, ALU.subtract), "xqTs")
                for m in range(HC + 3):
                    if m < HC:
                        need(dve, "f1_mm", g, m + 1)
                        if m == 0:
                            need(dve, "deqBs", g)
                        need(dve, "cact", g, max(m - RING + 1, 0))
                        need(dve, "cv2", g, max(m - RING + 1, 0))
                        inc(d.tensor_tensor(hpad[:, m % RING, :, 1:S + 1],
                                            psB[:, m % 4, 0:T].rearrange("p (n s) -> p n s", s=S),
                                            deqB[:].rearrange("p (n s) -> p n s", s=S), ALU.mult), "deq")
                    if 2 <= m < HC + 2:
                        j = m - 2
                        y = yc[:, j % RING, :].rearrange("p (n s) -> p n s", s=S)
                        need(dve, "cact", g, j + 1)
                        inc(d.scalar_tensor_tensor(y, hpad[:, j % RING, :, 0:S], convw[:, j, 0:1], y, ALU.mult, ALU.add), "cv1")
                    if m >= 3:
                        j = m - 3
                        y = yc[:, j % RING, :].rearrange("p (n s) -> p n s", s=S)
                        need(dve, "cv1", g, j + 1)
                        inc(d.scalar_tensor_tensor(y, hpad[:, j % RING, :, 2:S + 2], convw[:, j, 2:3], y, ALU.mult, ALU.add), "cv2")
                need(dve, "silu", g)
                inc(d.tensor_reduce(vmax[:], v[:].rearrange("p m t -> p t m"), AX, ALU.max, apply_absolute_value=True), "vmaxs")
                need(dve, "vT_ps", g)
                d.tensor_reduce(am2[:, 0:2], psB[0:PT, 0, 0:256].rearrange("p (i k) -> p i k", k=128), AX, ALU.max)
                inc(d.tensor_reduce(am2[0:ROWS[2], 2:3], psB[0:ROWS[2], 0, 256:384], AX, ALU.max), "qs2")
                scales(g, am2, am2r, qsc2, deqs2, 1, "qs2")
                need(dve, "scb_ps", g)
                for k in range(2):
                    h = slice(k * HC // 2, (k + 1) * HC // 2)
                    inc(d.tensor_tensor(v[:, h, :], v[:, h, :],
                                        psB[:, 1, 0:T].unsqueeze(1).to_broadcast([128, HC // 2, T]), ALU.mult), "vsc")
                for i in range(NT):
                    need(dve, "f2_mm", g, BANKED[i])
                    inc(d.scalar_tensor_tensor(row(i), row_slot(psB, i, 2), deqs2[0:ROWS[i], i:i + 1], row(i),
                                               ALU.mult, ALU.add), "h2")
                stats(g, row, "h2", "st3", "mv3", 1)
                normalise(g, row, xnB, 1, "rstd3", "xn3")
                need(dve, "s3_mm", g)
                need(dve, "p3", g - 1)
                n = ROWS[2]
                s3v = psB[0:PT, 2, 0:2 * PT].rearrange("p (i q) -> p i q", q=PT)
                inc(d.tensor_tensor(S3[:, 0:2, :], s3v, cmask[:].unsqueeze(1).to_broadcast([PT, 2, PT]), ALU.add), "s3")
                inc(d.tensor_tensor(S3[0:n, 2, 0:n], psB[0:n, 2, 2 * PT:2 * PT + n], cmask[0:n, 0:n], ALU.add), "s3")
                need(dve, "s3", g, 1)
                inc(d.tensor_reduce(mx3[:, 0:2], S3[:, 0:2, :], AX, ALU.max), "s3")
                need(dve, "s3", g, 2)
                inc(d.tensor_reduce(mx3[0:n, 2:3], S3[0:n, 2, 0:n], AX, ALU.max), "s3")
                need(dve, "s3", g, 4)
                inc(d.tensor_scalar(nm3[:], mx3[:], -ASCALE, None, ALU.mult), "s3")
                need(dve, "p3", g)
                inc(d.reciprocal(rr3[:], rs3[:]), "rr")
                need(dve, "rr", g)
                for i in range(NT):
                    need(dve, "pv3_mm", g, BANKED[i])
                    inc(d.scalar_tensor_tensor(row(i), row_slot(psB, i, 0), rr3[0:ROWS[i], i:i + 1], row(i),
                                               ALU.mult, ALU.add), "h3")
                stats(g, row, "h3", "st4", "mv4", 1)
                dve.wait_ge(dispatched, 16 * 2 * NT * g) if not isinstance(g, int) or g else None
                normalise(g, row, xs, 1, "rstd4", "xn4")
                need(dve, "lg_mm", g)
                n = ROWS[2]
                d.tensor_tensor(lgt[:, 0:2, :], psB[0:PT, 0, 0:2 * E].rearrange("p (i e) -> p i e", e=E),
                                brb[0:PT], ALU.add)
                inc(d.tensor_tensor(lgt[0:n, 2, :], psB[0:n, 0, 2 * E:3 * E], brb[0:n, 0, :], ALU.add), "lg")
                need(dve, "lg", g)
                for i in range(NT):
                    ins = d.max(top[:, i, :], lgt[:, i, :])
                inc(ins, "rt")
                need(dve, "rt", g, 1)
                for i in range(NT):
                    ins = d.max_index(topi[:, i, :], top[:, i, :], lgt[:, i, :])
                inc(ins, "rt")
                need(dve, "rt", g, 2)
                inc(d.tensor_copy(topf[:], topi[:, :, 0:2]), "rt")
                need(dve, "rt", g, 3)
                for k in range(2):
                    ins = d.tensor_tensor(hot[:, k], iota8[:], topf[:, :, k:k + 1].to_broadcast([PT, NT, E]), ALU.is_equal)
                inc(ins, "rt")
                need(dve, "rt", g, 4)
                d.tensor_tensor(cnt[:], hot[:, 0], hot[:, 1], ALU.add).then_inc(route_cnt, 1)
                dve.wait_ge(route_cnt, g + 1)
                inc(d.tensor_tensor(cntb[:, 0:NT, :], cnt[:], valid[:], ALU.mult), "rt")
                need(dve, "rank_mm", g)
                inc(d.tensor_tensor(slot[:], psB[0:PT, 1, 0:NT * E].rearrange("p (t e) -> p t e", e=E),
                                    run[0:PT].unsqueeze(1).to_broadcast([PT, NT, E]), ALU.add), "rt")
                need(dve, "rt", g, 6)
                inc(d.tensor_tensor(run[:], psB[:, 1, NT * E:(NT + 1) * E], run[:], ALU.add), "rt")
                for k in range(2):
                    ins = d.tensor_tensor(hslot[:, k], hot[:, k], slot[:], ALU.mult)
                inc(ins, "rt")
                need(dve, "rt", g, 8)
                inc(d.tensor_reduce(slotf[:], hslot[:], AX, ALU.add), "rt")
                inc(d.tensor_tensor(gd[:], top[:, :, 1], top[:, :, 0], ALU.subtract), "rt")
                need(dve, "rt", g, 9)
                inc(d.tensor_copy(slotu[:], slotf[:]), "rt")
                d.tensor_copy(hots[:, g], hot[:].rearrange("p k t e -> p (k t) e"))
                inc(d.tensor_copy(slotfs[:, g, :], slotf[:].rearrange("p k t -> p (k t)")), "rt")
                need(dve, "gexp", g)
                inc(d.tensor_scalar(gs[:], ge[:], 1.0, None, ALU.add), "rt")
                need(dve, "rt", g, 13)
                gt = gates[:, bass.ts(g, NT), :]
                inc(d.reciprocal(gd[:], gs[:]), "rt")
                need(dve, "rt", g, 14)
                inc(d.tensor_copy(gt[:, :, 0], gd[:]), "rt")
                inc(d.tensor_tensor(gt[:, :, 1], gd[:], ge[:], ALU.mult), "rt")

            for g in range(G):
                first(g)
                second(g)

            steps = [0]

            def step(ins):
                ins.then_inc(plan, 1)
                steps[0] += 1
                dve.wait_ge(plan, steps[0])

            used, whole, end, start, off, shift = (nblk[:, n, :] for n in range(6))
            need(dve, "rt", G - 1)
            d.tensor_copy(padint[:], run[0:1, :])
            step(d.tensor_tensor(used, run[:], base[:], ALU.subtract))
            step(d.tensor_scalar(whole, used, 1.0 / 128, 127.0 / 256, ALU.mult, ALU.add))
            step(d.tensor_scalar(whole, whole, MAGIC, -MAGIC, ALU.add, ALU.add))
            step(d.tensor_tensor_scan(end, onesf[:, 0:E], whole, 0.0, ALU.mult, ALU.add))
            step(d.tensor_tensor(start, end, whole, ALU.subtract))
            d.tensor_tensor(bw[0:1, 0], blkno[:], nblk[0:1, 3, :].unsqueeze(1).to_broadcast([1, NBLK, E]), ALU.is_ge)
            d.tensor_tensor(bw[0:1, 1], blkno[:], nblk[0:1, 2, :].unsqueeze(1).to_broadcast([1, NBLK, E]), ALU.is_ge)
            step(d.scalar_tensor_tensor(shift, start, 128.0, base[:], ALU.mult, ALU.subtract))
            d.tensor_tensor(bw[0:1, 2], bw[0:1, 0], bw[0:1, 1], ALU.subtract)
            step(d.tensor_scalar(off, shift, -1.0, float(128 * LEAST - DUMMY), ALU.mult, ALU.add))
            d.tensor_tensor(bw[0:1, 0], bw[0:1, 2], eno[:], ALU.mult)
            step(d.tensor_tensor(bw[0:1, 1], bw[0:1, 2], nblk[0:1, 4, :].unsqueeze(1).to_broadcast([1, NBLK, E]), ALU.mult))
            step(d.tensor_reduce(bres[:], bw[0:1, 0:2], AX, ALU.add))
            d.tensor_copy(bint[0:1, 0], bres[0:1, 0])
            step(d.tensor_tensor(bint[0:1, 1], bres[0:1, 1], idle[:], ALU.add))
            assert steps[0] == PLAN
            hv = hots[:].rearrange("p g j e -> p (g j) e")
            step(d.tensor_tensor(hv, hv, nblk[0:PT, 5, :].unsqueeze(1).to_broadcast([PT, G * 2 * NT, E]), ALU.mult))
            step(d.tensor_reduce(hcor[:], hv, AX, ALU.add))
            step(d.tensor_tensor(slots[:].rearrange("p g j -> p (g j)"), slotfs[:].rearrange("p g j -> p (g j)"), hcor[:], ALU.add))

            def h_columns(b, j):
                e = dve.value_load(bint[0:1, 0, bass.ds(b, 1)], min_val=0, max_val=E - 1)
                need(dve, "h_turned", b)
                need(dve, "y_mm", b - 2)
                for f in range(FFC):
                    inc(d.tensor_scalar(hTe[:, j, f, :], psB[:, 2 + j, f * 128:(f + 1) * 128],
                                        mb1[:, bass.ds(e, 1), f], 0.0, ALU.add, ALU.max), "hTs")
                return e

            def y_rows(b, j, e):
                need(dve, "y_mm", b)
                if not isinstance(b, int) or b >= 2:
                    dve.wait_ge(y_stored[j], (b - j) * 8)
                inc(d.tensor_tensor(yb[:, j, :], psA[:, 2 + j, 0:D], mb2[:, bass.ds(e, 1), :], ALU.add), "ys")

            dve.wait_ge(w_moe, N_MOE)
            for b in range(NBLK):
                y_rows(b, b % 2, h_columns(b, b % 2))
            for t in range(G * NT):
                n = ROWS[t % NT]
                for k in range(2):
                    if k == 0:
                        dve.wait_ge(gathered[t], 32)
                    if k:
                        dve.wait_ge(added, 2 * t + 1)
                    d.scalar_tensor_tensor(hall[0:n, t, :], back[0:n, t, k, :], gates[0:n, t, k:k + 1], hall[0:n, t, :],
                                           ALU.mult, ALU.add).then_inc(added, 1)


def lay_out(i):
    import numpy as np
    f = np.ascontiguousarray

    def cols(w):
        w = np.asarray(w)
        return f(w.reshape(w.shape[0] // 128, 128, -1).transpose(1, 0, 2))

    def vec(b):
        return f(np.asarray(b).reshape(-1, 128).T)

    x = np.asarray(i["x"])
    n = IMG // PATCH
    pt = x.reshape(B, C, n, PATCH, n, PATCH).transpose(1, 3, 5, 0, 2, 4).reshape(C * PATCH * PATCH, B, n * n)
    pat = np.zeros((C * PATCH * PATCH, B, S), x.dtype)
    pat[:, :, 1:] = pt
    pat = f(pat.reshape(FC, 128, G, T).transpose(1, 2, 0, 3))
    row = np.concatenate([np.asarray(i["L0_tok_cls_token"])[0], np.tile(np.asarray(i["L0_tok_b"])[None], (S - 1, 1))])
    w1, w2 = np.asarray(i["L1_ffn_W1"]), np.asarray(i["L1_ffn_W2"])
    o = {
        "pat": pat, "tokw": cols(np.asarray(i["L0_tok_W"]).T),
        "rowc": f(np.tile(row, (3, 1))), "posr": f(np.tile(np.asarray(i["L0_tok_pos_enc"])[0], (3, 1))),
        "qkw": cols(i["L0_attn_proj_qk_w"]), "pvw": cols(i["L0_attn_proj_v_w"]),
        "inwT": cols(np.asarray(i["L0_attn_in_proj_w"]).T), "qkb": vec(i["L0_attn_proj_qk_b"]),
        "pvb": vec(i["L0_attn_proj_v_b"]), "inb": vec(i["L0_attn_in_proj_b"]),
        "owT": cols(np.asarray(i["L0_attn_out_proj_w"]).T),
        "ob3": f(np.tile(np.asarray(i["L0_attn_out_proj_b"])[None], (PT, 1))),
        "w1f": cols(np.asarray(i["L0_ffn_w1"]).T), "w2f": cols(np.asarray(i["L0_ffn_w2"]).T),
        "convw": cols(np.asarray(i["L0_ffn_conv_w"]).reshape(HID, 3)), "convb": vec(i["L0_ffn_conv_b"]),
        "aq": cols(i["L1_attn_Wq"]), "ak": cols(i["L1_attn_Wk"]), "avT": cols(np.asarray(i["L1_attn_Wv"]).T),
        "wr": cols(i["L1_ffn_Wr"]), "brb": f(np.tile(np.asarray(i["L1_ffn_br"])[None, None], (128, 2, 1))),
        "mw1": f(w1.reshape(E, DC, 128, FF).transpose(2, 0, 1, 3)),
        "mw2": f(w2.reshape(E, FFC, 128, D).transpose(2, 0, 1, 3)),
        "mb1": f(np.asarray(i["L1_ffn_b1"]).reshape(E, FFC, 128).transpose(2, 0, 1)),
        "mb2": f(np.tile(np.asarray(i["L1_ffn_b2"])[None], (128, 1, 1))),
    }
    return o


def kernel(**inputs):
    import concourse.bacc as bacc
    from concourse.bass_utils import run_bass_kernel_spmd

    nc = bacc.Bacc("TRN2", target_bir_lowering=False, num_devices=1)
    arrays = {f"in_{k}": v for k, v in lay_out(inputs).items()}
    aps = {k[3:]: nc.dram_tensor(k, v.shape, mybir.dt.from_np(v.dtype), kind="ExternalInput").ap()
           for k, v in arrays.items()}
    out = nc.dram_tensor("out_rows", (B * S, D), F32, kind="ExternalOutput").ap()
    vit_tower(nc, aps, out)
    r = run_bass_kernel_spmd(nc, [arrays], core_ids=[0])
    return r.results[0]["out_rows"].reshape(B, S, D)
```

```python
from contextlib import ExitStack

import concourse.bass as bass
from concourse import mybir

F32 = mybir.dt.float32
BF16 = mybir.dt.bfloat16
U32 = mybir.dt.uint32
I32 = mybir.dt.int32
ALU = mybir.AluOpType
ACT = mybir.ActivationFunctionType
AX = mybir.AxisListType.X

B, C, IMG, PATCH, D = 32, 3, 96, 16, 256
S = (IMG // PATCH) ** 2 + 1
SEG, HEADS = 4, 8
HD = D // HEADS
SP4 = (S // SEG + 1) * SEG
GI = 8
G = B // GI
T = GI * S
TP = GI * SP4
TILES = [(0, 3), (3, 3), (6, 2)]
NT = len(TILES)
PT = 3 * S
DC = D // 128
FC = C * PATCH * PATCH // 128
HID, HC = 1024, 1024 // 128
E, FF = 8, 512
FFC = FF // 128
ROWS = [n * S for _, n in TILES]
COL = [a * S for a, _ in TILES]
RING = 5
BANKED = (2, 2, 3)
NBLK = (2 * B * S + E * 127) // 128
RS = -(-B * S // 128) * 128 + 128
LEAST = -(-2 * B * S // 128)
DUMMY = E * RS
ROWS_ALL = DUMMY + (NBLK - LEAST) * 128
MAGIC = 1.5 * 2.0 ** 23
QSCALE = float(HD) ** -0.5
ASCALE = float(D) ** -0.5
NEG = -1.0e30


ORDER = ("a_tok b_ln2 c_st3 b_norm2 c_ln3 b_q c_cols3 b_f1a c_yv a_ln a_norm a_cols c_sc b_f1b a_proj c_pv "
         "a_prod b_amax c_ln4 a_soft b_spread c_cols4 a_pv c_rt b_f2 c_rank a_out c_slot").split()


class Signal:

    def __init__(self, sem, per):
        self.sem, self.per = sem, per

    def at(self, g, k):
        return g * self.per + (1 + k)


def vit_tower(nc, a, out):
    ctx = ExitStack()
    with ctx:
        def sb(name, shape, dt=F32):
            return ctx.enter_context(nc.sbuf_tensor(name, shape, dt))

        def pb(name, shape, dt=F32):
            return ctx.enter_context(nc.psum_tensor(name, shape, dt))

        def sem(name):
            return ctx.enter_context(nc.semaphore(name))

        mw1 = sb("mw1", [128, E, DC, FF])
        early = mw1[:].rearrange("p e c f -> p (e c f)")
        at = 0

        def view(shape):
            nonlocal at
            n = shape[0] * shape[1]
            at += n
            return early[:, at - n:at].rearrange("p (a b) -> p a b", b=shape[1])

        w1f, w2f = view([DC, HID]), view([HC, D])
        qkw, pvw, inwT = view([DC, D]), view([DC, D]), view([DC, 3 * D])
        aq, ak = view([DC, D]), view([DC, D])
        tokw = sb("tokw", [128, FC, D])
        rowc = sb("rowc", [PT, D])
        posr = early[0:PT, at:at + D]
        qkb = sb("qkb", [128, DC])
        pvb = sb("pvb", [128, DC])
        inb = sb("inb", [128, 3 * DC])
        fusw = sb("fusw", [128, DC, 3 * D])
        fusb = sb("fusb", [128, 3 * DC])
        owT = sb("owT", [128, DC, D])
        ob3 = sb("ob3", [PT, D])
        headsel = sb("headsel", [128, HEADS // DC])
        expsel = sb("expsel", [24, 3, DC, 128])
        w1q = sb("w1q", [128, DC, HID], BF16)
        w2q = sb("w2q", [128, HC, D], BF16)
        wsum = sb("wsum", [128, 2])
        wmean = sb("wmean", [128, 2])
        wscale = sb("wscale", [128, 2])
        wdeq = sb("wdeq", [128, 2])
        convw = sb("convw", [128, HC, 3])
        convb = sb("convb", [128, HC])
        avT = sb("avT", [128, DC, D])
        aqk = sb("aqk", [128, DC, D])
        wr = sb("wr", [128, DC, E])
        brb = sb("brb", [128, 2, E])
        mw2 = sb("mw2", [128, E, FFC, D])
        mb1 = sb("mb1", [128, E, FFC])
        ident = sb("ident", [128, 128])
        onesf = sb("onesf", [128, 128])
        cmask = sb("cmask", [PT, PT])
        magic = sb("magic", [128, 1])
        power = sb("power", [128, NT])
        front = sb("front", [128, FC * T + 3 * DC * TP])
        pat = front[:, 0:FC * T].rearrange("p (c t) -> p c t", t=T)
        prod = front[:, FC * T:].rearrange("p (r c t) -> p r c t", c=DC, t=TP)
        mb2 = front[:, 0:E * D].rearrange("p (e d) -> p e d", d=D)
        hA = sb("hA", [PT, NT, D])
        xnA = sb("xnA", [PT, NT, D])
        xT40 = sb("xT40", [128, DC, TP])
        qT = sb("qT", [128, DC, TP])
        kT = sb("kT", [128, DC, TP])
        vT = sb("vT", [128, DC, TP])
        smax = sb("smax", [128, 3, HEADS])
        ssum = sb("ssum", [128, 3, HEADS])
        sexp = sb("sexp", [128, 3, 3, HEADS])
        prb = sb("prb", [128, 3, 3, HEADS])
        prT = sb("prT", [24, TP])
        pv1, pv2 = qT, kT
        oT = sb("oT", [128, DC, TP])
        oTc = sb("oTc", [128, DC, T])
        hall = sb("hall", [PT, G * NT, D])
        xnB = sb("xnB", [PT, NT, D])
        xq = sb("xq", [PT, NT, D])
        am = sb("am", [PT, NT])
        amr = sb("amr", [PT, NT])
        qsc = sb("qsc", [PT, NT])
        deqs = sb("deqs", [PT, NT])
        am2 = sb("am2", [PT, NT])
        am2r = sb("am2r", [PT, NT])
        qsc2 = sb("qsc2", [PT, NT])
        deqs2 = sb("deqs2", [PT, NT])
        diag = sb("diag", [PT, NT, PT])
        xqT = sb("xqT", [128, DC, T], BF16)
        deqB = sb("deqB", [128, T])
        hpad = sb("hpad", [128, RING, GI, S + 2])
        yc = sb("yc", [128, RING, T])
        v = sb("v", [128, HC, T])
        vmax = sb("vmax", [128, T])
        vq = sb("vq", [128, HC, T], BF16)
        xT3 = sb("xT3", [128, DC, T])
        yT3 = sb("yT3", [128, DC, T])
        V3 = sb("V3", [PT, NT, D])
        S3 = sb("S3", [PT, NT, PT])
        P3 = sb("P3", [PT, NT, PT])
        PT3 = S3
        mx3 = sb("mx3", [PT, NT])
        nm3 = sb("nm3", [PT, NT])
        rs3 = sb("rs3", [PT, NT])
        rr3 = sb("rr3", [PT, NT])
        xs = sb("xs", [PT, NT, D])
        lgt = sb("lgt", [PT, NT, E])
        top = sb("top", [PT, NT, 8])
        topi = sb("topi", [PT, NT, 8], U32)
        topf = sb("topf", [PT, NT, 2])
        hot = sb("hot", [PT, 2, NT, E])
        cnt = sb("cnt", [PT, NT, E])
        cntb = sb("cntb", [PT, NT + 1, E], BF16)
        valid = sb("valid", [PT, NT, E])
        iota8 = sb("iota8", [PT, NT, E])
        before = sb("before", [PT, 128], BF16)
        onesb = sb("onesb", [PT, 128], BF16)
        run = sb("run", [128, E])
        base = sb("base", [128, E])
        slot = sb("slot", [PT, NT, E])
        hslot = sb("hslot", [PT, 2, NT, E])
        slotf = sb("slotf", [PT, 2, NT])
        slotu = sb("slotu", [PT, 2, NT], U32)
        slots = sb("slots", [PT, G, 2 * NT], U32)
        gd = sb("gd", [PT, NT])
        ge = sb("ge", [PT, NT])
        gs = sb("gs", [PT, NT])
        gates = sb("gates", [PT, G * NT, 2])
        zeros = sb("zeros", [128, D])
        nblk = sb("nblk", [128, 6, E])
        hots = sb("hots", [PT, G, 2 * NT, E])
        hcor = sb("hcor", [PT, G * 2 * NT])
        slotfs = sb("slotfs", [PT, G, 2 * NT])
        idle = sb("idle", [1, NBLK])
        blkno = sb("blkno", [1, NBLK, E])
        eno = sb("eno", [1, NBLK, E])
        bw = yc[0:1].rearrange("p j t -> p (j t)")[:, 0:4 * NBLK * E].rearrange("p (j b e) -> p j b e", b=NBLK, e=E)
        bres = sb("bres", [1, 2, NBLK])
        bint = sb("bint", [1, 2, NBLK], I32)
        padint = sb("padint", [1, E], I32)
        vflat = v[:].rearrange("p m t -> p (m t)")
        hraw = vflat[:, 0:2 * FF].rearrange("p (j f) -> p j f", f=FF)
        hTe = vflat[:, 2 * FF:4 * FF].rearrange("p (j f t) -> p j f t", f=FFC, t=128)
        late = front[:, E * D:]
        xb = late[:, 0:2 * D].rearrange("p (j d) -> p j d", d=D)
        xbT = xT3[:].rearrange("p c t -> p (c t)")[:, 0:512].rearrange("p (j c t) -> p j c t", c=DC, t=128)
        yb = late[:, 2 * D:4 * D].rearrange("p (j d) -> p j d", d=D)
        back = early[0:PT, 0:2 * G * NT * D].rearrange("p (t k d) -> p t k d", k=2, d=D)
        disp = nc.dram_tensor("dispatched", (ROWS_ALL, D), F32, kind="Internal").ap()
        ydisp = nc.dram_tensor("expert_out", (NBLK * 128, D), F32, kind="Internal").ap()
        lnst = [sb(f"lnst{n}", [PT, NT, 6]) for n in range(3)]
        lnmv = [sb(f"lnmv{n}", [PT, NT, 2]) for n in range(3)]
        lnv = [sb(f"lnv{n}", [PT, NT]) for n in range(3)]
        lnr = [sb(f"lnr{n}", [PT, NT]) for n in range(3)]
        psA = pb("psA", [128, 4, 512])
        psB = pb("psB", [128, 4, 512])

        per = dict(
            tok_mm=3, h0=3, st1=3, mv1=3, eps1=1, rstd1=1, xn1=3, hb=1, xT1_ps=1, xT1=1, proj_mm=6, proj_sb=6,
            prods=3, sc_mm=1, smx=5, pexp=1, prT_ps=1, prTs=1, ex_mm=3, pv=5, op_mm=3, h1=3,
            st2=3, mv2=3, eps2=1, rstd2=1, xn2=3, qs1=5, xqs=3, diag1=1, xTq_ps=1, deq_ps=1, xqTs=1, deqBs=1,
            f1_mm=8, deq=8, cact=8, cv1=8, cv2=8, silu=8, vmaxs=1, vT_ps=1, qs2=5, diag2=1, scb_ps=1,
            vsc=2, vqs=2, f2_mm=3, h2=3, st3=3, mv3=3, eps3=1, rstd3=1, xn3=3, xT3_ps=1, xT3s=1,
            yT_ps=1, vv_ps=1, yTs=1, v3s=1, s3_mm=1, s3=5, p3=3, rr=1, pT3_ps=1, pT3s=1, pv3_mm=3, h3=3,
            st4=3, mv4=3, eps4=1, rstd4=1, xn4=3, xT4_ps=1, xT4s=1, lg_mm=1, lg=1,
            rt=16, gexp=1, rank_mm=1)
        per_block = dict(x_turned=1, xTs=1, h_mm=1, hraws=1, h_turned=1, hTs=FFC, y_mm=1, ys=1)
        sg = {k: Signal(sem(k), n) for k, n in (per | per_block).items()}
        dispatched, pads, plan, added = (sem(n) for n in ("dispatched", "pads", "plan", "added"))
        x_loaded = [sem(f"x_loaded{n}") for n in range(2)]
        y_stored = [sem(f"y_stored{n}") for n in range(2)]
        gathered = [sem(f"gathered{n}") for n in range(G * NT)]
        pat_loaded = sem("pat_loaded")
        w_tok, w_attn, w_ffn, w_l1, w_moe = (sem(n) for n in ("w_tok", "w_attn", "w_ffn", "w_l1", "w_moe"))
        setup_dve, setup_pool, setup_pe, setup_act = (sem(n) for n in ("setup_dve", "setup_pool", "setup_pe", "setup_act"))
        out_done = sem("out_done")
        route_cnt = sem("route_cnt")

        block = ctx.enter_context(nc.Block())

        def in_order(*parts):
            mine = {f.__name__: f for f in parts}
            for period in range(G + 2):
                for step in ORDER:
                    g = period - "abc".index(step[0])
                    if step in mine and 0 <= g < G:
                        mine[step](g)

        def inc(ins, name):
            ins.then_inc(sg[name].sem, 1)

        def need(eng, name, g, k=None):
            s = sg[name]
            value = s.at(g, s.per if k is None else k)
            if not isinstance(value, int) or value > 1:
                eng.wait_ge(s.sem, value)

        N_TOK, N_ATTN, N_FFN, N_L1, N_MOE = 3 * 16, 8 * 16, 4 * 16, 5 * 16, 4 * 16
        PLAN = 10

        @block.sync
        def _(sp):
            for s in sg.values():
                sp.sem_inc(s.sem, 1)
            sp.dma_start(pat[:], a["pat"][:, 0]).then_inc(pat_loaded, 16)
            loads = [(w_tok, tokw[:], "tokw"), (w_tok, rowc[:], "rowc"), (w_tok, posr, "posr"),
                     (w_attn, qkw, "qkw"), (w_attn, inwT, "inwT"), (w_attn, pvw, "pvw"), (w_attn, qkb[:], "qkb"),
                     (w_attn, pvb[:], "pvb"), (w_attn, inb[:], "inb"), (w_attn, owT[:], "owT"), (w_attn, ob3[:], "ob3"),
                     (w_ffn, w1f, "w1f"), (w_ffn, w2f, "w2f"), (w_ffn, convw[:], "convw"), (w_ffn, convb[:], "convb"),
                     (w_l1, aq, "aq"), (w_l1, ak, "ak"), (w_l1, avT[:], "avT"), (w_l1, wr[:], "wr"), (w_l1, brb[:], "brb")]
            for s, t, n in loads:
                sp.dma_start(t, a[n]).then_inc(s, 16)
            for g in range(1, G):
                need(sp, "tok_mm", g - 1)
                sp.dma_start(pat[:], a["pat"][:, g]).then_inc(pat_loaded, 16)
            sp.wait_ge(setup_dve, 7)
            sp.wait_ge(setup_pe, 3)
            for s, t, n in [(w_moe, mw1[:], "mw1"), (w_moe, mw2[:], "mw2"), (w_moe, mb1[:], "mb1")]:
                sp.dma_start(t, a[n]).then_inc(s, 16)
            need(sp, "sc_mm", G - 1)
            sp.dma_start(mb2, a["mb2"]).then_inc(w_moe, 16)
            sp.wait_ge(plan, PLAN)
            sp.dma_start(disp[DUMMY:, :].rearrange("(n p) d -> p n d", p=128),
                         zeros[:].unsqueeze(1).to_broadcast([128, NBLK - LEAST, D])).then_inc(pads, 16)
            for e in range(E):
                row = sp.value_load(padint[0:1, e:e + 1], min_val=0, max_val=E * RS - 128)
                sp.dma_start(disp[bass.ds(row, 128), :], zeros[:]).then_inc(pads, 16)
            sp.wait_ge(pads, 16 * (E + 1))
            sp.wait_ge(dispatched, 16 * 2 * G * NT)
            need(sp, "lg_mm", G - 1)

            def load(b, j):
                need(sp, "x_turned", b - 2)
                row = sp.value_load(bint[0:1, 1, bass.ds(b, 1)], min_val=0, max_val=ROWS_ALL - 128)
                sp.dma_start(xb[:, j, :], disp[bass.ds(row, 128), :]).then_inc(x_loaded[j], 16)

            for b in range(2):
                row = sp.value_load(bint[0:1, 1, b:b + 1], min_val=0, max_val=ROWS_ALL - 128)
                sp.dma_start(xb[:, b, :], disp[bass.ds(row, 128), :]).then_inc(x_loaded[b], 16)
            for b in range(2, NBLK):
                load(b, b % 2)
            for t in range(G * NT):
                n = ROWS[t % NT]
                r0 = (t // NT) * T + COL[t % NT]
                sp.wait_ge(added, 2 * t + 2)
                sp.dma_start(out[r0:r0 + n, :], hall[0:n, t, :]).then_inc(out_done, 16)
            sp.wait_ge(out_done, 16 * G * NT)
            sp.wait_ge(w_moe, N_MOE)


        @block.gpsimd
        def _(pool):
            p = nc.gpsimd
            p.memset(ident[:], 0.0)
            p.memset(onesf[:], 1.0)
            p.memset(headsel[:], 1.0)
            p.memset(expsel[:], 1.0)
            p.memset(cmask[:], 0.0)
            p.memset(zeros[:], 0.0)
            p.memset(onesb[:], 1.0)
            p.memset(before[:], 1.0)
            p.memset(valid[:], 1.0)
            p.iota(iota8[:], pattern=[[0, NT], [1, E]], base=0, channel_multiplier=0, allow_small_or_imprecise_dtypes=True)
            p.iota(run[:], pattern=[[RS, E]], base=0, channel_multiplier=0, allow_small_or_imprecise_dtypes=True)
            p.iota(base[:], pattern=[[RS, E]], base=0, channel_multiplier=0, allow_small_or_imprecise_dtypes=True)
            p.iota(blkno[:], pattern=[[1, NBLK], [0, E]], base=0, channel_multiplier=0, allow_small_or_imprecise_dtypes=True)
            p.iota(idle[:], pattern=[[128, NBLK]], base=DUMMY - 128 * LEAST, channel_multiplier=0, allow_small_or_imprecise_dtypes=True)
            p.iota(eno[:], pattern=[[0, NBLK], [1, E]], base=0, channel_multiplier=0, allow_small_or_imprecise_dtypes=True)
            p.memset(power[:], -0.5).then_inc(setup_pool, 1)
            pool.wait_ge(setup_pool, 1)
            p.affine_select(out=ident[:], in_=ident[:], compare_op=ALU.not_equal, fill=1.0, base=0,
                            pattern=[[-1, 128]], channel_multiplier=1)
            p.affine_select(out=before[:], in_=before[:], compare_op=ALU.is_gt, fill=0.0, base=0,
                            pattern=[[1, 128]], channel_multiplier=-1)
            p.affine_select(out=valid[:, 2, :], in_=valid[:, 2, :], compare_op=ALU.is_ge, fill=0.0, base=ROWS[2] - 1,
                            pattern=[[0, E]], channel_multiplier=-1)
            p.affine_select(out=headsel[:], in_=headsel[:], compare_op=ALU.is_ge, fill=0.0, base=0,
                            pattern=[[-HD, HEADS // DC]], channel_multiplier=1).then_inc(setup_pool, 1)
            pool.wait_ge(setup_pool, 2)
            p.affine_select(out=headsel[:], in_=headsel[:], compare_op=ALU.is_ge, fill=0.0, base=HD - 1,
                            pattern=[[HD, HEADS // DC]], channel_multiplier=-1)
            ev = expsel[:].rearrange("p r c (h m) -> p r (c h) m", m=HD)
            p.affine_select(out=ev, in_=ev, compare_op=ALU.is_equal, fill=0.0, base=0,
                            pattern=[[-HEADS, 3], [-1, HEADS], [0, HD]], channel_multiplier=1)
            p.affine_select(out=cmask[:], in_=cmask[:], compare_op=ALU.is_ge, fill=NEG, base=0,
                            pattern=[[-1, PT]], channel_multiplier=1).then_inc(setup_pool, 1)
            pool.wait_ge(setup_pool, 3)
            cv = cmask[:].rearrange("p (n s) -> p n s", s=S)
            p.affine_select(out=cv, in_=cv, compare_op=ALU.is_ge, fill=NEG, base=S - 1,
                            pattern=[[S, 3], [0, S]], channel_multiplier=-1).then_inc(setup_pool, 1)

            def rstd(g, mv, ep, rs, n):
                need(pool, mv, g)
                inc(p.tensor_scalar(lnv[n][:], lnmv[n][:, :, 1], 1e-5, None, ALU.add), ep)
                need(pool, ep, g)
                inc(p.tensor_tensor(lnr[n][:], lnv[n][:], power[0:PT, :], ALU.pow), rs)


            def a_ln(g):
                rstd(g, "mv1", "eps1", "rstd1", 0)
                if isinstance(g, int) and g == 0:
                    pool.wait_ge(w_attn, N_ATTN)
                need(pool, "xn1", g)
                inc(p.tensor_tensor(hA[:], hA[:], ob3[:].unsqueeze(1).to_broadcast([PT, NT, D]), ALU.add), "hb")


            def b_ln2(g):
                rstd(g, "mv2", "eps2", "rstd2", 1)

            def b_q(g):
                need(pool, "qs1", g)
                need(pool, "scb_ps", g - 1)
                for i in range(NT):
                    ins = p.tensor_scalar(diag[:, i, :], ident[0:PT, 0:PT], deqs[:, i:i + 1], None, ALU.mult)
                inc(ins, "diag1")

            def b_amax(g):
                need(pool, "qs2", g, 4)
                need(pool, "deq_ps", g)
                for i in range(NT):
                    ins = p.tensor_scalar(diag[:, i, :], ident[0:PT, 0:PT], qsc2[:, i:i + 1], None, ALU.mult)
                inc(ins, "diag2")

            def c_ln3(g):
                rstd(g, "mv3", "eps3", "rstd3", 2)

            def c_ln4(g):
                rstd(g, "mv4", "eps4", "rstd4", 2)

            def c_slot(g):
                need(pool, "rt", g)
                for k in range(2):
                    for i in range(NT):
                        n = ROWS[i]
                        p.indirect_dma_start(out=disp, out_offset=bass.IndirectOffsetOnAxis(ap=slotu[0:n, k, i:i + 1], axis=0),
                                             in_=xs[0:n, i, :], in_offset=None).then_inc(dispatched, 16)

            in_order(a_ln, b_ln2, b_q, b_amax, c_ln3, c_ln4, c_slot)
            pool.wait_ge(dispatched, 16 * 2 * NT * G)

            def store(b, j):
                need(pool, "ys", b)
                p.dma_start(ydisp[bass.ts(b, 128), :], yb[:, j, :]).then_inc(y_stored[j], 16)

            pool.wait_ge(plan, PLAN)
            for b in range(NBLK):
                store(b, b % 2)
            for j in range(2):
                pool.wait_ge(y_stored[j], 16 * (NBLK // 2))
            pool.wait_ge(plan, PLAN + 3)
            for t in range(G * NT):
                for k in range(2):
                    n = ROWS[t % NT]
                    o = k * NT + t % NT
                    p.indirect_dma_start(out=back[0:n, t, k, :], out_offset=None, in_=ydisp,
                                         in_offset=bass.IndirectOffsetOnAxis(ap=slots[0:n, t // NT, o:o + 1], axis=0))\
                        .then_inc(gathered[t], 16)

        @block.tensor
        def _(pe):
            mm, tr = nc.tensor.matmul, nc.tensor.transpose
            pe.wait_ge(setup_pool, 4)
            pe.wait_ge(w_attn, N_ATTN)
            for j, w in enumerate((qkw, qkw, pvw)):
                for c in range(DC):
                    for m in range(DC):
                        ins = mm(psA[:, j, c * D:(c + 1) * D], w[:, m, c * 128:(c + 1) * 128],
                                 inwT[:, m, j * D:(j + 1) * D], start=(m == 0), stop=(m == DC - 1))
            for o in range(3 * DC):
                b = qkb if o < 2 * DC else pvb
                for m in range(DC):
                    ins = mm(psA[:, 3, o:o + 1], inwT[:, m, o * 128:(o + 1) * 128], b[:, m:m + 1],
                             start=(m == 0), stop=(m == DC - 1))
            ins.then_inc(setup_pe, 1)
            pe.wait_ge(setup_dve, 2)
            mm(psB[:, 0, 0:2], onesf[:], wsum[:], start=True, stop=True).then_inc(setup_pe, 1)
            pe.wait_ge(w_l1, N_L1)
            for c in range(DC):
                for o in range(DC):
                    ins = mm(psB[:, 1, c * D:(c + 1) * D], aq[:, o, c * 128:(c + 1) * 128], ak[:, o, :],
                             start=(o == 0), stop=(o == DC - 1))
            ins.then_inc(setup_pe, 1)
            pe.wait_ge(w_tok, N_TOK)
            pe.wait_ge(setup_act, 2)
            pe.wait_ge(setup_dve, 5)

            def to_columns(src, ps, tile_signal, g, done, bank=0):
                for i in range(NT):
                    need(pe, tile_signal, g, i + 1)
                    for c in range(DC):
                        ins = tr(ps[:, bank + c, COL[i]:COL[i] + ROWS[i]], src[0:ROWS[i], i, c * 128:(c + 1) * 128],
                                 ident[0:ROWS[i], 0:ROWS[i]])
                inc(ins, done)

            def row_slot(ps, i, b):
                return ps[0:ROWS[i], b + i // 2, (i % 2) * D:(i % 2) * D + D]


            def a_tok(g):
                pe.wait_ge(pat_loaded, g * 16 + 16)
                for i in range(NT):
                    for c in range(FC):
                        ins = mm(row_slot(psA, i, 2), pat[:, c, COL[i]:COL[i] + ROWS[i]], tokw[:, c, :],
                                 start=(c == 0), stop=(c == FC - 1))
                    inc(ins, "tok_mm")

            def a_cols(g):
                need(pe, "h1", g - 1)
                to_columns(xnA, psA, "xn1", g, "xT1_ps")

            def a_proj(g):
                need(pe, "xT1", g)
                for o, bank in enumerate((2, 3, 0, 1, 2, 3)):
                    if o >= 4:
                        need(pe, "proj_sb", g, o - 3)
                    for c in range(DC):
                        ins = mm(psA[:, bank, 0:TP], fusw[:, c, o * 128:(o + 1) * 128], xT40[:, c, :],
                                 start=(c == 0), stop=(c == DC - 1))
                    inc(ins, "proj_mm")

            def a_prod(g):
                for r in range(3):
                    need(pe, "prods", g, r + 1)
                    for t, off in enumerate((0, 128, TP - 128)):
                        for c in range(DC):
                            o = t * 24 + r * 8 + c * 4
                            ins = mm(psA[:, 0, o:o + 4], prod[:, r, c, off:off + 128], headsel[:], start=True, stop=True)
                inc(ins, "sc_mm")

            def a_soft(g):
                need(pe, "smx", g)
                for t in range(3):
                    ins = tr(psA[0:24, 1, t * 128:(t + 1) * 128],
                             prb[:, t].rearrange("p r h -> p (r h)"), ident[:])
                inc(ins, "prT_ps")

            def a_pv(g):
                need(pe, "prTs", g)
                need(pe, "proj_sb", g)
                for r in range(3):
                    if r == 2:
                        need(pe, "pv", g, 1)
                    for c in range(DC):
                        ins = mm(psA[:, (2, 0, 2)[r] + c, 0:TP], expsel[:, r, c, :], prT[:], start=True, stop=True)
                    inc(ins, "ex_mm")

            def a_out(g):
                need(pe, "pv", g)
                for i in range(NT):
                    for c in range(DC):
                        ins = mm(row_slot(psA, i, 0), oTc[:, c, COL[i]:COL[i] + ROWS[i]], owT[:, c, :],
                                 start=(c == 0), stop=(c == DC - 1))
                    inc(ins, "op_mm")

            def spread(g, done, bank):
                for i in range(NT):
                    ins = mm(psB[:, bank, COL[i]:COL[i] + ROWS[i]], onesf[0:ROWS[i], :],
                             diag[0:ROWS[i], i, 0:ROWS[i]], start=True, stop=True)
                inc(ins, done)


            def b_q(g):
                need(pe, "h2", g - 1)
                to_columns(xq, psB, "xqs", g, "xTq_ps")
                need(pe, "diag1", g)
                need(pe, "xqTs", g)
                spread(g, "deq_ps", 0)

            def hidden(g, lo, hi):
                need(pe, "xqTs", g)
                for m in range(lo, hi):
                    if m == 1:
                        need(pe, "deqBs", g)
                    if m >= 2:
                        need(pe, "deq", g, m - 1)
                    for c in range(DC):
                        ins = mm(psB[:, (m + 1) % 2, 0:T], w1q[:, c, m * 128:(m + 1) * 128], xqT[:, c, :],
                                 start=(c == 0), stop=(c == DC - 1))
                    inc(ins, "f1_mm")

            def b_f1a(g):
                hidden(g, 0, 4)

            def b_f1b(g):
                hidden(g, 4, HC)

            def b_amax(g):
                need(pe, "vmaxs", g)
                for i in range(NT):
                    ins = tr(psB[0:ROWS[i], 0, i * 128:(i + 1) * 128], vmax[:, COL[i]:COL[i] + ROWS[i]], ident[:])
                inc(ins, "vT_ps")

            def b_spread(g):
                need(pe, "diag2", g)
                spread(g, "scb_ps", 1)

            def b_f2(g):
                need(pe, "vqs", g)
                for i in range(NT):
                    for m in range(HC):
                        ins = mm(row_slot(psB, i, 0), vq[:, m, COL[i]:COL[i] + ROWS[i]], w2q[:, m, :],
                                 start=(m == 0), stop=(m == HC - 1))
                    inc(ins, "f2_mm")

            def c_cols3(g):
                need(pe, "rt", g - 1)
                to_columns(xs, psB, "xn3", g, "xT3_ps", 2)

            def c_yv(g):
                need(pe, "xT3s", g)
                for o in range(DC):
                    for c in range(DC):
                        ins = mm(psB[:, 2 + o, 0:T], aqk[:, c, o * 128:(o + 1) * 128], xT3[:, c, :],
                                 start=(c == 0), stop=(c == DC - 1))
                inc(ins, "yT_ps")
                need(pe, "yTs", g)
                for i in range(NT):
                    for c in range(DC):
                        ins = mm(row_slot(psB, i, 2), xT3[:, c, COL[i]:COL[i] + ROWS[i]], avT[:, c, :],
                                 start=(c == 0), stop=(c == DC - 1))
                inc(ins, "vv_ps")

            def c_sc(g):
                need(pe, "v3s", g)
                for i in range(NT):
                    cols = slice(COL[i], COL[i] + ROWS[i])
                    for c in range(DC):
                        ins = mm(psB[0:ROWS[i], 2, i * PT:i * PT + ROWS[i]], yT3[:, c, cols], xT3[:, c, cols],
                                 start=(c == 0), stop=(c == DC - 1))
                inc(ins, "s3_mm")

            def c_pv(g):
                for i in range(NT):
                    need(pe, "p3", g, i + 1)
                    n = ROWS[i]
                    ins = tr(psB[0:n, 3, i * PT:i * PT + n], P3[0:n, i, 0:n], ident[0:n, 0:n])
                inc(ins, "pT3_ps")
                need(pe, "pT3s", g)
                for i in range(NT):
                    n = ROWS[i]
                    ins = mm(row_slot(psB, i, 2), PT3[0:n, i, 0:n], V3[0:n, i, :], start=True, stop=True)
                    inc(ins, "pv3_mm")

            def c_cols4(g):
                need(pe, "h3", g)
                to_columns(xs, psB, "xn4", g, "xT4_ps", 2)

            def c_rt(g):
                need(pe, "xT4s", g)
                for i in range(NT):
                    for c in range(DC):
                        ins = mm(psB[0:ROWS[i], 2, i * E:(i + 1) * E], xT3[:, c, COL[i]:COL[i] + ROWS[i]], wr[:, c, :],
                                 start=(c == 0), stop=(c == DC - 1))
                inc(ins, "lg_mm")

            def c_rank(g):
                need(pe, "rt", g, 5)
                need(pe, "lg", g)
                mm(psB[:, 3, 0:(NT + 1) * E], before[:], cntb[:].rearrange("p t e -> p (t e)"), start=True, stop=False)
                for i in range(NT):
                    ins = mm(psB[:, 3, (i + 1) * E:(NT + 1) * E].rearrange("p (t e) -> p t e", e=E), onesb[:],
                             cntb[:, i, :].unsqueeze(1).to_broadcast([PT, NT - i, E]), start=False, stop=(i == NT - 1))
                inc(ins, "rank_mm")

            in_order(a_tok, a_cols, a_proj, a_prod, a_soft, a_pv, a_out, b_q, b_f1a, b_f1b, b_amax, b_spread, b_f2,
                     c_cols3, c_yv, c_sc, c_pv, c_cols4, c_rt, c_rank)

            def turn_x(b, j):
                pe.wait_ge(x_loaded[j], (b - j) * 8 + 16)
                need(pe, "xTs", b - 2)
                for c in range(DC):
                    ins = tr(psA[:, j, c * 128:(c + 1) * 128], xb[:, j, c * 128:(c + 1) * 128], ident[:])
                inc(ins, "x_turned")

            def up(b, j):
                e = pe.value_load(bint[0:1, 0, bass.ds(b, 1)], min_val=0, max_val=E - 1)
                need(pe, "xTs", b)
                need(pe, "hraws", b - 2)
                for c in range(DC):
                    ins = mm(psB[:, j, :], xbT[:, j, c, :], mw1[:, bass.ds(e, 1), c, :], start=(c == 0), stop=(c == DC - 1))
                inc(ins, "h_mm")

            def turn_h(b, j):
                need(pe, "hraws", b)
                need(pe, "hTs", b - 2)
                for f in range(FFC):
                    ins = tr(psB[:, 2 + j, f * 128:(f + 1) * 128], hraw[:, j, f * 128:(f + 1) * 128], ident[:])
                inc(ins, "h_turned")

            def down(b, j):
                e = pe.value_load(bint[0:1, 0, bass.ds(b, 1)], min_val=0, max_val=E - 1)
                need(pe, "ys", b - 2)
                for f in range(FFC):
                    need(pe, "hTs", b, f + 1)
                    ins = mm(psA[:, 2 + j, 0:D], hTe[:, j, f, :], mw2[:, bass.ds(e, 1), f, :],
                             start=(f == 0), stop=(f == FFC - 1))
                inc(ins, "y_mm")

            need(pe, "rt", G - 1)
            need(pe, "h1", G - 1)
            pe.wait_ge(plan, PLAN)
            pe.wait_ge(w_moe, N_MOE)
            turn_x(0, 0)
            up(0, 0)
            turn_x(1, 1)
            for b in range(1, NBLK):
                up(b, b % 2)
                turn_h(b - 1, (b - 1) % 2)
                if b + 1 < NBLK:
                    turn_x(b + 1, (b + 1) % 2)
                down(b - 1, (b - 1) % 2)
            turn_h(NBLK - 1, (NBLK - 1) % 2)
            down(NBLK - 1, (NBLK - 1) % 2)

        @block.scalar
        def _(act):
            A = nc.scalar.activation
            act.wait_ge(setup_dve, 1)
            act.wait_ge(setup_pe, 1)
            for j in range(3):
                A(fusw[:, :, j * D:(j + 1) * D], psA[:, j, :].rearrange("p (c d) -> p c d", d=D), ACT.Copy)\
                    .then_inc(setup_act, 1) if j == 2 else \
                    A(fusw[:, :, j * D:(j + 1) * D], psA[:, j, :].rearrange("p (c d) -> p c d", d=D), ACT.Copy)
            act.wait_ge(setup_pe, 3)
            A(aqk[:], psB[:, 1, :].rearrange("p (c d) -> p c d", d=D), ACT.Copy).then_inc(setup_act, 1)
            act.wait_ge(setup_dve, 5)


            def a_cols(g):
                need(act, "xT1_ps", g)
                need(act, "proj_mm", g - 1)
                x4 = xT40[:].rearrange("p c (n s) -> p c n s", s=SP4)
                for c in range(DC):
                    src = psA[:, c, 0:T].rearrange("p (n s) -> p n s", s=S)
                    A(x4[:, c, :, 0:S], src, ACT.Copy)
                    ins = A(x4[:, c, :, S:SP4], src[:, :, 0:SP4 - S], ACT.Copy)
                inc(ins, "xT1")

            def a_proj(g):
                need(act, "prods", g - 1)
                need(act, "pv", g - 1)
                for o, bank in enumerate((2, 3, 0, 1, 2, 3)):
                    dst = (qT, qT, kT, kT, vT, vT)[o][:, o % 2, :]
                    need(act, "proj_mm", g, o + 1)
                    inc(A(dst, psA[:, bank, 0:TP], ACT.Identity, bias=fusb[:, o:o + 1], scale=QSCALE if o < 2 else 1.0), "proj_sb")

            def a_soft(g):
                need(act, "smx", g, 2)
                inc(A(sexp[:], sexp[:], ACT.Exp), "pexp")

            def a_pv(g):
                need(act, "prT_ps", g)
                need(act, "ex_mm", g - 1)
                A(prT[:, 0:256], psA[0:24, 1, 0:256], ACT.Copy)
                inc(A(prT[:, 256:TP], psA[0:24, 1, 256 + (384 - TP):384], ACT.Copy), "prTs")


            def b_ln2(g):
                need(act, "qs1", g, 4)
                need(act, "xTq_ps", g - 1)
                for i in range(NT):
                    n = ROWS[i]
                    inc(A(xq[0:n, i, :], xnB[0:n, i, :], ACT.Identity, bias=magic[0:n, :], scale=qsc[0:n, i:i + 1]), "xqs")

            def b_q(g):
                need(act, "deq_ps", g)
                need(act, "deq", g - 1)
                inc(A(deqB[:], psB[:, 0, 0:T], ACT.Copy), "deqBs")

            def convolved(g, lo, hi):
                for m in range(lo, hi):
                    if m < HC:
                        need(act, "deq", g, m + 1)
                        need(act, "silu", g, max(m - RING + 1, 0))
                        dst = yc[:, m % RING, :].rearrange("p (n s) -> p n s", s=S)
                        inc(A(dst, hpad[:, m % RING, :, 1:S + 1], ACT.Identity, bias=convb[:, m:m + 1],
                              scale=convw[:, m, 1:2]), "cact")
                    if m >= 3:
                        need(act, "cv2", g, m - 2)
                        if m == 3:
                            need(act, "vqs", g - 1)
                        inc(A(v[:, m - 3, :], yc[:, (m - 3) % RING, :], ACT.Silu), "silu")

            def b_f1a(g):
                convolved(g, 0, 4)

            def b_f1b(g):
                convolved(g, 4, HC + 3)

            def c_cols3(g):
                need(act, "xT3_ps", g)
                need(act, "lg_mm", g - 1)
                inc(A(xT3[:], psB[:, 2:4, 0:T], ACT.Copy), "xT3s")

            def c_yv(g):
                need(act, "yT_ps", g)
                inc(A(yT3[:], psB[:, 2:4, 0:T], ACT.Copy), "yTs")
                need(act, "vv_ps", g)
                A(V3[:, 0:2, :].rearrange("p i d -> p (i d)"), psB[0:PT, 2, :], ACT.Copy)
                inc(A(V3[0:ROWS[2], 2, :], psB[0:ROWS[2], 3, 0:D], ACT.Copy), "v3s")

            def c_sc(g):
                need(act, "s3", g)
                for i in range(NT):
                    n = ROWS[i]
                    inc(A(P3[0:n, i, 0:n], S3[0:n, i, 0:n], ACT.Exp, bias=nm3[0:n, i:i + 1], scale=ASCALE,
                          accum_out=rs3[0:n, i:i + 1]), "p3")

            def c_pv(g):
                need(act, "pT3_ps", g)
                n = ROWS[2]
                A(PT3[:, 0:2, :].rearrange("p i q -> p (i q)"), psB[0:PT, 3, 0:2 * PT], ACT.Copy)
                inc(A(PT3[0:n, 2, 0:n], psB[0:n, 3, 2 * PT:2 * PT + n], ACT.Copy), "pT3s")

            def c_cols4(g):
                need(act, "xT4_ps", g)
                inc(A(xT3[:], psB[:, 2:4, 0:T], ACT.Copy), "xT4s")

            def c_rank(g):
                need(act, "rt", g, 10)
                inc(A(ge[:], gd[:], ACT.Exp), "gexp")

            in_order(a_cols, a_proj, a_soft, a_pv, b_ln2, b_q, b_f1a, b_f1b, c_cols3, c_yv, c_sc, c_pv, c_cols4,
                     c_rank)
            need(act, "rank_mm", G - 1)

            def x_columns(b, j):
                need(act, "x_turned", b)
                need(act, "h_mm", b - 2)
                inc(A(xbT[:, j], psA[:, j, 0:D].rearrange("p (c t) -> p c t", t=128), ACT.Copy), "xTs")

            def h_rows(b, j):
                need(act, "h_mm", b)
                need(act, "h_turned", b - 2)
                inc(A(hraw[:, j, :], psB[:, j, :], ACT.Copy), "hraws")

            x_columns(0, 0)
            for b in range(NBLK):
                if b + 1 < NBLK:
                    x_columns(b + 1, (b + 1) % 2)
                h_rows(b, b % 2)

        @block.vector
        def _(dve):
            d = nc.vector
            for t in (hA, xnB, am2, mx3, rs3, lgt, xs, lnmv[0], lnmv[1], lnmv[2]):
                d.memset(t[:], 1.0)
            d.memset(hpad[:], 0.0)
            d.memset(cntb[:], 0.0)
            d.memset(magic[:], MAGIC).then_inc(setup_dve, 1)
            dve.wait_ge(w_ffn, N_FFN)
            d.tensor_reduce(wsum[:, 0:1], w1f[:].rearrange("p c f -> p (c f)"), AX, ALU.add, apply_absolute_value=True)
            d.tensor_reduce(wsum[:, 1:2], w2f[:].rearrange("p c f -> p (c f)"), AX, ALU.add,
                            apply_absolute_value=True).then_inc(setup_dve, 1)
            dve.wait_ge(setup_pe, 2)
            d.tensor_scalar(wmean[:], psB[:, 0, 0:2], 1.0 / (HID * D), 1e-5, ALU.mult, ALU.max).then_inc(setup_dve, 1)
            dve.wait_ge(setup_dve, 3)
            d.tensor_scalar(wdeq[:], wmean[:], 1.0 / 127.0, None, ALU.mult)
            d.reciprocal(wscale[:], wmean[:]).then_inc(setup_dve, 1)
            dve.wait_ge(setup_dve, 4)
            d.tensor_scalar(w1f[:], w1f[:], wscale[:, 0:1], MAGIC, ALU.mult, ALU.add)
            d.tensor_scalar(w2f[:], w2f[:], wscale[:, 1:2], MAGIC, ALU.mult, ALU.add)
            dve.wait_ge(w_tok, N_TOK)
            d.tensor_tensor(rowc[:], rowc[:], posr, ALU.add)
            d.tensor_tensor(fusb[:], psA[:, 3, 0:6], inb[:], ALU.add).then_inc(setup_dve, 1)
            dve.wait_ge(setup_dve, 5)
            d.tensor_scalar(fusb[:, 0:2], fusb[:, 0:2], QSCALE, None, ALU.mult)
            d.tensor_scalar(w1f[:], w1f[:], MAGIC - 1.0, MAGIC + 1.0, ALU.max, ALU.min)
            d.tensor_scalar(w2f[:], w2f[:], MAGIC - 1.0, MAGIC + 1.0, ALU.max, ALU.min).then_inc(setup_dve, 1)
            dve.wait_ge(setup_dve, 6)
            d.tensor_scalar(w1q[:], w1f[:], MAGIC, None, ALU.subtract)
            d.tensor_scalar(w2q[:], w2f[:], MAGIC, None, ALU.subtract).then_inc(setup_dve, 1)
            dve.wait_ge(w_l1, N_L1)

            def stats(g, x, ready, st, mv, n):
                for i in range(NT):
                    r = ROWS[i]
                    need(dve, ready, g, i + 1)
                    inc(d.bn_stats(lnst[n][0:r, i, :], x(i)), st)
                for i in range(NT):
                    need(dve, st, g, i + 1)
                    inc(d.bn_aggr(lnmv[n][0:ROWS[i], i, :], lnst[n][0:ROWS[i], i, :]), mv)

            def normalise(g, x, y, n, rs, done):
                need(dve, rs, g)
                for i in range(NT):
                    r = ROWS[i]
                    inc(d.tensor_scalar(y[0:r, i, :], x(i), lnmv[n][0:r, i, 0:1], lnr[n][0:r, i:i + 1],
                                        ALU.subtract, ALU.mult), done)

            def row_slot(ps, i, b):
                return ps[0:ROWS[i], b + i // 2, (i % 2) * D:(i % 2) * D + D]


            def a_ln(g):
                for i in range(NT):
                    r = ROWS[i]
                    need(dve, "tok_mm", g, BANKED[i])
                    inc(d.tensor_tensor(hA[0:r, i, :], row_slot(psA, i, 2), rowc[0:r, :], ALU.add), "h0")
                stats(g, lambda i: hA[0:ROWS[i], i, :], "h0", "st1", "mv1", 0)

            def a_norm(g):
                need(dve, "xT1_ps", g - 1)
                normalise(g, lambda i: hA[0:ROWS[i], i, :], xnA, 0, "rstd1", "xn1")

            q4, k4, v4 = (t[:].rearrange("p c (n s) -> p c n s", s=SEG) for t in (qT, kT, vT))

            def a_prod(g):
                need(dve, "proj_sb", g, 4)
                need(dve, "sc_mm", g - 1)
                for r in range(1, SEG):
                    o4 = prod[:, r - 1].rearrange("p c (n s) -> p c n s", s=SEG)
                    d.tensor_tensor(o4[:, :, :, 0:SEG - r], q4[:, :, :, 0:SEG - r], k4[:, :, :, r:SEG], ALU.mult)
                    inc(d.tensor_tensor(o4[:, :, :, SEG - r:SEG], q4[:, :, :, SEG - r:SEG], k4[:, :, :, 0:r], ALU.mult), "prods")

            def a_soft(g):
                need(dve, "sc_mm", g)
                sc = psA[:, 0, 0:72].rearrange("p (t r h) -> p t r h", r=3, h=HEADS)
                inc(d.tensor_reduce(smax[:], sc.rearrange("p t r h -> p t h r"), AX, ALU.max), "smx")
                need(dve, "smx", g, 1)
                inc(d.tensor_tensor(sexp[:], sc, smax[:].unsqueeze(2).to_broadcast([128, 3, 3, HEADS]), ALU.subtract), "smx")
                need(dve, "pexp", g)
                inc(d.tensor_reduce(ssum[:], sexp[:].rearrange("p t r h -> p t h r"), AX, ALU.add), "smx")
                need(dve, "smx", g, 3)
                inc(d.reciprocal(smax[:], ssum[:]), "smx")
                need(dve, "smx", g, 4)
                inc(d.tensor_tensor(prb[:], sexp[:], smax[:].unsqueeze(2).to_broadcast([128, 3, 3, HEADS]), ALU.mult), "smx")

            def a_pv(g):
                need(dve, "op_mm", g - 1)
                for r in range(1, SEG):
                    bank = (2, 0, 2)[r - 1]
                    dst = (oT, pv1, pv2)[r - 1][:].rearrange("p c (n s) -> p c n s", s=SEG)
                    w4 = psA[:, bank:bank + 2, 0:TP].rearrange("p c (n s) -> p c n s", s=SEG)
                    need(dve, "ex_mm", g, r)
                    if r == 1:
                        need(dve, "proj_sb", g)
                    d.tensor_tensor(dst[:, :, :, 0:SEG - r], w4[:, :, :, 0:SEG - r], v4[:, :, :, r:SEG], ALU.mult)
                    inc(d.tensor_tensor(dst[:, :, :, SEG - r:SEG], w4[:, :, :, SEG - r:SEG], v4[:, :, :, 0:r], ALU.mult), "pv")
                    if r > 1:
                        need(dve, "pv", g, 2 * r - 2)
                        if r == 2:
                            inc(d.tensor_tensor(oT[:], oT[:], pv1[:], ALU.add), "pv")
                        else:
                            a4, b4 = (t[:].rearrange("p c (n s) -> p c n s", s=SP4)[:, :, :, 0:S] for t in (oT, pv2))
                            inc(d.tensor_tensor(oTc[:].rearrange("p c (n s) -> p c n s", s=S), a4, b4, ALU.add), "pv")

            def a_out(g):
                need(dve, "hb", g)
                for i in range(NT):
                    r = ROWS[i]
                    need(dve, "op_mm", g, BANKED[i])
                    inc(d.tensor_tensor(hall[0:r, g * NT + i, :], row_slot(psA, i, 0), hA[0:r, i, :], ALU.add), "h1")

            def scales(g, amx, rec, qs, dq, w, name):
                need(dve, name, g, 1)
                inc(d.tensor_scalar(amx[:], amx[:], 1e-5, None, ALU.max), name)
                need(dve, name, g, 2)
                inc(d.reciprocal(rec[:], amx[:]), name)
                need(dve, name, g, 3)
                inc(d.tensor_scalar(qs[:], rec[:], 127.0, None, ALU.mult), name)
                inc(d.tensor_scalar(dq[:], amx[:], wdeq[0:PT, w:w + 1], None, ALU.mult), name)

            def row(g, i):
                return hall[0:ROWS[i], g * NT + i, :]

            def b_ln2(g):
                stats(g, lambda i: row(g, i), "h1", "st2", "mv2", 1)

            def b_norm2(g):
                need(dve, "xqs", g - 1)
                normalise(g, lambda i: row(g, i), xnB, 1, "rstd2", "xn2")
                need(dve, "xn2", g)
                inc(d.tensor_reduce(am[:], xnB[:], AX, ALU.max, apply_absolute_value=True), "qs1")
                scales(g, am, amr, qsc, deqs, 0, "qs1")

            def b_q(g):
                need(dve, "xTq_ps", g)
                need(dve, "f1_mm", g - 1)
                inc(d.tensor_scalar(xqT[:], psB[:, 0:2, 0:T], MAGIC, None, ALU.subtract), "xqTs")

            def convolved(g, lo, hi):
                for m in range(lo, hi):
                    if m < HC:
                        need(dve, "f1_mm", g, m + 1)
                        if m == 0:
                            need(dve, "deqBs", g)
                        need(dve, "cact", g, max(m - RING + 1, 0))
                        need(dve, "cv2", g, max(m - RING + 1, 0))
                        inc(d.tensor_tensor(hpad[:, m % RING, :, 1:S + 1],
                                            psB[:, (m + 1) % 2, 0:T].rearrange("p (n s) -> p n s", s=S),
                                            deqB[:].rearrange("p (n s) -> p n s", s=S), ALU.mult), "deq")
                    if 2 <= m < HC + 2:
                        j = m - 2
                        y = yc[:, j % RING, :].rearrange("p (n s) -> p n s", s=S)
                        need(dve, "cact", g, j + 1)
                        inc(d.scalar_tensor_tensor(y, hpad[:, j % RING, :, 0:S], convw[:, j, 0:1], y, ALU.mult, ALU.add), "cv1")
                    if m >= 3:
                        j = m - 3
                        y = yc[:, j % RING, :].rearrange("p (n s) -> p n s", s=S)
                        need(dve, "cv1", g, j + 1)
                        inc(d.scalar_tensor_tensor(y, hpad[:, j % RING, :, 2:S + 2], convw[:, j, 2:3], y, ALU.mult, ALU.add), "cv2")

            def b_f1a(g):
                convolved(g, 0, 4)

            def b_f1b(g):
                convolved(g, 4, HC + 3)

            def b_amax(g):
                need(dve, "silu", g)
                inc(d.tensor_reduce(vmax[:], v[:].rearrange("p m t -> p t m"), AX, ALU.max, apply_absolute_value=True), "vmaxs")
                need(dve, "vT_ps", g)
                d.tensor_reduce(am2[:, 0:2], psB[0:PT, 0, 0:256].rearrange("p (i k) -> p i k", k=128), AX, ALU.max)
                inc(d.tensor_reduce(am2[0:ROWS[2], 2:3], psB[0:ROWS[2], 0, 256:384], AX, ALU.max), "qs2")
                scales(g, am2, am2r, qsc2, deqs2, 1, "qs2")

            def b_spread(g):
                need(dve, "scb_ps", g)
                for k in range(2):
                    h = slice(k * HC // 2, (k + 1) * HC // 2)
                    inc(d.tensor_tensor(v[:, h, :], v[:, h, :],
                                        psB[:, 1, 0:T].unsqueeze(1).to_broadcast([128, HC // 2, T]), ALU.mult), "vsc")
                need(dve, "f2_mm", g - 1)
                for k in range(2):
                    need(dve, "vsc", g, k + 1)
                    h = slice(k * HC // 2, (k + 1) * HC // 2)
                    inc(d.tensor_scalar(vq[:, h, :], v[:, h, :], MAGIC, -MAGIC, ALU.add, ALU.add), "vqs")

            def b_f2(g):
                for i in range(NT):
                    need(dve, "f2_mm", g, BANKED[i])
                    inc(d.scalar_tensor_tensor(row(g, i), row_slot(psB, i, 0), deqs2[0:ROWS[i], i:i + 1], row(g, i),
                                               ALU.mult, ALU.add), "h2")

            def c_st3(g):
                stats(g, lambda i: row(g, i), "h2", "st3", "mv3", 2)

            def c_ln3(g):
                if g:
                    dve.wait_ge(dispatched, 16 * 2 * NT * g)
                normalise(g, lambda i: row(g, i), xs, 2, "rstd3", "xn3")

            def c_sc(g):
                need(dve, "s3_mm", g)
                need(dve, "p3", g - 1)
                n = ROWS[2]
                s3v = psB[0:PT, 2, 0:2 * PT].rearrange("p (i q) -> p i q", q=PT)
                inc(d.tensor_tensor(S3[:, 0:2, :], s3v, cmask[:].unsqueeze(1).to_broadcast([PT, 2, PT]), ALU.add), "s3")
                inc(d.tensor_tensor(S3[0:n, 2, 0:n], psB[0:n, 2, 2 * PT:2 * PT + n], cmask[0:n, 0:n], ALU.add), "s3")
                need(dve, "s3", g, 1)
                inc(d.tensor_reduce(mx3[:, 0:2], S3[:, 0:2, :], AX, ALU.max), "s3")
                need(dve, "s3", g, 2)
                inc(d.tensor_reduce(mx3[0:n, 2:3], S3[0:n, 2, 0:n], AX, ALU.max), "s3")
                need(dve, "s3", g, 4)
                inc(d.tensor_scalar(nm3[:], mx3[:], -ASCALE, None, ALU.mult), "s3")

            def c_pv(g):
                need(dve, "p3", g)
                inc(d.reciprocal(rr3[:], rs3[:]), "rr")
                need(dve, "rr", g)
                for i in range(NT):
                    need(dve, "pv3_mm", g, BANKED[i])
                    inc(d.scalar_tensor_tensor(row(g, i), row_slot(psB, i, 2), rr3[0:ROWS[i], i:i + 1], row(g, i),
                                               ALU.mult, ALU.add), "h3")
                stats(g, lambda i: row(g, i), "h3", "st4", "mv4", 2)

            def c_ln4(g):
                normalise(g, lambda i: row(g, i), xs, 2, "rstd4", "xn4")

            def c_rt(g):
                need(dve, "lg_mm", g)
                n = ROWS[2]
                d.tensor_tensor(lgt[:, 0:2, :], psB[0:PT, 2, 0:2 * E].rearrange("p (i e) -> p i e", e=E),
                                brb[0:PT], ALU.add)
                inc(d.tensor_tensor(lgt[0:n, 2, :], psB[0:n, 2, 2 * E:3 * E], brb[0:n, 0, :], ALU.add), "lg")
                need(dve, "lg", g)
                for i in range(NT):
                    ins = d.max(top[:, i, :], lgt[:, i, :])
                inc(ins, "rt")
                need(dve, "rt", g, 1)
                for i in range(NT):
                    ins = d.max_index(topi[:, i, :], top[:, i, :], lgt[:, i, :])
                inc(ins, "rt")
                need(dve, "rt", g, 2)
                inc(d.tensor_copy(topf[:], topi[:, :, 0:2]), "rt")
                need(dve, "rt", g, 3)
                for k in range(2):
                    ins = d.tensor_tensor(hot[:, k], iota8[:], topf[:, :, k:k + 1].to_broadcast([PT, NT, E]), ALU.is_equal)
                inc(ins, "rt")
                need(dve, "rt", g, 4)
                d.tensor_tensor(cnt[:], hot[:, 0], hot[:, 1], ALU.add).then_inc(route_cnt, 1)
                dve.wait_ge(route_cnt, g + 1)
                inc(d.tensor_tensor(cntb[:, 0:NT, :], cnt[:], valid[:], ALU.mult), "rt")

            def c_rank(g):
                need(dve, "rank_mm", g)
                inc(d.tensor_tensor(slot[:], psB[0:PT, 3, 0:NT * E].rearrange("p (t e) -> p t e", e=E),
                                    run[0:PT].unsqueeze(1).to_broadcast([PT, NT, E]), ALU.add), "rt")
                need(dve, "rt", g, 6)
                inc(d.tensor_tensor(run[:], psB[:, 3, NT * E:(NT + 1) * E], run[:], ALU.add), "rt")
                for k in range(2):
                    ins = d.tensor_tensor(hslot[:, k], hot[:, k], slot[:], ALU.mult)
                inc(ins, "rt")
                need(dve, "rt", g, 8)
                inc(d.tensor_reduce(slotf[:], hslot[:], AX, ALU.add), "rt")
                inc(d.tensor_tensor(gd[:], top[:, :, 1], top[:, :, 0], ALU.subtract), "rt")
                need(dve, "rt", g, 9)
                inc(d.tensor_copy(slotu[:], slotf[:]), "rt")
                d.tensor_copy(hots[:, g], hot[:].rearrange("p k t e -> p (k t) e"))
                inc(d.tensor_copy(slotfs[:, g, :], slotf[:].rearrange("p k t -> p (k t)")), "rt")
                need(dve, "gexp", g)
                inc(d.tensor_scalar(gs[:], ge[:], 1.0, None, ALU.add), "rt")
                need(dve, "rt", g, 13)
                gt = gates[:, bass.ts(g, NT), :]
                inc(d.reciprocal(gd[:], gs[:]), "rt")
                need(dve, "rt", g, 14)
                inc(d.tensor_copy(gt[:, :, 0], gd[:]), "rt")
                inc(d.tensor_tensor(gt[:, :, 1], gd[:], ge[:], ALU.mult), "rt")

            in_order(a_ln, a_norm, a_prod, a_soft, a_pv, a_out, b_ln2, b_norm2, b_q, b_f1a, b_f1b, b_amax, b_spread,
                     b_f2, c_st3, c_ln3, c_sc, c_pv, c_ln4, c_rt, c_rank)

            steps = [0]

            def step(ins):
                ins.then_inc(plan, 1)
                steps[0] += 1
                dve.wait_ge(plan, steps[0])

            used, whole, end, start, off, shift = (nblk[:, n, :] for n in range(6))
            need(dve, "rt", G - 1)
            d.tensor_copy(padint[:], run[0:1, :])
            step(d.tensor_tensor(used, run[:], base[:], ALU.subtract))
            step(d.tensor_scalar(whole, used, 1.0 / 128, 127.0 / 256, ALU.mult, ALU.add))
            step(d.tensor_scalar(whole, whole, MAGIC, -MAGIC, ALU.add, ALU.add))
            step(d.tensor_tensor_scan(end, onesf[:, 0:E], whole, 0.0, ALU.mult, ALU.add))
            step(d.tensor_tensor(start, end, whole, ALU.subtract))
            d.tensor_tensor(bw[0:1, 0], blkno[:], nblk[0:1, 3, :].unsqueeze(1).to_broadcast([1, NBLK, E]), ALU.is_ge)
            d.tensor_tensor(bw[0:1, 1], blkno[:], nblk[0:1, 2, :].unsqueeze(1).to_broadcast([1, NBLK, E]), ALU.is_ge)
            step(d.scalar_tensor_tensor(shift, start, 128.0, base[:], ALU.mult, ALU.subtract))
            d.tensor_tensor(bw[0:1, 2], bw[0:1, 0], bw[0:1, 1], ALU.subtract)
            step(d.tensor_scalar(off, shift, -1.0, float(128 * LEAST - DUMMY), ALU.mult, ALU.add))
            d.tensor_tensor(bw[0:1, 0], bw[0:1, 2], eno[:], ALU.mult)
            step(d.tensor_tensor(bw[0:1, 1], bw[0:1, 2], nblk[0:1, 4, :].unsqueeze(1).to_broadcast([1, NBLK, E]), ALU.mult))
            step(d.tensor_reduce(bres[:], bw[0:1, 0:2], AX, ALU.add))
            d.tensor_copy(bint[0:1, 0], bres[0:1, 0])
            step(d.tensor_tensor(bint[0:1, 1], bres[0:1, 1], idle[:], ALU.add))
            assert steps[0] == PLAN
            hv = hots[:].rearrange("p g j e -> p (g j) e")
            step(d.tensor_tensor(hv, hv, nblk[0:PT, 5, :].unsqueeze(1).to_broadcast([PT, G * 2 * NT, E]), ALU.mult))
            step(d.tensor_reduce(hcor[:], hv, AX, ALU.add))
            step(d.tensor_tensor(slots[:].rearrange("p g j -> p (g j)"), slotfs[:].rearrange("p g j -> p (g j)"), hcor[:], ALU.add))

            def h_columns(b, j):
                e = dve.value_load(bint[0:1, 0, bass.ds(b, 1)], min_val=0, max_val=E - 1)
                need(dve, "h_turned", b)
                need(dve, "y_mm", b - 2)
                for f in range(FFC):
                    inc(d.tensor_scalar(hTe[:, j, f, :], psB[:, 2 + j, f * 128:(f + 1) * 128],
                                        mb1[:, bass.ds(e, 1), f], 0.0, ALU.add, ALU.max), "hTs")
                return e

            def y_rows(b, j, e):
                need(dve, "y_mm", b)
                if not isinstance(b, int) or b >= 2:
                    dve.wait_ge(y_stored[j], (b - j) * 8)
                inc(d.tensor_tensor(yb[:, j, :], psA[:, 2 + j, 0:D], mb2[:, bass.ds(e, 1), :], ALU.add), "ys")

            dve.wait_ge(w_moe, N_MOE)
            for b in range(NBLK):
                y_rows(b, b % 2, h_columns(b, b % 2))
            for t in range(G * NT):
                n = ROWS[t % NT]
                for k in range(2):
                    if k == 0:
                        dve.wait_ge(gathered[t], 32)
                    if k:
                        dve.wait_ge(added, 2 * t + 1)
                    d.scalar_tensor_tensor(hall[0:n, t, :], back[0:n, t, k, :], gates[0:n, t, k:k + 1], hall[0:n, t, :],
                                           ALU.mult, ALU.add).then_inc(added, 1)


def lay_out(i):
    import numpy as np
    f = np.ascontiguousarray

    def cols(w):
        w = np.asarray(w)
        return f(w.reshape(w.shape[0] // 128, 128, -1).transpose(1, 0, 2))

    def vec(b):
        return f(np.asarray(b).reshape(-1, 128).T)

    x = np.asarray(i["x"])
    n = IMG // PATCH
    pt = x.reshape(B, C, n, PATCH, n, PATCH).transpose(1, 3, 5, 0, 2, 4).reshape(C * PATCH * PATCH, B, n * n)
    pat = np.zeros((C * PATCH * PATCH, B, S), x.dtype)
    pat[:, :, 1:] = pt
    pat = f(pat.reshape(FC, 128, G, T).transpose(1, 2, 0, 3))
    row = np.concatenate([np.asarray(i["L0_tok_cls_token"])[0], np.tile(np.asarray(i["L0_tok_b"])[None], (S - 1, 1))])
    w1, w2 = np.asarray(i["L1_ffn_W1"]), np.asarray(i["L1_ffn_W2"])
    o = {
        "pat": pat, "tokw": cols(np.asarray(i["L0_tok_W"]).T),
        "rowc": f(np.tile(row, (3, 1))), "posr": f(np.tile(np.asarray(i["L0_tok_pos_enc"])[0], (3, 1))),
        "qkw": cols(i["L0_attn_proj_qk_w"]), "pvw": cols(i["L0_attn_proj_v_w"]),
        "inwT": cols(np.asarray(i["L0_attn_in_proj_w"]).T), "qkb": vec(i["L0_attn_proj_qk_b"]),
        "pvb": vec(i["L0_attn_proj_v_b"]), "inb": vec(i["L0_attn_in_proj_b"]),
        "owT": cols(np.asarray(i["L0_attn_out_proj_w"]).T),
        "ob3": f(np.tile(np.asarray(i["L0_attn_out_proj_b"])[None], (PT, 1))),
        "w1f": cols(np.asarray(i["L0_ffn_w1"]).T), "w2f": cols(np.asarray(i["L0_ffn_w2"]).T),
        "convw": cols(np.asarray(i["L0_ffn_conv_w"]).reshape(HID, 3)), "convb": vec(i["L0_ffn_conv_b"]),
        "aq": cols(i["L1_attn_Wq"]), "ak": cols(i["L1_attn_Wk"]), "avT": cols(np.asarray(i["L1_attn_Wv"]).T),
        "wr": cols(i["L1_ffn_Wr"]), "brb": f(np.tile(np.asarray(i["L1_ffn_br"])[None, None], (128, 2, 1))),
        "mw1": f(w1.reshape(E, DC, 128, FF).transpose(2, 0, 1, 3)),
        "mw2": f(w2.reshape(E, FFC, 128, D).transpose(2, 0, 1, 3)),
        "mb1": f(np.asarray(i["L1_ffn_b1"]).reshape(E, FFC, 128).transpose(2, 0, 1)),
        "mb2": f(np.tile(np.asarray(i["L1_ffn_b2"])[None], (128, 1, 1))),
    }
    return o


def kernel(**inputs):
    import concourse.bacc as bacc
    from concourse.bass_utils import run_bass_kernel_spmd

    nc = bacc.Bacc("TRN2", target_bir_lowering=False, num_devices=1)
    arrays = {f"in_{k}": v for k, v in lay_out(inputs).items()}
    aps = {k[3:]: nc.dram_tensor(k, v.shape, mybir.dt.from_np(v.dtype), kind="ExternalInput").ap()
           for k, v in arrays.items()}
    out = nc.dram_tensor("out_rows", (B * S, D), F32, kind="ExternalOutput").ap()
    vit_tower(nc, aps, out)
    r = run_bass_kernel_spmd(nc, [arrays], core_ids=[0])
    return r.results[0]["out_rows"].reshape(B, S, D)
```

```python
from contextlib import ExitStack

import concourse.bass as bass
from concourse import mybir

F32 = mybir.dt.float32
BF16 = mybir.dt.bfloat16
U32 = mybir.dt.uint32
I32 = mybir.dt.int32
ALU = mybir.AluOpType
ACT = mybir.ActivationFunctionType
AX = mybir.AxisListType.X

B, C, IMG, PATCH, D = 32, 3, 96, 16, 256
S = (IMG // PATCH) ** 2 + 1
SEG, HEADS = 4, 8
HD = D // HEADS
SP4 = (S // SEG + 1) * SEG
GI = 8
G = B // GI
T = GI * S
TP = GI * SP4
TILES = [(0, 3), (3, 3), (6, 2)]
NT = len(TILES)
PT = 3 * S
DC = D // 128
FC = C * PATCH * PATCH // 128
HID, HC = 1024, 1024 // 128
E, FF = 8, 512
FFC = FF // 128
ROWS = [n * S for _, n in TILES]
COL = [a * S for a, _ in TILES]
RING = 5
BANKED = (2, 2, 3)
NBLK = (2 * B * S + E * 127) // 128
RS = -(-B * S // 128) * 128 + 128
XBUF = 4
LEAST = -(-2 * B * S // 128)
DUMMY = E * RS
ROWS_ALL = DUMMY + (NBLK - LEAST) * 128
MAGIC = 1.5 * 2.0 ** 23
QSCALE = float(HD) ** -0.5
ASCALE = float(D) ** -0.5
NEG = -1.0e30
WARM = 9
PAD = T + 128
DW = D + 4
ROWS_Y = 2 * B * S


ORDER = ("b_spread:2 b_round:2 c_cols4:3 c_rt:3 a_pv:1 c_rank:3 a_pv2:1 b_f2:2 b_f2b:2 s_l1:1 a_out:1 "
         "c_slot:3 a_tok:0 c_slot2:3 a_tok2:0 s_bias:0 b_ln2:1 c_st3:2 b_norm2:1 c_ln3:2 s_fuse:0 b_q:1 "
         "a_ln:0 c_cols3:2 b_f1a:1 a_norm:0 c_yv:2 a_cols:0 s_tern:0 b_f1b:1 c_v:2 b_f1c:1 a_proj:0 "
         "b_f1d:1 c_sc:2 a_proj2:0 a_prod:0 b_amax:1 c_pv:2 a_soft:0 c_ln4:2 ").split()
STEPS = [(step[:-2], int(step[-1])) for step in ORDER]


class Signal:

    def __init__(self, sem, per):
        self.sem, self.per = sem, per

    def at(self, g, k):
        return g * self.per + (1 + k)


def vit_tower(nc, a, out):
    ctx = ExitStack()
    with ctx:
        def sb(name, shape, dt=F32):
            return ctx.enter_context(nc.sbuf_tensor(name, shape, dt))

        def pb(name, shape, dt=F32):
            return ctx.enter_context(nc.psum_tensor(name, shape, dt))

        def sem(name):
            return ctx.enter_context(nc.semaphore(name))

        mw1 = sb("mw1", [128, E, DC, FF])
        early = mw1[:].rearrange("p e c f -> p (e c f)")
        at = 0

        def view(shape):
            nonlocal at
            n = shape[0] * shape[1]
            at += n
            return early[:, at - n:at].rearrange("p (a b) -> p a b", b=shape[1])

        w1f, w2f = view([DC, HID]), view([HC, D])
        qkw, pvw, inwT = view([DC, D]), view([DC, D]), view([DC, 3 * D])
        aq, ak = view([DC, D]), view([DC, D])
        tokw = sb("tokw", [128, FC, D])
        rowc = sb("rowc", [PT, D])
        posr = early[0:PT, at:at + D]
        qkb = sb("qkb", [128, DC])
        pvb = sb("pvb", [128, DC])
        inb = sb("inb", [128, 3 * DC])
        fusw = sb("fusw", [128, DC, 3 * D])
        fusb = sb("fusb", [128, 3 * DC])
        owT = sb("owT", [128, DC, D])
        ob3 = sb("ob3", [PT, D])
        headsel = sb("headsel", [128, HEADS // DC])
        expsel = sb("expsel", [3 * 24, 3, DC, 128], BF16)
        w1q = sb("w1q", [128, DC, HID], BF16)
        w2q = sb("w2q", [128, HC, D], BF16)
        wsum = sb("wsum", [128, 2])
        wmean = sb("wmean", [128, 2])
        wscale = sb("wscale", [128, 2])
        wdeq = sb("wdeq", [128, 2])
        convw = sb("convw", [128, HC, 3])
        convb = sb("convb", [128, HC])
        avT = sb("avT", [128, DC, D])
        aqk = sb("aqk", [128, DC, D])
        wr = sb("wr", [128, DC, E])
        brb = sb("brb", [128, 2, E])
        mw2 = sb("mw2", [128, E, FFC, D])
        mb1 = sb("mb1", [128, E, FFC])
        ident = sb("ident", [128, 128])
        identb = sb("identb", [128, 128], BF16)
        onesf = sb("onesf", [128, 128])
        cmask = sb("cmask", [PT, PT])
        magic = sb("magic", [128, 1])
        power = sb("power", [128, NT])
        front = sb("front", [128, FC * T + 3 * DC * TP])
        pat = front[:, 0:FC * T].rearrange("p (c t) -> p c t", t=T)
        prod = front[:, FC * T:].rearrange("p (r c t) -> p r c t", c=DC, t=TP)
        mb2 = front[:, 0:E * D].rearrange("p (e d) -> p e d", d=D)
        hA = sb("hA", [PT, NT, D])
        xnA = sb("xnA", [PT, NT, D])
        xT40 = sb("xT40", [128, DC, TP])
        qT = sb("qT", [128, DC, TP])
        kT = sb("kT", [128, DC, TP])
        vT = sb("vT", [128, DC, TP])
        smax = sb("smax", [128, 3, HEADS])
        ssum = sb("ssum", [128, 3, HEADS])
        sexp = sb("sexp", [128, 3, 3, HEADS])
        prb = sb("prb", [128, 3, 3, HEADS])
        prs = sb("prs", [128, 3, 3, 24], BF16)
        prT = sb("prT", [3 * 24, TP], BF16)
        pv1, pv2 = qT, kT
        oT = sb("oT", [128, DC, TP])
        oTc = sb("oTc", [128, DC, T])
        hall = sb("hall", [PT, G * NT, D])
        xnB = sb("xnB", [PT, NT, D])
        xq = sb("xq", [PT, NT, D])
        am = sb("am", [PT, NT])
        amr = sb("amr", [PT, NT])
        qsc = sb("qsc", [PT, NT])
        deqs = sb("deqs", [PT, NT])
        am2 = sb("am2", [PT, NT])
        am2r = sb("am2r", [PT, NT])
        qsc2 = sb("qsc2", [PT, NT])
        deqs2 = sb("deqs2", [PT, NT])
        diag = sb("diag", [PT, NT, PT])
        xqT = sb("xqT", [128, DC, T], BF16)
        deqB = sb("deqB", [128, T])
        hpad = sb("hpad", [128, RING, GI, S + 2])
        yc = sb("yc", [128, RING, T])
        v = sb("v", [128, HC, T])
        vmax = sb("vmax", [128, T])
        vq = sb("vq", [128, HC, T], BF16)
        xT3 = sb("xT3", [128, DC, T])
        yT3 = sb("yT3", [128, DC, T])
        V3 = sb("V3", [PT, NT, D])
        P3 = sb("P3", [PT, NT, PT])
        PT3 = sb("PT3", [PT, NT, PT])
        mx3 = sb("mx3", [PT, NT])
        nm3 = sb("nm3", [PT, NT])
        rs3 = sb("rs3", [PT, NT])
        rr3 = sb("rr3", [PT, NT])
        xs = sb("xs", [PT, NT, DW])
        tid = sb("tid", [PT, NT])
        lgt = sb("lgt", [PT, NT, E])
        top = sb("top", [PT, NT, 8])
        topi = sb("topi", [PT, NT, 8], U32)
        topf = sb("topf", [PT, NT, 2])
        hot = sb("hot", [PT, 2, NT, E])
        cnt = sb("cnt", [PT, NT, E])
        cntb = sb("cntb", [PT, NT + 1, E], BF16)
        valid = sb("valid", [PT, NT, E])
        iota8 = sb("iota8", [PT, NT, E])
        before = sb("before", [PT, 128], BF16)
        onesb = sb("onesb", [PT, 128], BF16)
        run = sb("run", [128, E])
        base = sb("base", [128, E])
        slot = sb("slot", [PT, NT, E])
        hslot = sb("hslot", [PT, 2, NT, E])
        slotf = sb("slotf", [PT, 2, NT])
        slotu = sb("slotu", [PT, 2, NT], U32)
        gd = sb("gd", [PT, NT])
        ge = sb("ge", [PT, NT])
        gs = sb("gs", [PT, NT])
        gates = sb("gates", [PT, G * NT, 2])
        padrow = sb("padrow", [128, DW])
        nblk = sb("nblk", [128, 5, E])
        idle = sb("idle", [128, NBLK])
        blkno = sb("blkno", [128, NBLK, E])
        eno = sb("eno", [128, NBLK, E])
        bw = yc[:].rearrange("p j t -> p (j t)")[:, 0:3 * NBLK * E].rearrange("p (j b e) -> p j b e", b=NBLK, e=E)
        bres = sb("bres", [128, 2, NBLK])
        second = sb("second", [128, XBUF])
        yrow = sb("yrow", [128, XBUF], U32)
        bint = sb("bint", [1, 2, NBLK], I32)
        padint = sb("padint", [1, E], I32)
        vflat = v[:].rearrange("p m t -> p (m t)")
        w1s = vflat[:, 0:2 * DC * FF].rearrange("p (j c f) -> p j c f", c=DC, f=FF)
        hTe = hpad[:].rearrange("p r n s -> p (r n s)")[:, 0:2 * FF].rearrange("p (j f t) -> p j f t", f=FFC, t=128)
        late = front[:, E * D:]
        xb = late[:, 0:XBUF * DW].rearrange("p (j d) -> p j d", d=DW)
        xbT = xT3[:].rearrange("p c t -> p (c t)")[:, 0:512].rearrange("p (j c t) -> p j c t", c=DC, t=128)
        yb = late[:, XBUF * DW:XBUF * DW + 2 * D].rearrange("p (j d) -> p j d", d=D)
        back = early[0:PT, 0:2 * G * NT * D].rearrange("p (t k d) -> p t k d", k=2, d=D)
        disp = nc.dram_tensor("dispatched", (ROWS_ALL, DW), F32, kind="Internal").ap()
        ydisp = nc.dram_tensor("expert_out", (ROWS_Y + 128, D), F32, kind="Internal").ap()
        lnst = [sb(f"lnst{n}", [PT, NT, 6]) for n in range(3)]
        lnmv = [sb(f"lnmv{n}", [PT, NT, 2]) for n in range(3)]
        lnv = [sb(f"lnv{n}", [PT, NT]) for n in range(3)]
        lnr = [sb(f"lnr{n}", [PT, NT]) for n in range(3)]
        psA = pb("psA", [128, 4, 512])
        psB = pb("psB", [128, 4, 512])

        per = dict(
            tok_mm=3, h0=3, st1=3, mv1=3, eps1=1, rstd1=1, xn1=3, hb=1, xT1_ps=1, xT1=1, proj_mm=6, proj_sb=6,
            prods=3, sc_mm=1, smx=9, pexp=1, prT_ps=1, prTs=1, ex_mm=3, pv=5, op_mm=3, h1=3,
            st2=3, mv2=3, eps2=1, rstd2=1, xn2=3, qs1=5, xqs=3, diag1=1, xTq_ps=1, deq_ps=1, xqTs=1, deqBs=1,
            f1_mm=8, deq=8, cact=8, cv1=8, cv2=8, silu=8, vmaxs=1, vT_ps=1, qs2=5, diag2=1, scb_ps=1,
            vsc=2, vqs=2, f2_mm=3, h2=3, st3=3, mv3=3, eps3=1, rstd3=1, xn3=3, xT3_ps=1, xT3s=1,
            yT_ps=1, vv_ps=1, yTs=1, v3s=1, s3_mm=1, s3=3, p3=3, rr=1, pT3_ps=1, pT3s=1, pv3_mm=3, h3=3,
            st4=3, mv4=3, eps4=1, rstd4=1, xn4=3, xT4_ps=1, xT4s=1, lg_mm=1, lg=1,
            rt=15, gexp=1, rank_mm=1)
        per_block = dict(x_turned=1, xTs=1, w1_in=1, h_mm=1, hTs=FFC, y_mm=1, ys=1, seconds=1, yrows=1)
        sg = {k: Signal(sem(k), n) for k, n in (per | per_block).items()}
        dispatched, pads, plan, added = (sem(n) for n in ("dispatched", "pads", "plan", "added"))
        x_loaded = [sem(f"x_loaded{n}") for n in range(XBUF)]
        y_stored = [sem(f"y_stored{n}") for n in range(2)]
        returned = [sem(f"returned{n}") for n in range(G)]
        pat_loaded = sem("pat_loaded")
        w_tok, w_attn, w_ffn, w_l1, w_late, w_moe = (sem(n) for n in ("w_tok", "w_attn", "w_ffn", "w_l1", "w_late", "w_moe"))
        constants, tables = sem("constants"), sem("tables")
        clipped, pad_starts, counting = sem("clipped"), sem("pad_starts"), sem("counting")
        gated, pool_added, bias_ps = sem("gated"), sem("pool_added"), sem("bias_ps")
        row_consts, fused_ps, fused, biases = (sem(n) for n in ("row_consts", "fused_ps", "fused", "biases"))
        abs_sums, abs_ps, ternary, qk_ps, qk_fused = (sem(n) for n in ("abs_sums", "abs_ps", "ternary", "qk_ps", "qk_fused"))
        out_done = sem("out_done")
        route_cnt = sem("route_cnt")

        prT_ps = psA[0:72, 1, 0:192].bitcast(BF16)

        block = ctx.enter_context(nc.Block())

        def in_order(*parts):
            mine = {f.__name__: f for f in parts}
            for period in range(G + max(lag for _, lag in STEPS)):
                for step, lag in STEPS:
                    g = period - lag
                    if step in mine and 0 <= g < (1 if step[0] == "s" else G):
                        mine[step](g)

        def inc(ins, name):
            ins.then_inc(sg[name].sem, 1)

        def need(eng, name, g, k=None):
            s = sg[name]
            value = s.at(g, s.per if k is None else k)
            if not isinstance(value, int) or value > 1:
                eng.wait_ge(s.sem, value)

        N_TOK, N_ATTN, N_FFN, N_L1, N_LATE, N_MOE = (16 * n for n in (3, 6, 4, 2, 5, 4))
        PLAN = 10
        TERNARY = 6

        def load_all(eng, loads):
            for s, t, n in loads:
                eng.dma_start(t, a[n]).then_inc(s, 16)

        def bring_back(eng, i0, n):
            for j in range(2):
                eng.wait_ge(y_stored[j], 16 * (NBLK // 2))
            both = ydisp[0:ROWS_Y, :].rearrange("(k r) d -> k r d", k=2)
            for g in range(G):
                t, r0, r = g * NT + i0, g * T + COL[i0], ROWS[i0]
                if n == 1:
                    eng.dma_start(back[0:r, t, :, :], both[:, r0:r0 + r, :].rearrange("k p d -> p k d")).then_inc(returned[g], 16)
                else:
                    for k in range(2):
                        eng.dma_start(back[0:r, t:t + n, k, :],
                                      both[k, r0:r0 + n * r, :].rearrange("(i p) d -> p i d", p=r)).then_inc(returned[g], 16)

        def each_block(eng, body, first, end):
            turns = range(XBUF, end - XBUF + 1, XBUF)
            after = turns[-1] + XBUF
            for b in range(first, XBUF):
                body(b, b)
            with eng.Fori(1, after // XBUF) as i:
                for q in range(XBUF):
                    body(XBUF * i + q, q)
            for b in range(after, end):
                body(b, b % XBUF)

        def wait_loaded(eng, b, q):
            eng.wait_ge(x_loaded[q], (b - q) * (16 // XBUF) + 16)

        @block.sync
        def _(sp):
            sp.dma_start(pat[:], a["pat"][:, 0]).then_inc(pat_loaded, 16)
            for s in sg.values():
                sp.sem_inc(s.sem, 1)
            sp.sem_inc(counting, 1)
            load_all(sp, [(w_ffn, w1f, "w1f"), (w_ffn, w2f, "w2f"), (w_l1, aq, "aq"), (w_l1, ak, "ak"),
                          (w_ffn, convw[:], "convw"), (w_ffn, convb[:], "convb"), (w_late, owT[:], "owT"),
                          (w_late, ob3[:], "ob3"), (w_late, avT[:], "avT"), (w_late, wr[:], "wr"),
                          (w_late, brb[:], "brb")])
            sp.wait_ge(tables, 4)
            sp.dma_start(disp[DUMMY:, :].rearrange("(n p) d -> p n d", p=128),
                         padrow[:].unsqueeze(1).to_broadcast([128, NBLK - LEAST, DW])).then_inc(pads, 16)
            for g in range(1, G):
                need(sp, "tok_mm", g - 1)
                sp.dma_start(pat[:], a["pat"][:, g]).then_inc(pat_loaded, 16)
            sp.wait_ge(row_consts, 1)
            sp.wait_ge(fused_ps, 1)
            sp.wait_ge(bias_ps, 1)
            sp.wait_ge(ternary, TERNARY)
            sp.wait_ge(qk_ps, 1)
            load_all(sp, [(w_moe, mw1[:], "mw1"), (w_moe, mw2[:], "mw2"), (w_moe, mb1[:], "mb1")])
            need(sp, "sc_mm", G - 1)
            sp.dma_start(mb2, a["mb2"]).then_inc(w_moe, 16)
            sp.wait_ge(pad_starts, 1)
            for e in range(E):
                row = sp.value_load(padint[0:1, e:e + 1], min_val=0, max_val=E * RS - PAD)
                sp.dma_start(disp[bass.ds(row, PAD), :].rearrange("(n p) d -> p n d", n=4),
                             padrow[0:PAD // 4].unsqueeze(1).to_broadcast([PAD // 4, 4, DW])).then_inc(pads, 16)
            sp.wait_ge(plan, PLAN)
            sp.wait_ge(dispatched, 16 * 2 * G * NT)
            need(sp, "lg_mm", G - 1)

            def load(b, q):
                if not isinstance(b, int) or b >= XBUF:
                    need(sp, "x_turned", b - XBUF)
                    need(sp, "yrows", b - XBUF)
                row = sp.value_load(bint[0:1, 1, bass.ds(b, 1)], min_val=0, max_val=ROWS_ALL - 128)
                sp.dma_start(xb[:, q, :], disp[bass.ds(row, 128), :]).then_inc(x_loaded[q], 16)

            each_block(sp, load, 0, NBLK)
            bring_back(sp, 0, 2)
            for g in range(G):
                for i0, n in ((0, 2), (2, 1)):
                    t, r0, r = g * NT + i0, g * T + COL[i0], ROWS[i0]
                    sp.wait_ge(added, 4 * (g + 1))
                    if i0 == 0:
                        sp.wait_ge(pool_added, 2 * (g + 1))
                    sp.dma_start(out[r0:r0 + n * r, :].rearrange("(i p) d -> p i d", p=r),
                                 hall[0:r, t:t + n, :]).then_inc(out_done, 16)
            sp.wait_ge(out_done, 16 * 2 * G)
            sp.wait_ge(w_moe, N_MOE)

        @block.gpsimd
        def _(pool):
            p = nc.gpsimd
            p.memset(ident[:], 0.0)
            p.memset(onesf[:], 1.0)
            p.memset(headsel[:], 1.0)
            p.memset(expsel[:], 0.0)
            p.memset(identb[:], 0.0)
            p.memset(cmask[:], 0.0)
            p.memset(padrow[:], 0.0)
            p.memset(onesb[:], 1.0)
            p.memset(before[:], 1.0)
            p.memset(valid[:], 1.0)
            p.iota(iota8[:], pattern=[[0, NT], [1, E]], base=0, channel_multiplier=0, allow_small_or_imprecise_dtypes=True)
            p.iota(tid[:], pattern=[[PT, NT]], base=0, channel_multiplier=1, allow_small_or_imprecise_dtypes=True)
            p.iota(run[:], pattern=[[RS, E]], base=0, channel_multiplier=0, allow_small_or_imprecise_dtypes=True)
            p.iota(base[:], pattern=[[RS, E]], base=0, channel_multiplier=0, allow_small_or_imprecise_dtypes=True)
            p.iota(blkno[:], pattern=[[1, NBLK], [0, E]], base=0, channel_multiplier=0, allow_small_or_imprecise_dtypes=True)
            p.iota(idle[:], pattern=[[128, NBLK]], base=DUMMY - 128 * LEAST, channel_multiplier=0, allow_small_or_imprecise_dtypes=True)
            p.iota(eno[:], pattern=[[0, NBLK], [1, E]], base=0, channel_multiplier=0, allow_small_or_imprecise_dtypes=True)
            p.memset(power[:], -0.5).then_inc(tables, 1)
            def expand(k):
                ev = expsel[:].rearrange("p r c (h m) -> p r (c h) m", m=HD)
                p.affine_select(out=ev, in_=ev, compare_op=ALU.not_equal, fill=1.0, base=-24 * k,
                                pattern=[[-HEADS, 3], [-1, HEADS], [0, HD]], channel_multiplier=1)

            pool.wait_ge(tables, 1)
            expand(0)
            p.affine_select(out=identb[:], in_=identb[:], compare_op=ALU.not_equal, fill=1.0, base=0,
                            pattern=[[-1, 128]], channel_multiplier=1)
            p.affine_select(out=ident[:], in_=ident[:], compare_op=ALU.not_equal, fill=1.0, base=0,
                            pattern=[[-1, 128]], channel_multiplier=1)
            p.affine_select(out=before[:], in_=before[:], compare_op=ALU.is_gt, fill=0.0, base=0,
                            pattern=[[1, 128]], channel_multiplier=-1)
            p.affine_select(out=valid[:, 2, :], in_=valid[:, 2, :], compare_op=ALU.is_ge, fill=0.0, base=ROWS[2] - 1,
                            pattern=[[0, E]], channel_multiplier=-1)
            p.affine_select(out=headsel[:], in_=headsel[:], compare_op=ALU.is_ge, fill=0.0, base=0,
                            pattern=[[-HD, HEADS // DC]], channel_multiplier=1).then_inc(tables, 1)
            pool.wait_ge(tables, 2)
            p.iota(padrow[:, D:D + 1], pattern=[[0, 1]], base=B * S, channel_multiplier=1, allow_small_or_imprecise_dtypes=True)
            p.memset(padrow[:, D + 1:D + 2], -1.0)
            p.affine_select(out=headsel[:], in_=headsel[:], compare_op=ALU.is_ge, fill=0.0, base=HD - 1,
                            pattern=[[HD, HEADS // DC]], channel_multiplier=-1)
            expand(1)
            p.affine_select(out=cmask[:], in_=cmask[:], compare_op=ALU.is_ge, fill=NEG, base=0,
                            pattern=[[-1, PT]], channel_multiplier=1).then_inc(tables, 1)
            pool.wait_ge(tables, 3)
            expand(2)
            cv = cmask[:].rearrange("p (n s) -> p n s", s=S)
            p.affine_select(out=cv, in_=cv, compare_op=ALU.is_ge, fill=NEG, base=S - 1,
                            pattern=[[S, 3], [0, S]], channel_multiplier=-1).then_inc(tables, 1)

            def rstd(g, mv, ep, rs, n):
                need(pool, mv, g)
                inc(p.tensor_scalar(lnv[n][:], lnmv[n][:, :, 1], 1e-5, None, ALU.add), ep)
                need(pool, ep, g)
                inc(p.tensor_tensor(lnr[n][:], lnv[n][:], power[0:PT, :], ALU.pow), rs)

            def a_ln(g):
                rstd(g, "mv1", "eps1", "rstd1", 0)
                if g == 0:
                    pool.wait_ge(w_late, N_LATE)
                need(pool, "xn1", g)
                inc(p.tensor_tensor(hA[:], hA[:], ob3[:].unsqueeze(1).to_broadcast([PT, NT, D]), ALU.add), "hb")

            def b_ln2(g):
                rstd(g, "mv2", "eps2", "rstd2", 1)

            def b_q(g):
                need(pool, "qs1", g)
                need(pool, "scb_ps", g - 1)
                for i in range(NT):
                    ins = p.tensor_scalar(diag[:, i, :], ident[0:PT, 0:PT], deqs[:, i:i + 1], None, ALU.mult)
                inc(ins, "diag1")

            def b_amax(g):
                need(pool, "qs2", g, 4)
                need(pool, "deq_ps", g)
                for i in range(NT):
                    ins = p.tensor_scalar(diag[:, i, :], ident[0:PT, 0:PT], qsc2[:, i:i + 1], None, ALU.mult)
                inc(ins, "diag2")

            def c_ln3(g):
                rstd(g, "mv3", "eps3", "rstd3", 2)

            def c_ln4(g):
                rstd(g, "mv4", "eps4", "rstd4", 2)

            def c_slot(g):
                need(pool, "rt", g, 10)
                if g == G - 1:
                    pool.wait_ge(pads, 16 * (E + 1))
                dispatch(0)

            def c_slot2(g):
                dispatch(1)

            def dispatch(k):
                for i in range(NT):
                    n = ROWS[i]
                    p.indirect_dma_start(out=disp, out_offset=bass.IndirectOffsetOnAxis(ap=slotu[0:n, k, i:i + 1], axis=0),
                                         in_=xs[0:n, i, :], in_offset=None).then_inc(dispatched, 16)

            in_order(a_ln, b_ln2, b_q, b_amax, c_ln3, c_ln4, c_slot, c_slot2)
            pool.wait_ge(dispatched, 16 * 2 * NT * G)

            def store(b, q):
                j = q % 2
                need(pool, "ys", b)
                need(pool, "yrows", b)
                if b:
                    pool.wait_ge(y_stored[1 - j], ((b - 1) // 2 + 1) * 16)
                p.indirect_dma_start(out=ydisp, out_offset=bass.IndirectOffsetOnAxis(ap=yrow[:, q:q + 1], axis=0),
                                     in_=yb[:, j, :], in_offset=None).then_inc(y_stored[j], 16)

            for b in range(NBLK):
                store(b, b % XBUF)

            for g in range(G):
                t = g * NT + 1
                for k in range(2):
                    pool.wait_ge(gated, 2 * g + k + 1)
                    if k:
                        pool.wait_ge(pool_added, 2 * g + 1)
                    p.tensor_tensor(hall[0:PT, t, :], hall[0:PT, t, :], back[0:PT, t, k, :], ALU.add).then_inc(pool_added, 1)

        @block.tensor
        def _(pe):
            mm, tr = nc.tensor.matmul, nc.tensor.transpose
            def s_fuse(g):
                pe.wait_ge(w_attn, N_ATTN)
                for j, w in enumerate((qkw, qkw, pvw)):
                    for c in range(DC):
                        for m in range(DC):
                            ins = mm(psB[:, j, c * D:(c + 1) * D], w[:, m, c * 128:(c + 1) * 128],
                                     inwT[:, m, j * D:(j + 1) * D], start=(m == 0), stop=(m == DC - 1))
                ins.then_inc(fused_ps, 1)

            def s_bias(g):
                pe.wait_ge(w_attn, N_ATTN)
                for o in range(3 * DC):
                    b = qkb if o < 2 * DC else pvb
                    for m in range(DC):
                        ins = mm(psB[:, 3, o:o + 1], inwT[:, m, o * 128:(o + 1) * 128], b[:, m:m + 1],
                                 start=(m == 0), stop=(m == DC - 1))
                ins.then_inc(bias_ps, 1)

            def s_tern(g):
                pe.wait_ge(tables, 1)
                pe.wait_ge(fused, 1)
                pe.wait_ge(abs_sums, 1)
                mm(psB[:, 0, 0:2], onesf[:], wsum[:], start=True, stop=True).then_inc(abs_ps, 1)

            def s_l1(g):
                pe.wait_ge(w_l1, N_L1)
                pe.wait_ge(fused, 1)
                for c in range(DC):
                    for o in range(DC):
                        ins = mm(psB[:, 1, c * D:(c + 1) * D], aq[:, o, c * 128:(c + 1) * 128], ak[:, o, :],
                                 start=(o == 0), stop=(o == DC - 1))
                ins.then_inc(qk_ps, 1)

            def to_columns(src, ps, tile_signal, g, done, bank=0):
                for i in range(NT):
                    need(pe, tile_signal, g, i + 1)
                    for c in range(DC):
                        ins = tr(ps[:, bank + c, COL[i]:COL[i] + ROWS[i]], src[0:ROWS[i], i, c * 128:(c + 1) * 128],
                                 ident[0:ROWS[i], 0:ROWS[i]])
                inc(ins, done)

            def row_slot(ps, i, b):
                return ps[0:ROWS[i], b + i // 2, (i % 2) * D:(i % 2) * D + D]

            def token_rows(tiles):
                for i in tiles:
                    for c in range(FC):
                        ins = mm(row_slot(psA, i, 2), pat[:, c, COL[i]:COL[i] + ROWS[i]], tokw[:, c, :],
                                 start=(c == 0), stop=(c == FC - 1))
                    inc(ins, "tok_mm")

            def a_tok(g):
                if g == 0:
                    pe.wait_ge(counting, 1)
                    pe.wait_ge(w_tok, N_TOK)
                else:
                    need(pe, "proj_sb", g - 1)
                    need(pe, "pv", g - 1)
                pe.wait_ge(pat_loaded, g * 16 + 16)
                token_rows((0, 1))

            def a_tok2(g):
                token_rows((2,))

            def a_cols(g):
                need(pe, "h1", g - 1)
                pe.wait_ge(tables, 4)
                to_columns(xnA, psA, "xn1", g, "xT1_ps")

            def a_proj(g):
                need(pe, "xT1", g)
                pe.wait_ge(fused, 1)
                project(g, 0, 4)

            def a_proj2(g):
                project(g, 4, 6)

            def project(g, lo, hi):
                for o in range(lo, hi):
                    bank = (2, 3, 0, 1, 2, 3)[o]
                    if o >= 4:
                        need(pe, "proj_sb", g, o - 3)
                    for c in range(DC):
                        ins = mm(psA[:, bank, 0:TP], fusw[:, c, o * 128:(o + 1) * 128], xT40[:, c, :],
                                 start=(c == 0), stop=(c == DC - 1))
                    inc(ins, "proj_mm")

            def a_prod(g):
                for r in range(3):
                    need(pe, "prods", g, r + 1)
                    for t, off in enumerate((0, 128, TP - 128)):
                        for c in range(DC):
                            o = t * 24 + r * 8 + c * 4
                            ins = mm(psA[:, 0, o:o + 4], prod[:, r, c, off:off + 128], headsel[:], start=True, stop=True)
                inc(ins, "sc_mm")

            def a_soft(g):
                need(pe, "smx", g)
                for t in range(3):
                    ins = tr(prT_ps[:, t * 128:(t + 1) * 128], prs[:, t].rearrange("p k h -> p (k h)"), identb[:])
                inc(ins, "prT_ps")

            def a_pv(g):
                need(pe, "prTs", g)
                need(pe, "proj_sb", g)
                spread_heads(0)
                spread_heads(1)

            def a_pv2(g):
                need(pe, "pv", g, 1)
                spread_heads(2)

            def spread_heads(r):
                for c in range(DC):
                    ins = mm(psA[:, (2, 0, 2)[r] + c, 0:TP], expsel[:, r, c, :], prT[:], start=True, stop=True)
                inc(ins, "ex_mm")

            def a_out(g):
                if g == 0:
                    pe.wait_ge(w_late, N_LATE)
                need(pe, "pv", g)
                for i in range(NT):
                    for c in range(DC):
                        ins = mm(row_slot(psA, i, 0), oTc[:, c, COL[i]:COL[i] + ROWS[i]], owT[:, c, :],
                                 start=(c == 0), stop=(c == DC - 1))
                    inc(ins, "op_mm")

            def spread(g, done, bank):
                for i in range(NT):
                    ins = mm(psB[:, bank, COL[i]:COL[i] + ROWS[i]], onesf[0:ROWS[i], :],
                             diag[0:ROWS[i], i, 0:ROWS[i]], start=True, stop=True)
                inc(ins, done)

            def b_q(g):
                need(pe, "h2", g - 1)
                if g == 0:
                    pe.wait_ge(ternary, TERNARY)
                    pe.wait_ge(qk_fused, 1)
                to_columns(xq, psB, "xqs", g, "xTq_ps")
                need(pe, "diag1", g)
                need(pe, "xqTs", g)
                spread(g, "deq_ps", 0)

            def hidden(g, lo, hi):
                need(pe, "xqTs", g)
                for m in range(lo, hi):
                    if m == 1:
                        need(pe, "deqBs", g)
                    if m >= 2:
                        need(pe, "deq", g, m - 1)
                    for c in range(DC):
                        ins = mm(psB[:, (m + 1) % 2, 0:T], w1q[:, c, m * 128:(m + 1) * 128], xqT[:, c, :],
                                 start=(c == 0), stop=(c == DC - 1))
                    inc(ins, "f1_mm")

            def b_f1a(g):
                hidden(g, 0, 3)

            def b_f1b(g):
                hidden(g, 3, 6)

            def b_f1c(g):
                hidden(g, 6, HC)

            def b_amax(g):
                need(pe, "vmaxs", g)
                for i in range(NT):
                    ins = tr(psB[0:ROWS[i], 0, i * 128:(i + 1) * 128], vmax[:, COL[i]:COL[i] + ROWS[i]], ident[:])
                inc(ins, "vT_ps")

            def b_spread(g):
                need(pe, "diag2", g)
                spread(g, "scb_ps", 1)

            def b_f2(g):
                need(pe, "vqs", g)
                contract((0, 1))

            def b_f2b(g):
                contract((2,))

            def contract(tiles):
                for i in tiles:
                    for m in range(HC):
                        ins = mm(row_slot(psB, i, 0), vq[:, m, COL[i]:COL[i] + ROWS[i]], w2q[:, m, :],
                                 start=(m == 0), stop=(m == HC - 1))
                    inc(ins, "f2_mm")

            def c_cols3(g):
                need(pe, "rt", g - 1)
                pe.wait_ge(biases, 2)
                to_columns(xs, psB, "xn3", g, "xT3_ps", 2)

            def c_yv(g):
                need(pe, "xT3s", g)
                for o in range(DC):
                    for c in range(DC):
                        ins = mm(psB[:, 2 + o, 0:T], aqk[:, c, o * 128:(o + 1) * 128], xT3[:, c, :],
                                 start=(c == 0), stop=(c == DC - 1))
                inc(ins, "yT_ps")

            def c_v(g):
                need(pe, "yTs", g)
                for i in range(NT):
                    for c in range(DC):
                        ins = mm(row_slot(psB, i, 2), xT3[:, c, COL[i]:COL[i] + ROWS[i]], avT[:, c, :],
                                 start=(c == 0), stop=(c == DC - 1))
                inc(ins, "vv_ps")

            def c_sc(g):
                need(pe, "v3s", g)
                for i in range(NT):
                    cols = slice(COL[i], COL[i] + ROWS[i])
                    scores = psB[0:ROWS[i], 2, i * PT:i * PT + ROWS[i]]
                    for c in range(DC):
                        mm(scores, yT3[:, c, cols], xT3[:, c, cols], start=(c == 0), stop=False)
                    ins = mm(scores, ident[0:ROWS[i], 0:ROWS[i]], cmask[0:ROWS[i], 0:ROWS[i]], start=False, stop=True)
                inc(ins, "s3_mm")

            def c_pv(g):
                for i in range(NT):
                    need(pe, "p3", g, i + 1)
                    n = ROWS[i]
                    ins = tr(psB[0:n, 3, i * PT:i * PT + n], P3[0:n, i, 0:n], ident[0:n, 0:n])
                inc(ins, "pT3_ps")
                need(pe, "pT3s", g)
                for i in range(NT):
                    n = ROWS[i]
                    ins = mm(row_slot(psB, i, 2), PT3[0:n, i, 0:n], V3[0:n, i, :], start=True, stop=True)
                    inc(ins, "pv3_mm")

            def c_cols4(g):
                need(pe, "h3", g)
                to_columns(xs, psB, "xn4", g, "xT4_ps", 2)

            def c_rt(g):
                need(pe, "xT4s", g)
                for i in range(NT):
                    for c in range(DC):
                        ins = mm(psB[0:ROWS[i], 2, i * E:(i + 1) * E], xT3[:, c, COL[i]:COL[i] + ROWS[i]], wr[:, c, :],
                                 start=(c == 0), stop=(c == DC - 1))
                inc(ins, "lg_mm")

            def c_rank(g):
                need(pe, "rt", g, 5)
                need(pe, "lg", g)
                mm(psB[:, 3, 0:(NT + 1) * E], before[:], cntb[:].rearrange("p t e -> p (t e)"), start=True, stop=False)
                for i in range(NT):
                    ins = mm(psB[:, 3, (i + 1) * E:(NT + 1) * E].rearrange("p (t e) -> p t e", e=E), onesb[:],
                             cntb[:, i, :].unsqueeze(1).to_broadcast([PT, NT - i, E]), start=False, stop=(i == NT - 1))
                inc(ins, "rank_mm")

            in_order(s_fuse, s_bias, s_tern, s_l1, a_tok, a_tok2, a_cols, a_proj, a_proj2, a_prod, a_soft, a_pv, a_pv2, a_out,
                     b_q, b_f1a, b_f1b, b_f1c, b_amax, b_spread, b_f2, b_f2b,
                     c_cols3, c_yv, c_v, c_sc, c_pv, c_cols4, c_rt, c_rank)

            def turn_x(b, q):
                j = q % 2
                wait_loaded(pe, b, q)
                need(pe, "xTs", b - 2)
                for c in range(DC):
                    ins = tr(psA[:, j, c * 128:(c + 1) * 128], xb[:, q, c * 128:(c + 1) * 128], ident[:])
                inc(ins, "x_turned")

            def up(b, j):
                need(pe, "xTs", b)
                need(pe, "w1_in", b)
                need(pe, "hTs", b - 2)
                for f in range(FFC):
                    for c in range(DC):
                        ins = mm(psB[:, j, f * 128:(f + 1) * 128], w1s[:, j, c, f * 128:(f + 1) * 128], xbT[:, j, c, :],
                                 start=(c == 0), stop=(c == DC - 1))
                inc(ins, "h_mm")

            def down(b, j):
                e = pe.value_load(bint[0:1, 0, bass.ds(b, 1)], min_val=0, max_val=E - 1)
                need(pe, "ys", b - 2)
                need(pe, "hTs", b)
                for f in range(FFC):
                    ins = mm(psA[:, 2 + j, 0:D], hTe[:, j, f, :], mw2[:, bass.ds(e, 1), f, :],
                             start=(f == 0), stop=(f == FFC - 1))
                inc(ins, "y_mm")

            def ahead(b, q):
                up(b, q % 2)
                turn_x(b + 1, (q + 1) % XBUF)
                down(b - 1, (q + 1) % 2)

            need(pe, "rt", G - 1)
            need(pe, "h1", G - 1)
            pe.wait_ge(w_moe, N_MOE)
            for n in range(WARM):
                mm(psA[:, 2, :], ident[:], mw2[:, 0, 0:2, :], start=True, stop=True)
            pe.wait_ge(plan, PLAN)
            turn_x(0, 0)
            up(0, 0)
            turn_x(1, 1)
            each_block(pe, ahead, 1, NBLK - 1)
            up(NBLK - 1, 1)
            down(NBLK - 2, 0)
            down(NBLK - 1, 1)

        @block.scalar
        def _(act):
            A = nc.scalar.activation
            load_all(act, [(w_tok, tokw[:], "tokw"), (w_tok, rowc[:], "rowc"), (w_tok, posr, "posr"), (w_attn, qkw, "qkw"),
                           (w_attn, inwT, "inwT"), (w_attn, pvw, "pvw"), (w_attn, qkb[:], "qkb"),
                           (w_attn, pvb[:], "pvb"), (w_attn, inb[:], "inb")])

            def s_fuse(g):
                act.wait_ge(fused_ps, 1)
                A(fusw[:, :, 0:D], psB[:, 0, :].rearrange("p (c d) -> p c d", d=D), ACT.Copy)
                A(fusw[:, :, D:2 * D], psB[:, 1, :].rearrange("p (c d) -> p c d", d=D), ACT.Copy)
                A(fusw[:, :, 2 * D:], psB[:, 2, :].rearrange("p (c d) -> p c d", d=D), ACT.Copy).then_inc(fused, 1)

            def s_l1(g):
                act.wait_ge(qk_ps, 1)
                A(aqk[:], psB[:, 1, :].rearrange("p (c d) -> p c d", d=D), ACT.Copy).then_inc(qk_fused, 1)

            def a_cols(g):
                need(act, "xT1_ps", g)
                need(act, "proj_mm", g - 1)
                x4 = xT40[:].rearrange("p c (n s) -> p c n s", s=SP4)
                for c in range(DC):
                    src = psA[:, c, 0:T].rearrange("p (n s) -> p n s", s=S)
                    A(x4[:, c, :, 0:S], src, ACT.Copy)
                    ins = A(x4[:, c, :, S:SP4], src[:, :, 0:SP4 - S], ACT.Copy)
                inc(ins, "xT1")

            def a_proj(g):
                need(act, "prods", g - 1)
                need(act, "pv", g - 1)
                act.wait_ge(biases, 2)
                projected(g, 0, 4)

            def a_proj2(g):
                projected(g, 4, 6)

            def projected(g, lo, hi):
                for o in range(lo, hi):
                    bank = (2, 3, 0, 1, 2, 3)[o]
                    dst = (qT, qT, kT, kT, vT, vT)[o][:, o % 2, :]
                    need(act, "proj_mm", g, o + 1)
                    inc(A(dst, psA[:, bank, 0:TP], ACT.Identity, bias=fusb[:, o:o + 1], scale=QSCALE if o < 2 else 1.0), "proj_sb")

            def a_soft(g):
                need(act, "smx", g, 2)
                inc(A(sexp[:], sexp[:], ACT.Exp), "pexp")

            def a_pv(g):
                need(act, "prT_ps", g)
                need(act, "ex_mm", g - 1)
                A(prT[:, 0:256], prT_ps[:, 0:256], ACT.Copy)
                inc(A(prT[:, 256:TP], prT_ps[:, 256 + (384 - TP):384], ACT.Copy), "prTs")

            def b_ln2(g):
                if g == 0:
                    act.wait_ge(constants, 1)
                need(act, "qs1", g, 4)
                need(act, "xTq_ps", g - 1)
                for i in range(NT):
                    n = ROWS[i]
                    inc(A(xq[0:n, i, :], xnB[0:n, i, :], ACT.Identity, bias=magic[0:n, :], scale=qsc[0:n, i:i + 1]), "xqs")

            def b_q(g):
                need(act, "deq_ps", g)
                need(act, "deq", g - 1)
                inc(A(deqB[:], psB[:, 0, 0:T], ACT.Copy), "deqBs")

            def convolved(g, lo, hi):
                for m in range(lo, hi):
                    if m < HC:
                        need(act, "deq", g, m + 1)
                        need(act, "silu", g, max(m - RING + 1, 0))
                        dst = yc[:, m % RING, :].rearrange("p (n s) -> p n s", s=S)
                        inc(A(dst, hpad[:, m % RING, :, 1:S + 1], ACT.Identity, bias=convb[:, m:m + 1],
                              scale=convw[:, m, 1:2]), "cact")
                    if m >= 3:
                        need(act, "cv2", g, m - 2)
                        if m == 3:
                            need(act, "vqs", g - 1)
                        inc(A(v[:, m - 3, :], yc[:, (m - 3) % RING, :], ACT.Silu), "silu")

            def b_f1a(g):
                convolved(g, 0, 3)

            def b_f1b(g):
                convolved(g, 3, 6)

            def b_f1c(g):
                convolved(g, 6, HC)

            def b_f1d(g):
                convolved(g, HC, HC + 3)

            def c_cols3(g):
                need(act, "xT3_ps", g)
                need(act, "lg_mm", g - 1)
                inc(A(xT3[:], psB[:, 2:4, 0:T], ACT.Copy), "xT3s")

            def c_yv(g):
                need(act, "yT_ps", g)
                inc(A(yT3[:], psB[:, 2:4, 0:T], ACT.Copy), "yTs")

            def c_v(g):
                need(act, "vv_ps", g)
                A(V3[:, 0:2, :].rearrange("p i d -> p (i d)"), psB[0:PT, 2, :], ACT.Copy)
                inc(A(V3[0:ROWS[2], 2, :], psB[0:ROWS[2], 3, 0:D], ACT.Copy), "v3s")

            def c_sc(g):
                need(act, "s3", g)
                for i in range(NT):
                    n = ROWS[i]
                    inc(A(P3[0:n, i, 0:n], psB[0:n, 2, i * PT:i * PT + n], ACT.Exp, bias=nm3[0:n, i:i + 1], scale=ASCALE,
                          accum_out=rs3[0:n, i:i + 1]), "p3")

            def c_pv(g):
                need(act, "pT3_ps", g)
                n = ROWS[2]
                A(PT3[:, 0:2, :].rearrange("p i q -> p (i q)"), psB[0:PT, 3, 0:2 * PT], ACT.Copy)
                inc(A(PT3[0:n, 2, 0:n], psB[0:n, 3, 2 * PT:2 * PT + n], ACT.Copy), "pT3s")

            def c_cols4(g):
                need(act, "xT4_ps", g)
                inc(A(xT3[:], psB[:, 2:4, 0:T], ACT.Copy), "xT4s")

            def c_rank(g):
                need(act, "rt", g, 11)
                inc(A(ge[:], gd[:], ACT.Exp), "gexp")

            in_order(s_fuse, s_l1, a_cols, a_proj, a_proj2, a_soft, a_pv, b_ln2, b_q, b_f1a, b_f1b, b_f1c, b_f1d, c_cols3, c_yv, c_v, c_sc, c_pv, c_cols4,
                     c_rank)
            need(act, "rank_mm", G - 1)

            need(act, "vqs", G - 1)
            def w1_columns(b, j):
                e = act.value_load(bint[0:1, 0, bass.ds(b, 1)], min_val=0, max_val=E - 1)
                need(act, "h_mm", b - 2)
                inc(A(w1s[:, j], mw1[:, bass.ds(e, 1), :, :], ACT.Copy), "w1_in")

            def x_columns(b, j):
                need(act, "x_turned", b)
                inc(A(xbT[:, j], psA[:, j, 0:D].rearrange("p (c t) -> p c t", t=128), ACT.Copy), "xTs")

            def columns(b, q):
                w1_columns(b, q % 2)
                x_columns(b, q % 2)

            act.wait_ge(plan, PLAN)
            act.wait_ge(w_moe, N_MOE)
            each_block(act, columns, 0, NBLK)
            bring_back(act, 2, 1)
            need(act, "rt", G - 1)
            for g in range(G):
                t = g * NT + 1
                act.wait_ge(returned[g], 48)
                for k in range(2):
                    A(back[0:PT, t, k, :], back[0:PT, t, k, :], ACT.Copy, scale=gates[0:PT, t, k:k + 1]).then_inc(gated, 1)

        @block.vector
        def _(dve):
            d = nc.vector
            for t in (hA, xnB, am2, mx3, rs3, lgt, xs, lnmv[0], lnmv[1], lnmv[2]):
                d.memset(t[:], 1.0)
            d.memset(hpad[:], 0.0)
            d.memset(cntb[:], 0.0)
            d.memset(magic[:], MAGIC).then_inc(constants, 1)
            dve.wait_ge(w_tok, N_TOK)
            d.tensor_tensor(rowc[:], rowc[:], posr, ALU.add).then_inc(row_consts, 1)

            def s_bias(g):
                dve.wait_ge(bias_ps, 1)
                d.tensor_tensor(fusb[:], psB[:, 3, 0:6], inb[:], ALU.add).then_inc(biases, 1)
                dve.wait_ge(biases, 1)
                d.tensor_scalar(fusb[:, 0:2], fusb[:, 0:2], QSCALE, None, ALU.mult).then_inc(biases, 1)

            def s_tern(g):
                dve.wait_ge(w_ffn, N_FFN)
                d.tensor_reduce(wsum[:, 0:1], w1f[:].rearrange("p c f -> p (c f)"), AX, ALU.add, apply_absolute_value=True)
                d.tensor_reduce(wsum[:, 1:2], w2f[:].rearrange("p c f -> p (c f)"), AX, ALU.add,
                                apply_absolute_value=True).then_inc(abs_sums, 1)
                dve.wait_ge(abs_ps, 1)
                d.tensor_scalar(wmean[:], psB[:, 0, 0:2], 1.0 / (HID * D), 1e-5, ALU.mult, ALU.max).then_inc(ternary, 1)
                dve.wait_ge(ternary, 1)
                d.tensor_scalar(wdeq[:], wmean[:], 1.0 / 127.0, None, ALU.mult)
                d.reciprocal(wscale[:], wmean[:]).then_inc(ternary, 1)
                dve.wait_ge(ternary, 2)
                for n, (w, q) in enumerate(((w1f, w1q), (w2f, w2q))):
                    d.tensor_scalar(w[:], w[:], wscale[:, n:n + 1], MAGIC, ALU.mult, ALU.add).then_inc(ternary, 1)
                for n, (w, q) in enumerate(((w1f, w1q), (w2f, w2q))):
                    dve.wait_ge(ternary, 3 + n)
                    d.tensor_scalar(w[:], w[:], MAGIC - 1.0, MAGIC + 1.0, ALU.max, ALU.min).then_inc(clipped, 1)
                for n, (w, q) in enumerate(((w1f, w1q), (w2f, w2q))):
                    dve.wait_ge(clipped, 1 + n)
                    d.tensor_scalar(q[:], w[:], MAGIC, None, ALU.subtract).then_inc(ternary, 1)

            def stats(g, x, ready, st, mv, n):
                for i in range(NT):
                    r = ROWS[i]
                    need(dve, ready, g, i + 1)
                    inc(d.bn_stats(lnst[n][0:r, i, :], x(i)), st)
                for i in range(NT):
                    need(dve, st, g, i + 1)
                    inc(d.bn_aggr(lnmv[n][0:ROWS[i], i, :], lnst[n][0:ROWS[i], i, :]), mv)

            def normalise(g, x, y, n, rs, done):
                need(dve, rs, g)
                for i in range(NT):
                    r = ROWS[i]
                    inc(d.tensor_scalar(y[0:r, i, :], x(i), lnmv[n][0:r, i, 0:1], lnr[n][0:r, i:i + 1],
                                        ALU.subtract, ALU.mult), done)

            def row_slot(ps, i, b):
                return ps[0:ROWS[i], b + i // 2, (i % 2) * D:(i % 2) * D + D]

            def a_ln(g):
                dve.wait_ge(row_consts, 1)
                for i in range(NT):
                    r = ROWS[i]
                    need(dve, "tok_mm", g, BANKED[i])
                    inc(d.tensor_tensor(hA[0:r, i, :], row_slot(psA, i, 2), rowc[0:r, :], ALU.add), "h0")
                stats(g, lambda i: hA[0:ROWS[i], i, :], "h0", "st1", "mv1", 0)

            def a_norm(g):
                need(dve, "xT1_ps", g - 1)
                normalise(g, lambda i: hA[0:ROWS[i], i, :], xnA, 0, "rstd1", "xn1")

            q4, k4, v4 = (t[:].rearrange("p c (n s) -> p c n s", s=SEG) for t in (qT, kT, vT))

            def a_prod(g):
                need(dve, "proj_sb", g, 4)
                need(dve, "sc_mm", g - 1)
                for r in range(1, SEG):
                    o4 = prod[:, r - 1].rearrange("p c (n s) -> p c n s", s=SEG)
                    d.tensor_tensor(o4[:, :, :, 0:SEG - r], q4[:, :, :, 0:SEG - r], k4[:, :, :, r:SEG], ALU.mult)
                    inc(d.tensor_tensor(o4[:, :, :, SEG - r:SEG], q4[:, :, :, SEG - r:SEG], k4[:, :, :, 0:r], ALU.mult), "prods")

            def a_soft(g):
                need(dve, "sc_mm", g)
                sc = psA[:, 0, 0:72].rearrange("p (t r h) -> p t r h", r=3, h=HEADS)
                inc(d.tensor_reduce(smax[:], sc.rearrange("p t r h -> p t h r"), AX, ALU.max), "smx")
                need(dve, "smx", g, 1)
                inc(d.tensor_tensor(sexp[:], sc, smax[:].unsqueeze(2).to_broadcast([128, 3, 3, HEADS]), ALU.subtract), "smx")
                need(dve, "pexp", g)
                inc(d.tensor_reduce(ssum[:], sexp[:].rearrange("p t r h -> p t h r"), AX, ALU.add), "smx")
                need(dve, "smx", g, 3)
                inc(d.reciprocal(smax[:], ssum[:]), "smx")
                need(dve, "smx", g, 4)
                inverse = smax[:].unsqueeze(2).to_broadcast([128, 3, 3, HEADS])
                inc(d.tensor_tensor(prb[:], sexp[:], inverse, ALU.mult), "smx")
                part = [prs[:, :, k, :].rearrange("p t (r h) -> p t r h", h=HEADS) for k in range(3)]
                inc(d.tensor_tensor(part[0], sexp[:], inverse, ALU.mult), "smx")
                need(dve, "smx", g, 6)
                inc(d.tensor_tensor(prb[:], prb[:], part[0], ALU.subtract), "smx")
                need(dve, "smx", g, 7)
                inc(d.tensor_copy(part[1], prb[:]), "smx")
                need(dve, "smx", g, 8)
                inc(d.tensor_tensor(part[2], prb[:], part[1], ALU.subtract), "smx")

            def a_pv(g):
                need(dve, "op_mm", g - 1)
                weigh(g, 1)
                weigh(g, 2)

            def a_pv2(g):
                weigh(g, 3)

            def weigh(g, r):
                bank = (2, 0, 2)[r - 1]
                dst = (oT, pv1, pv2)[r - 1][:].rearrange("p c (n s) -> p c n s", s=SEG)
                w4 = psA[:, bank:bank + 2, 0:TP].rearrange("p c (n s) -> p c n s", s=SEG)
                need(dve, "ex_mm", g, r)
                if r == 1:
                    need(dve, "proj_sb", g)
                d.tensor_tensor(dst[:, :, :, 0:SEG - r], w4[:, :, :, 0:SEG - r], v4[:, :, :, r:SEG], ALU.mult)
                inc(d.tensor_tensor(dst[:, :, :, SEG - r:SEG], w4[:, :, :, SEG - r:SEG], v4[:, :, :, 0:r], ALU.mult), "pv")
                if r > 1:
                    need(dve, "pv", g, 2 * r - 2)
                    if r == 2:
                        inc(d.tensor_tensor(oT[:], oT[:], pv1[:], ALU.add), "pv")
                    else:
                        a4, b4 = (t[:].rearrange("p c (n s) -> p c n s", s=SP4)[:, :, :, 0:S] for t in (oT, pv2))
                        inc(d.tensor_tensor(oTc[:].rearrange("p c (n s) -> p c n s", s=S), a4, b4, ALU.add), "pv")

            def a_out(g):
                need(dve, "hb", g)
                for i in range(NT):
                    r = ROWS[i]
                    need(dve, "op_mm", g, BANKED[i])
                    inc(d.tensor_tensor(hall[0:r, g * NT + i, :], row_slot(psA, i, 0), hA[0:r, i, :], ALU.add), "h1")

            def scales(g, amx, rec, qs, dq, w, name):
                need(dve, name, g, 1)
                inc(d.tensor_scalar(amx[:], amx[:], 1e-5, None, ALU.max), name)
                need(dve, name, g, 2)
                inc(d.reciprocal(rec[:], amx[:]), name)
                need(dve, name, g, 3)
                inc(d.tensor_scalar(qs[:], rec[:], 127.0, None, ALU.mult), name)
                inc(d.tensor_scalar(dq[:], amx[:], wdeq[0:PT, w:w + 1], None, ALU.mult), name)

            def row(g, i):
                return hall[0:ROWS[i], g * NT + i, :]

            def b_ln2(g):
                stats(g, lambda i: row(g, i), "h1", "st2", "mv2", 1)

            def b_norm2(g):
                need(dve, "xqs", g - 1)
                normalise(g, lambda i: row(g, i), xnB, 1, "rstd2", "xn2")
                need(dve, "xn2", g)
                inc(d.tensor_reduce(am[:], xnB[:], AX, ALU.max, apply_absolute_value=True), "qs1")
                scales(g, am, amr, qsc, deqs, 0, "qs1")

            def b_q(g):
                need(dve, "xTq_ps", g)
                need(dve, "f1_mm", g - 1)
                inc(d.tensor_scalar(xqT[:], psB[:, 0:2, 0:T], MAGIC, None, ALU.subtract), "xqTs")

            def convolved(g, lo, hi):
                for m in range(lo, hi):
                    if m < HC:
                        need(dve, "f1_mm", g, m + 1)
                        if m == 0:
                            need(dve, "deqBs", g)
                        need(dve, "cact", g, max(m - RING + 1, 0))
                        need(dve, "cv2", g, max(m - RING + 1, 0))
                        inc(d.tensor_tensor(hpad[:, m % RING, :, 1:S + 1],
                                            psB[:, (m + 1) % 2, 0:T].rearrange("p (n s) -> p n s", s=S),
                                            deqB[:].rearrange("p (n s) -> p n s", s=S), ALU.mult), "deq")
                    if 2 <= m < HC + 2:
                        j = m - 2
                        y = yc[:, j % RING, :].rearrange("p (n s) -> p n s", s=S)
                        need(dve, "cact", g, j + 1)
                        inc(d.scalar_tensor_tensor(y, hpad[:, j % RING, :, 0:S], convw[:, j, 0:1], y, ALU.mult, ALU.add), "cv1")
                    if m >= 3:
                        j = m - 3
                        y = yc[:, j % RING, :].rearrange("p (n s) -> p n s", s=S)
                        need(dve, "cv1", g, j + 1)
                        inc(d.scalar_tensor_tensor(y, hpad[:, j % RING, :, 2:S + 2], convw[:, j, 2:3], y, ALU.mult, ALU.add), "cv2")

            def b_f1a(g):
                convolved(g, 0, 3)

            def b_f1b(g):
                convolved(g, 3, 6)

            def b_f1c(g):
                convolved(g, 6, HC)

            def b_f1d(g):
                convolved(g, HC, HC + 3)

            def b_amax(g):
                need(dve, "silu", g)
                inc(d.tensor_reduce(vmax[:], v[:].rearrange("p m t -> p t m"), AX, ALU.max, apply_absolute_value=True), "vmaxs")
                need(dve, "vT_ps", g)
                d.tensor_reduce(am2[:, 0:2], psB[0:PT, 0, 0:256].rearrange("p (i k) -> p i k", k=128), AX, ALU.max)
                inc(d.tensor_reduce(am2[0:ROWS[2], 2:3], psB[0:ROWS[2], 0, 256:384], AX, ALU.max), "qs2")
                scales(g, am2, am2r, qsc2, deqs2, 1, "qs2")

            def b_spread(g):
                need(dve, "scb_ps", g)
                for k in range(2):
                    h = slice(k * HC // 2, (k + 1) * HC // 2)
                    inc(d.tensor_tensor(v[:, h, :], v[:, h, :],
                                        psB[:, 1, 0:T].unsqueeze(1).to_broadcast([128, HC // 2, T]), ALU.mult), "vsc")

            def b_round(g):
                need(dve, "f2_mm", g - 1)
                for k in range(2):
                    need(dve, "vsc", g, k + 1)
                    h = slice(k * HC // 2, (k + 1) * HC // 2)
                    inc(d.tensor_scalar(vq[:, h, :], v[:, h, :], MAGIC, -MAGIC, ALU.add, ALU.add), "vqs")

            def b_f2(g):
                contracted(g, (0, 1))

            def b_f2b(g):
                contracted(g, (2,))

            def contracted(g, tiles):
                for i in tiles:
                    need(dve, "f2_mm", g, BANKED[i])
                    inc(d.scalar_tensor_tensor(row(g, i), row_slot(psB, i, 0), deqs2[0:ROWS[i], i:i + 1], row(g, i),
                                               ALU.mult, ALU.add), "h2")

            def c_st3(g):
                stats(g, lambda i: row(g, i), "h2", "st3", "mv3", 2)

            def c_ln3(g):
                if g:
                    dve.wait_ge(dispatched, 16 * 2 * NT * g)
                normalise(g, lambda i: row(g, i), xs[:, :, 0:D], 2, "rstd3", "xn3")

            def c_sc(g):
                need(dve, "s3_mm", g)
                need(dve, "p3", g - 1)
                n = ROWS[2]
                inc(d.tensor_reduce(mx3[:, 0:2], psB[0:PT, 2, 0:2 * PT].rearrange("p (i q) -> p i q", q=PT), AX, ALU.max), "s3")
                inc(d.tensor_reduce(mx3[0:n, 2:3], psB[0:n, 2, 2 * PT:2 * PT + n], AX, ALU.max), "s3")
                need(dve, "s3", g, 2)
                inc(d.tensor_scalar(nm3[:], mx3[:], -ASCALE, None, ALU.mult), "s3")

            def c_pv(g):
                need(dve, "p3", g)
                inc(d.reciprocal(rr3[:], rs3[:]), "rr")
                need(dve, "rr", g)
                for i in range(NT):
                    need(dve, "pv3_mm", g, BANKED[i])
                    inc(d.scalar_tensor_tensor(row(g, i), row_slot(psB, i, 2), rr3[0:ROWS[i], i:i + 1], row(g, i),
                                               ALU.mult, ALU.add), "h3")
                stats(g, lambda i: row(g, i), "h3", "st4", "mv4", 2)

            def c_ln4(g):
                normalise(g, lambda i: row(g, i), xs[:, :, 0:D], 2, "rstd4", "xn4")

            def c_rt(g):
                if g == 0:
                    dve.wait_ge(w_late, N_LATE)
                need(dve, "lg_mm", g)
                n = ROWS[2]
                d.tensor_tensor(lgt[:, 0:2, :], psB[0:PT, 2, 0:2 * E].rearrange("p (i e) -> p i e", e=E),
                                brb[0:PT], ALU.add)
                inc(d.tensor_tensor(lgt[0:n, 2, :], psB[0:n, 2, 2 * E:3 * E], brb[0:n, 0, :], ALU.add), "lg")
                need(dve, "lg", g)
                for i in range(NT):
                    ins = d.max(top[:, i, :], lgt[:, i, :])
                inc(ins, "rt")
                need(dve, "rt", g, 1)
                for i in range(NT):
                    ins = d.max_index(topi[:, i, :], top[:, i, :], lgt[:, i, :])
                inc(ins, "rt")
                need(dve, "rt", g, 2)
                inc(d.tensor_copy(topf[:], topi[:, :, 0:2]), "rt")
                need(dve, "rt", g, 3)
                d.tensor_scalar(xs[:, :, D], tid[:], float(g * T), None, ALU.add)
                d.tensor_copy(xs[:, :, D + 1], topf[:, :, 0])
                for k in range(2):
                    ins = d.tensor_tensor(hot[:, k], iota8[:], topf[:, :, k:k + 1].to_broadcast([PT, NT, E]), ALU.is_equal)
                inc(ins, "rt")
                need(dve, "rt", g, 4)
                d.tensor_tensor(cnt[:], hot[:, 0], hot[:, 1], ALU.add).then_inc(route_cnt, 1)
                dve.wait_ge(route_cnt, g + 1)
                inc(d.tensor_tensor(cntb[:, 0:NT, :], cnt[:], valid[:], ALU.mult), "rt")

            def c_rank(g):
                need(dve, "rank_mm", g)
                inc(d.tensor_tensor(slot[:], psB[0:PT, 3, 0:NT * E].rearrange("p (t e) -> p t e", e=E),
                                    run[0:PT].unsqueeze(1).to_broadcast([PT, NT, E]), ALU.add), "rt")
                need(dve, "rt", g, 6)
                inc(d.tensor_tensor(run[:], psB[:, 3, NT * E:(NT + 1) * E], run[:], ALU.add), "rt")
                for k in range(2):
                    ins = d.tensor_tensor(hslot[:, k], hot[:, k], slot[:], ALU.mult)
                inc(ins, "rt")
                need(dve, "rt", g, 8)
                if g == G - 2:
                    d.tensor_copy(padint[:], run[0:1, :]).then_inc(pad_starts, 1)
                inc(d.tensor_reduce(slotf[:], hslot[:], AX, ALU.add), "rt")
                need(dve, "rt", g, 9)
                inc(d.tensor_copy(slotu[:], slotf[:]), "rt")
                inc(d.tensor_tensor(gd[:], top[:, :, 1], top[:, :, 0], ALU.subtract), "rt")
                need(dve, "gexp", g)
                inc(d.tensor_scalar(gs[:], ge[:], 1.0, None, ALU.add), "rt")
                need(dve, "rt", g, 12)
                gt = gates[:, bass.ts(g, NT), :]
                inc(d.reciprocal(gd[:], gs[:]), "rt")
                need(dve, "rt", g, 13)
                inc(d.tensor_copy(gt[:, :, 0], gd[:]), "rt")
                inc(d.tensor_tensor(gt[:, :, 1], gd[:], ge[:], ALU.mult), "rt")

            in_order(s_bias, s_tern, a_ln, a_norm, a_prod, a_soft, a_pv, a_pv2, a_out, b_ln2, b_norm2, b_q, b_f1a, b_f1b, b_f1c,
                     b_f1d, b_amax, b_spread, b_round, b_f2, b_f2b, c_st3, c_ln3, c_sc, c_pv, c_ln4, c_rt, c_rank)

            steps = [0]

            def step(ins):
                ins.then_inc(plan, 1)
                steps[0] += 1
                dve.wait_ge(plan, steps[0])

            used, whole, end, start, off = (nblk[:, n, :] for n in range(5))
            shift = used
            need(dve, "rt", G - 1)
            step(d.tensor_tensor(used, run[:], base[:], ALU.subtract))
            step(d.tensor_scalar(whole, used, 1.0 / 128, 127.0 / 256, ALU.mult, ALU.add))
            step(d.tensor_scalar(whole, whole, MAGIC, -MAGIC, ALU.add, ALU.add))
            step(d.tensor_tensor_scan(end, onesf[:, 0:E], whole, 0.0, ALU.mult, ALU.add))
            step(d.tensor_tensor(start, end, whole, ALU.subtract))
            d.tensor_tensor(bw[:, 0], blkno[:], nblk[:, 3, :].unsqueeze(1).to_broadcast([128, NBLK, E]), ALU.is_ge)
            d.tensor_tensor(bw[:, 1], blkno[:], nblk[:, 2, :].unsqueeze(1).to_broadcast([128, NBLK, E]), ALU.is_ge)
            step(d.scalar_tensor_tensor(shift, start, 128.0, base[:], ALU.mult, ALU.subtract))
            d.tensor_tensor(bw[:, 2], bw[:, 0], bw[:, 1], ALU.subtract)
            step(d.tensor_scalar(off, shift, -1.0, float(128 * LEAST - DUMMY), ALU.mult, ALU.add))
            d.tensor_tensor(bw[:, 0], bw[:, 2], eno[:], ALU.mult)
            step(d.tensor_tensor(bw[:, 1], bw[:, 2], nblk[:, 4, :].unsqueeze(1).to_broadcast([128, NBLK, E]), ALU.mult))
            step(d.tensor_reduce(bres[:], bw[:, 0:2], AX, ALU.add))
            d.tensor_copy(bint[0:1, 0], bres[0:1, 0])
            step(d.tensor_tensor(bint[0:1, 1], bres[0:1, 1], idle[0:1, :], ALU.add))
            assert steps[0] == PLAN

            def result_rows(b, q):
                wait_loaded(dve, b, q)
                inc(d.tensor_scalar(second[:, q:q + 1], xb[:, q, D + 1:D + 2], bres[:, 0, bass.ds(b, 1)], float(B * S),
                                    ALU.not_equal, ALU.mult), "seconds")
                need(dve, "seconds", b)
                inc(d.tensor_tensor(yrow[:, q:q + 1], second[:, q:q + 1], xb[:, q, D:D + 1], ALU.add), "yrows")

            def expert(b):
                return dve.value_load(bint[0:1, 0, bass.ds(b, 1)], min_val=0, max_val=E - 1)

            def h_columns(b, j, e):
                need(dve, "h_mm", b)
                need(dve, "y_mm", b - 2)
                for f in range(FFC):
                    inc(d.tensor_scalar(hTe[:, j, f, :], psB[:, j, f * 128:(f + 1) * 128],
                                        mb1[:, bass.ds(e, 1), f], 0.0, ALU.add, ALU.max), "hTs")

            def y_rows(b, j, e):
                need(dve, "y_mm", b)
                if not isinstance(b, int) or b >= 2:
                    dve.wait_ge(y_stored[j], (b - j) * 8)
                inc(d.tensor_tensor(yb[:, j, :], psA[:, 2 + j, 0:D], mb2[:, bass.ds(e, 1), :], ALU.add), "ys")

            def finish(b, q):
                e, e_before = expert(b), expert(b - 1)
                result_rows(b, q)
                h_columns(b, q % 2, e)
                y_rows(b - 1, (q + 1) % 2, e_before)

            dve.wait_ge(w_moe, N_MOE)
            result_rows(0, 0)
            h_columns(0, 0, expert(0))
            each_block(dve, finish, 1, NBLK)
            y_rows(NBLK - 1, 1, expert(NBLK - 1))
            for g in range(G):
                dve.wait_ge(returned[g], 48)
                for k in range(2):
                    for n, i in enumerate((0, 2)):
                        t, r = g * NT + i, ROWS[i]
                        if k:
                            dve.wait_ge(added, 4 * g + n + 1)
                        d.scalar_tensor_tensor(hall[0:r, t, :], back[0:r, t, k, :], gates[0:r, t, k:k + 1], hall[0:r, t, :],
                                               ALU.mult, ALU.add).then_inc(added, 1)


def lay_out(i):
    import numpy as np
    f = np.ascontiguousarray

    def cols(w):
        w = np.asarray(w)
        return f(w.reshape(w.shape[0] // 128, 128, -1).transpose(1, 0, 2))

    def vec(b):
        return f(np.asarray(b).reshape(-1, 128).T)

    x = np.asarray(i["x"])
    n = IMG // PATCH
    pt = x.reshape(B, C, n, PATCH, n, PATCH).transpose(1, 3, 5, 0, 2, 4).reshape(C * PATCH * PATCH, B, n * n)
    pat = np.zeros((C * PATCH * PATCH, B, S), x.dtype)
    pat[:, :, 1:] = pt
    pat = f(pat.reshape(FC, 128, G, T).transpose(1, 2, 0, 3))
    row = np.concatenate([np.asarray(i["L0_tok_cls_token"])[0], np.tile(np.asarray(i["L0_tok_b"])[None], (S - 1, 1))])
    w1, w2 = np.asarray(i["L1_ffn_W1"]), np.asarray(i["L1_ffn_W2"])
    o = {
        "pat": pat, "tokw": cols(np.asarray(i["L0_tok_W"]).T),
        "rowc": f(np.tile(row, (3, 1))), "posr": f(np.tile(np.asarray(i["L0_tok_pos_enc"])[0], (3, 1))),
        "qkw": cols(i["L0_attn_proj_qk_w"]), "pvw": cols(i["L0_attn_proj_v_w"]),
        "inwT": cols(np.asarray(i["L0_attn_in_proj_w"]).T), "qkb": vec(i["L0_attn_proj_qk_b"]),
        "pvb": vec(i["L0_attn_proj_v_b"]), "inb": vec(i["L0_attn_in_proj_b"]),
        "owT": cols(np.asarray(i["L0_attn_out_proj_w"]).T),
        "ob3": f(np.tile(np.asarray(i["L0_attn_out_proj_b"])[None], (PT, 1))),
        "w1f": cols(np.asarray(i["L0_ffn_w1"]).T), "w2f": cols(np.asarray(i["L0_ffn_w2"]).T),
        "convw": cols(np.asarray(i["L0_ffn_conv_w"]).reshape(HID, 3)), "convb": vec(i["L0_ffn_conv_b"]),
        "aq": cols(i["L1_attn_Wq"]), "ak": cols(i["L1_attn_Wk"]), "avT": cols(np.asarray(i["L1_attn_Wv"]).T),
        "wr": cols(i["L1_ffn_Wr"]), "brb": f(np.tile(np.asarray(i["L1_ffn_br"])[None, None], (128, 2, 1))),
        "mw1": f(w1.reshape(E, DC, 128, FF).transpose(2, 0, 1, 3)),
        "mw2": f(w2.reshape(E, FFC, 128, D).transpose(2, 0, 1, 3)),
        "mb1": f(np.asarray(i["L1_ffn_b1"]).reshape(E, FFC, 128).transpose(2, 0, 1)),
        "mb2": f(np.tile(np.asarray(i["L1_ffn_b2"])[None], (128, 1, 1))),
    }
    return o


def kernel(**inputs):
    import concourse.bacc as bacc
    from concourse.bass_utils import run_bass_kernel_spmd

    nc = bacc.Bacc("TRN2", target_bir_lowering=False, num_devices=1)
    arrays = {f"in_{k}": v for k, v in lay_out(inputs).items()}
    aps = {k[3:]: nc.dram_tensor(k, v.shape, mybir.dt.from_np(v.dtype), kind="ExternalInput").ap()
           for k, v in arrays.items()}
    out = nc.dram_tensor("out_rows", (B * S, D), F32, kind="ExternalOutput").ap()
    vit_tower(nc, aps, out)
    r = run_bass_kernel_spmd(nc, [arrays], core_ids=[0])
    return r.results[0]["out_rows"].reshape(B, S, D)
```
